# Optimizing a Trainium2 kernel written in Bass

```python
import numpy as np
import jax
import jax.numpy as jnp

def _softmax(x, axis=-1):
    return jax.nn.softmax(x, axis=axis)

def _gelu(x):
    return jax.nn.gelu(x, approximate=True)

def _silu(x):
    return jax.nn.silu(x)

def _sigmoid(x):
    return jax.nn.sigmoid(x)

def _layernorm(x, axis=-1, eps=1e-05):
    m = jnp.mean(x, axis=axis, keepdims=True)
    v = jnp.var(x, axis=axis, keepdims=True)
    return (x - m) / jnp.sqrt(v + eps)

def _scatter_add(tgt, idx, src, axis=0):
    return tgt.at[idx].add(src)

def _segment_sum(src, seg, n):
    return jax.ops.segment_sum(src, seg, n)
kernel_name = 'mk_decoder_preln_d1_seqx_r4_b09eec'

def setup_inputs(seed: int=0):
    np.random.seed(seed)
    _w = jnp.asarray

    def _rec_inputs():
        import jax
        import jax.numpy as jnp
        _rk = jax.random.key(seed)
        x = 0.5 + 0.2887 * jax.random.normal(jax.random.fold_in(_rk, 1), (4, 512, 512), jnp.float32)
        _lenS = 512 - jax.random.randint(jax.random.fold_in(_rk, 7), (4,), 0, max(1, 512 // 4) + 1, jnp.int32)
        _lenS2 = 512 - jax.random.randint(jax.random.fold_in(_rk, 8), (4,), 0, max(1, 512 // 4) + 1, jnp.int32)
        _ctx_512P = jax.random.normal(jax.random.fold_in(_rk, 11), (4, 16, 128), jnp.float32)
        _ctx_512c = jax.random.dirichlet(jax.random.fold_in(_rk, 511), 0.3 * jnp.ones((16,), jnp.float32), (4, 512))
        _ctx_512t = jnp.einsum('bsk,bkd->bsd', _ctx_512c, _ctx_512P)
        _ctx_512t = _ctx_512t * jax.lax.rsqrt(jnp.mean(jnp.square(_ctx_512t)) + 1e-12) * 0.953939
        ctx_512 = 7.22013e-05 + 1.00017 * (_ctx_512t + 0.3 * jax.random.normal(jax.random.fold_in(_rk, 611), (4, 512, 128), jnp.float32))
        _validS = jnp.arange(512)[None, :] < _lenS[:, None]
        _validS2 = jnp.arange(512)[None, :] < _lenS2[:, None]
        _causal = jnp.tril(jnp.ones((512, 512), dtype=bool))
        mask_SxS2_bk1 = jnp.broadcast_to(_validS2[0:1, :], (512, 512))
        mask_BxS2_bf0 = jnp.logical_not(jnp.ones((4, 512), dtype=bool))
        return (x, ctx_512, mask_SxS2_bk1, mask_BxS2_bf0)
    x, ctx_512, mask_SxS2_bk1, mask_BxS2_bf0 = _rec_inputs()

    def _L0_attn_setup():
        import jax, jax.numpy as jnp
        import numpy as np
        import math
        N_EMBD = 512
        N_HEADS = 16
        HEAD_DIM = N_EMBD // N_HEADS
        CTX = 512

        def alibi_bias(seq_len: int, n_heads: int) -> jnp.ndarray:
            i = jnp.arange(seq_len)[:, None]
            j = jnp.arange(seq_len)[None, :]
            pos = jnp.where(j <= i, (j - i).astype(jnp.float32), 0.0)
            slopes = 2.0 ** (-8.0 / jnp.arange(1, n_heads + 1, dtype=jnp.float32))
            return slopes[:, None, None] * pos[None, :, :]

        def causal_mask(seq_len: int) -> jnp.ndarray:
            i = jnp.arange(seq_len)[:, None]
            j = jnp.arange(seq_len)[None, :]
            return jnp.where(j > i, -jnp.inf, 0.0).astype(jnp.float32)
        key = jax.random.key(seed)
        k_x, k_qkv, k_o = jax.random.split(key, 3)
        scale = 1.0 / math.sqrt(N_EMBD)
        x = jax.random.normal(k_x, (2, CTX, N_EMBD), dtype=jnp.float32)
        W_qkv = jax.random.normal(k_qkv, (N_EMBD, 3 * N_EMBD), dtype=jnp.float32) * scale
        W_o = jax.random.normal(k_o, (N_EMBD, N_EMBD), dtype=jnp.float32) * scale
        return {'x': x, 'W_qkv': W_qkv, 'W_o': W_o}
    _L0_attn_all = _L0_attn_setup()
    _L0_attn_in = {k: v for k, v in _L0_attn_all.items() if k in ('W_qkv', 'W_o')}
    del _L0_attn_all

    def _L0_xattn_setup():
        import jax, jax.numpy as jnp
        import numpy as np
        B, S, H = (8, 512, 128)
        key = jax.random.key(seed)
        kq, kk, kqc, kwq, kwk = jax.random.split(key, 5)
        q = jax.random.normal(kq, (B, S, H), dtype=jnp.float32)
        k = jax.random.normal(kk, (B, S, H), dtype=jnp.float32)
        qc_score = jax.random.uniform(kqc, (B, S, S), dtype=jnp.float32)
        attn_mask = jnp.triu(jnp.ones((S, S), dtype=bool), k=1)
        key_padding_mask = jnp.zeros((B, S), dtype=bool)
        scale = 1.0 / np.sqrt(H)
        Wq = jax.random.normal(kwq, (H, H), dtype=jnp.float32) * scale
        Wk = jax.random.normal(kwk, (H, H), dtype=jnp.float32) * scale
        bq = jnp.zeros((H,), dtype=jnp.float32)
        bk = jnp.zeros((H,), dtype=jnp.float32)
        return {'q': q, 'k': k, 'attn_mask': attn_mask, 'key_padding_mask': key_padding_mask, 'qc_score': qc_score, 'Wq': Wq, 'bq': bq, 'Wk': Wk, 'bk': bk}
    _L0_xattn_all = _L0_xattn_setup()
    _L0_xattn_in = {k: v for k, v in _L0_xattn_all.items() if k in ('Wq', 'bq', 'Wk', 'bk')}
    del _L0_xattn_all

    def _L0_ffn_setup():
        import jax, jax.numpy as jnp
        import numpy as np
        B, S, D = (4, 512, 512)
        E, F, K = (8, 256, 2)
        SF = 256
        EPS = 1e-06

        def _rmsnorm(x, w, eps=EPS):
            var = jnp.mean(x * x, axis=-1, keepdims=True)
            return x * jax.lax.rsqrt(var + eps) * w
        key = jax.random.key(seed)
        ks = jax.random.split(key, 9)
        g = lambda k, shape, scale: jax.random.normal(k, shape, jnp.float32) * scale
        return {'x': g(ks[0], (B, S, D), 1.0), 'rms_weight': jnp.ones((D,), jnp.float32), 'router_w': g(ks[1], (D, E), 0.02), 'w_gate': g(ks[2], (E, D, F), 0.02), 'w_up': g(ks[3], (E, D, F), 0.02), 'w_down': g(ks[4], (E, F, D), 0.02), 'sw_gate': g(ks[5], (D, SF), 0.02), 'sw_up': g(ks[6], (D, SF), 0.02), 'sw_down': g(ks[7], (SF, D), 0.02)}
    _L0_ffn_all = _L0_ffn_setup()
    _L0_ffn_in = {k: v for k, v in _L0_ffn_all.items() if k in ('rms_weight', 'router_w', 'w_gate', 'w_up', 'w_down', 'sw_gate', 'sw_up', 'sw_down')}
    del _L0_ffn_all
    return {'x': x, 'ctx_512': ctx_512, 'mask_SxS2_bk1': mask_SxS2_bk1, 'mask_BxS2_bf0': mask_BxS2_bf0, 'L0_attn_W_qkv': _L0_attn_in['W_qkv'], 'L0_attn_W_o': _L0_attn_in['W_o'], 'L0_xattn_Wq': _L0_xattn_in['Wq'], 'L0_xattn_bq': _L0_xattn_in['bq'], 'L0_xattn_Wk': _L0_xattn_in['Wk'], 'L0_xattn_bk': _L0_xattn_in['bk'], 'L0_ffn_rms_weight': _L0_ffn_in['rms_weight'], 'L0_ffn_router_w': _L0_ffn_in['router_w'], 'L0_ffn_w_gate': _L0_ffn_in['w_gate'], 'L0_ffn_w_up': _L0_ffn_in['w_up'], 'L0_ffn_w_down': _L0_ffn_in['w_down'], 'L0_ffn_sw_gate': _L0_ffn_in['sw_gate'], 'L0_ffn_sw_up': _L0_ffn_in['sw_up'], 'L0_ffn_sw_down': _L0_ffn_in['sw_down']}

def reference(x, ctx_512, mask_SxS2_bk1, mask_BxS2_bf0, L0_attn_W_qkv, L0_attn_W_o, L0_xattn_Wq, L0_xattn_bq, L0_xattn_Wk, L0_xattn_bk, L0_ffn_rms_weight, L0_ffn_router_w, L0_ffn_w_gate, L0_ffn_w_up, L0_ffn_w_down, L0_ffn_sw_gate, L0_ffn_sw_up, L0_ffn_sw_down):
    import jax
    import jax.numpy as jnp

    def _L0_attn_ref(x, W_qkv, W_o):
        import jax, jax.numpy as jnp
        import numpy as np
        import math
        N_EMBD = 512
        N_HEADS = 16
        HEAD_DIM = N_EMBD // N_HEADS
        CTX = 512

        def alibi_bias(seq_len: int, n_heads: int) -> jnp.ndarray:
            i = jnp.arange(seq_len)[:, None]
            j = jnp.arange(seq_len)[None, :]
            pos = jnp.where(j <= i, (j - i).astype(jnp.float32), 0.0)
            slopes = 2.0 ** (-8.0 / jnp.arange(1, n_heads + 1, dtype=jnp.float32))
            return slopes[:, None, None] * pos[None, :, :]

        def causal_mask(seq_len: int) -> jnp.ndarray:
            i = jnp.arange(seq_len)[:, None]
            j = jnp.arange(seq_len)[None, :]
            return jnp.where(j > i, -jnp.inf, 0.0).astype(jnp.float32)
        bsz, seq_len, n_embd = x.shape
        qkv = jnp.einsum('bsd,de->bse', x, W_qkv)
        q, k, v = jnp.split(qkv, 3, axis=-1)

        def to_heads(t):
            return t.reshape(bsz, seq_len, N_HEADS, HEAD_DIM).transpose(0, 2, 1, 3)
        q, k, v = (to_heads(q), to_heads(k), to_heads(v))
        attn = jnp.einsum('bhqd,bhkd->bhqk', q, k) / math.sqrt(HEAD_DIM)
        attn = attn + alibi_bias(seq_len, N_HEADS)[None] + causal_mask(seq_len)[None, None]
        attn = jax.nn.softmax(attn, axis=-1)
        y = jnp.einsum('bhqk,bhkd->bhqd', attn, v)
        y = y.transpose(0, 2, 1, 3).reshape(bsz, seq_len, n_embd)
        return jnp.einsum('bsd,de->bse', y, W_o)

    def _L0_xattn_ref(q, k, attn_mask, key_padding_mask, qc_score, Wq, bq, Wk, bk):
        import jax, jax.numpy as jnp
        import numpy as np
        B, S, H = (8, 512, 128)
        qp = jnp.einsum('bsh,oh->bso', q, Wq) + bq
        kp = jnp.einsum('bth,oh->bto', k, Wk) + bk
        scaling = jnp.asarray(float(H) ** (-0.5), dtype=qp.dtype)
        scores = jnp.einsum('bsh,bth->bst', qp, kp) * scaling
        scores = scores * qc_score
        mask = attn_mask[None, :, :] | key_padding_mask[:, None, :]
        scores = jnp.where(mask, -jnp.inf, scores)
        return jax.nn.softmax(scores, axis=-1)

    def _L0_ffn_ref(x, rms_weight, router_w, w_gate, w_up, w_down, sw_gate, sw_up, sw_down):
        import jax, jax.numpy as jnp
        import numpy as np
        B, S, D = (4, 512, 512)
        E, F, K = (8, 256, 2)
        SF = 256
        EPS = 1e-06

        def _rmsnorm(x, w, eps=EPS):
            var = jnp.mean(x * x, axis=-1, keepdims=True)
            return x * jax.lax.rsqrt(var + eps) * w
        b, s, d = x.shape
        e = router_w.shape[1]
        h = _rmsnorm(x, rms_weight)
        ht = h.reshape(-1, d)
        t = ht.shape[0]
        logits = ht @ router_w
        probs = jax.nn.softmax(logits, axis=-1)
        topv, topi = jax.lax.top_k(probs, K)
        topv = topv / jnp.sum(topv, axis=-1, keepdims=True)
        w_dense = jnp.zeros((t, e), ht.dtype).at[jnp.arange(t)[:, None], topi].set(topv)
        g = jnp.einsum('td,edf->tef', ht, w_gate)
        u = jnp.einsum('td,edf->tef', ht, w_up)
        eo = jnp.einsum('tef,efd->ted', jax.nn.silu(g) * u, w_down)
        moe = jnp.einsum('te,ted->td', w_dense, eo)
        sh = jax.nn.silu(ht @ sw_gate) * (ht @ sw_up) @ sw_down
        return (moe + sh).reshape(b, s, d)
    x = x + _L0_attn_ref(_layernorm(x, axis=-1), L0_attn_W_qkv, L0_attn_W_o)
    x = x + _L0_xattn_ref(ctx_512, ctx_512, mask_SxS2_bk1, mask_BxS2_bf0, _layernorm(x, axis=-1), L0_xattn_Wq, L0_xattn_bq, L0_xattn_Wk, L0_xattn_bk)
    x = x + _L0_ffn_ref(_layernorm(x, axis=-1), L0_ffn_rms_weight, L0_ffn_router_w, L0_ffn_w_gate, L0_ffn_w_up, L0_ffn_w_down, L0_ffn_sw_gate, L0_ffn_sw_up, L0_ffn_sw_down)
    return x

_drawn_inputs = setup_inputs


def setup_inputs(seed=0):
    import zlib

    import numpy as np

    out = dict(_drawn_inputs(seed))
    spreads = {'L0_xattn_bq': (0.0, 2.0), 'L0_xattn_bk': (0.0, 2.0), 'L0_ffn_rms_weight': (1.0, 0.6)}
    factors = {'ctx_512': 3.278, 'L0_xattn_Wq': 3.316, 'L0_xattn_Wk': 3.211}
    for name, (base, spread) in spreads.items():
        noise = np.random.default_rng([zlib.crc32(name.encode()), seed]).standard_normal(out[name].shape)
        drawn = base * np.exp(spread * noise) if base else spread * noise
        out[name] = jnp.asarray(drawn.astype(out[name].dtype))
    for name, factor in factors.items():
        out[name] = (out[name] * factor).astype(out[name].dtype)
    return out
```

```python
from contextlib import ExitStack

import numpy as np

import concourse.bass as bass
from concourse import mybir

F32 = mybir.dt.float32
F32R = mybir.dt.float32r
BF16 = mybir.dt.bfloat16
U8 = mybir.dt.uint8
ALU = mybir.AluOpType
ACT = mybir.ActivationFunctionType
AX_X = mybir.AxisListType.X

P = 128
B, S, D = 4, 512, 512
HEADS, HD = 16, 32
CTX = 128
NT = S // P
KT = D // P
GROUPS = 4
HPG = HEADS // GROUPS
E, FF = 8, 256
FT = FF // P
TILES = B * NT
TOP = 2
SLOT_TILES = (TOP * TILES * P + E * (P - 1)) // P
LN_EPS, RMS_EPS = 1e-5, 1e-6
ATT_SCALE = HD ** -0.5
X_SCALE = CTX ** -0.5
MASK = -1.5e38
LEAST = -1.0e37
MASKED = -1e30
ROW_ALIBI, ROW_MAX, ROW_END = 3 * HD, 3 * HD + 4, 3 * HD + 6
SM_PIECES = [(0, 0, 4), (1, 0, 2), (1, 2, 2)] + [(q, j, 1) for q in (2, 3) for j in range(HPG)]
N_SM = len(SM_PIECES) + 1
ST_PIECES = ((0,), (1, 3), (2,))
N_ST = len(ST_PIECES) * HPG
P_AT = {0: 0, 1: 512, 3: 896, 2: 1024}
N_V, N_WO, N_CTX, N_PROJ, N_XT = NT, NT, 4, 2, NT
WK_START = N_XT + N_PROJ
WK_BEFORE = N_WO + N_CTX + GROUPS
WK_PER = N_V + GROUPS * N_PROJ + N_XT + WK_BEFORE
HI_PER = GROUPS * N_PROJ + N_XT
STACK_SP, STACK_POOL = 3 * HPG, 3 * HPG


def alibi_rows():
    slope = (2.0 ** (-8.0 / np.arange(1, HEADS + 1, dtype=np.float32))).astype(np.float32)
    hi = (slope.view(np.uint32) & np.uint32(0xFFFFF000)).view(np.float32)
    lo = slope - hi
    pos = np.arange(S, dtype=np.float32) - S // 2
    q = np.zeros((ROW_MAX - ROW_ALIBI, HEADS, S), np.float32)
    k = np.zeros((ROW_END - ROW_ALIBI, HEADS, S), np.float32)
    q[0], q[1], q[2], q[3] = hi[:, None], lo[:, None], pos, pos
    k[0], k[1], k[2], k[3] = pos, pos, -hi[:, None], -lo[:, None]
    k[4:] = 1.0
    return q, k


def raw(ap):
    return ap.bitcast(F32)


class Tick:

    def __init__(self, base=0):
        self.base, self.n = base, 0

    def up(self, k=1):
        self.n += k
        return self.base + self.n

    def now(self):
        return self.base + self.n


def nth(s, g):
    return s.b * (GROUPS // 2) + g // 2 + 1


class Step:

    def __init__(self, b, first=False, last=False, tail=False):
        self.b, self.first, self.last, self.tail = b, first, last, tail
        self.main = not tail
        self.before = not first
        self.wk_base = WK_START + b * WK_PER - (0 if first else WK_BEFORE) - (WK_START if tail else 0)

    def projects(self, g):
        return self.main and not (self.last and g == GROUPS - 1)

    def turns(self, g):
        return self.main and not self.last and g == GROUPS - 1


def over_batches(eng, body):
    body(Step(0, first=True))
    with eng.Fori(1, B - 1) as b:
        body(Step(b))
    body(Step(B - 1, last=True))
    body(Step(B, tail=True))


def attention_part(nc, io, x2_dram):
    with ExitStack() as st:
        sb = lambda name, shape, dt=F32: st.enter_context(nc.sbuf_tensor(name, shape, dt))
        banks = lambda name: [st.enter_context(nc.psum_tensor(f"{name}{i}", [P, 512], F32)) for i in range(2)]
        sem = lambda name: st.enter_context(nc.semaphore(name))
        pair = lambda name, shape: [sb(f"{name}_{p}", shape, F32R) for p in ("hi", "lo")]

        Wqk, Wv, Wo = pair("Wqk", [P, KT, 2 * D]), pair("Wv", [P, KT, D]), pair("Wo", [P, KT, D])
        XT = pair("XT", [P, KT, S])
        QS, KS = sb("QS", [P, 2, HPG, S], F32R), sb("KS", [P, 2, HPG, S], F32R)
        qT, kT = pair("qT", [P, S]), pair("kT", [P, S])
        V = sb("V", [P, NT, HEADS // 2, 3 * HD])
        PT = sb("PT", [P, 2, 1280])
        Yf, Sf = sb("Yf", [P, S]), sb("Sf", [P, S])
        Y = pair("Y", [P, GROUPS, S])
        NM = sb("NM", [P, HPG * NT])
        MT = pair("MT", [HPG * NT, P])
        XN = sb("XN", [P, 2, D])
        XL, XR = sb("XL", [P, NT, D]), sb("XR", [P, NT, D])
        Z, SC, AK = sb("Z", [P, D]), sb("SC", [P, D]), sb("AK", [P, D], BF16)
        CX = Z[:].rearrange("p (t c) -> p t c", t=NT)
        ctxT, qpT, kpT = sb("ctxT", [P, S]), sb("qpT", [P, S]), sb("kpT", [P, S])
        XW, XWT, bqk = sb("XW", [P, 2, P]), sb("XWT", [P, 2, P]), sb("bqk", [P, 2])
        AM, KM = sb("AM", [P, NT, S], BF16), sb("KM", [P, B, S], BF16)
        ident, identb = sb("ident", [P, P]), sb("identb", [P, P], BF16)
        causal, causalT = sb("causal", [P, P], BF16), sb("causalT", [P, P], BF16)
        stats = sb("stats", [P, NT, 6])
        mv1, rs1 = sb("mv1", [P, NT, 2]), sb("rs1", [P, NT])
        mv2, rs2 = sb("mv2", [P, NT, 2]), sb("rs2", [P, NT])
        mhalf = sb("mhalf", [P, NT])
        idle = sb("idle", [P, 2])
        col = sb("col", [P, 4])
        W_STAGE = [PT[:, :, :].rearrange("p a n -> p (a n)"), V[:, :, :, :].rearrange("p t m n -> p (t m n)")]
        AM_U8 = Yf[:].bitcast(U8).rearrange("p (t s) -> p t s", t=NT)
        KM_U8 = Sf[:].bitcast(U8).rearrange("p (t s) -> p t s", t=B)

        SM, ST, O, WK = banks("SM"), banks("ST"), banks("O"), banks("WK")

        xl_in, xr_in, x2_out = sem("xl_in"), sem("xr_in"), sem("x2_out")
        x2_ready = sem("x2_ready")
        w_in = [sem(f"w_in{k}") for k in range(2)]
        am_in, km_in, xw_in = sem("am_in"), sem("km_in"), sem("xw_in")
        ctx_in = sem("ctx_in")
        alibi_in = [sem(f"alibi_in{i}") for i in range(2)]
        stack_in, stack_in2 = [[sem(f"stack_in_{q}{i}") for i in range(2)] for q in ("sp", "pool")]
        mrow_in = [sem(f"mrow_in{i}") for i in range(2)]
        pool_c = sem("pool_c")
        pool_s = sem("pool_s")
        ones_ready = sem("ones_ready")
        stat1, rs1_ready = sem("stat1"), sem("rs1_ready")
        stat2, rs2_ready = sem("stat2"), sem("rs2_ready")
        ak_ready = sem("ak_ready")
        w_hi, w_lo = sem("w_hi"), sem("w_lo")
        mask_ready = sem("mask_ready")
        xn_ready = sem("xn_ready")
        wk_ready, wk_free = sem("wk_ready"), sem("wk_free")
        hi_ready = sem("hi_ready")
        sm_ready, sm_free = sem("sm_ready"), sem("sm_free")
        st_ready, p_ready = sem("st_ready"), sem("p_ready")
        o_ready, o_free = sem("o_ready"), sem("o_free")
        y_done = sem("y_done")
        sc_ready, nm_ready, ex_ready = sem("sc_ready"), sem("nm_ready"), sem("ex_ready")
        dv = sem("dv")
        block = st.enter_context(nc.Block())

        @block.sync
        def _(sp):
            def tiles(dram, b):
                return dram[bass.ds(b, 1)].rearrange("o (t p) d -> p (o t) d", p=P)

            wv = io["wqkv"].rearrange("(k p) n -> k p n", p=P)
            wov = io["wo"].rearrange("(k p) n -> k p n", p=P)
            sp.dma_start(XL[:], tiles(io["x"], 0)).then_inc(xl_in, 16)
            for k in range(KT):
                if k >= 2:
                    sp.wait_ge(w_hi, 2 * (k - 1))
                    sp.wait_ge(w_lo, 2 * (k - 1))
                sp.dma_start(W_STAGE[k % 2][:, 0:3 * D], wv[k]).then_inc(w_in[k % 2], 16)
                sp.dma_start(W_STAGE[k % 2][:, 3 * D:4 * D], wov[k]).then_inc(w_in[k % 2], 16)
            sp.dma_start(AM_U8, io["am"].rearrange("(t p) s -> p t s", p=P)).then_inc(am_in, 16)
            for b in range(B):
                sp.dma_start(KM_U8[:, b, :], io["km"][b:b + 1, :].broadcast_to([P, S])).then_inc(km_in, 16)
            sp.dma_start(XW[:, 0, :], io["xwq"]).then_inc(xw_in, 16)
            sp.dma_start(XW[:, 1, :], io["xwk"]).then_inc(x2_out, 16)
            sp.dma_start(bqk[:, 0:1], io["xbq"].rearrange("(p a) -> p a", a=1)).then_inc(xw_in, 16)
            sp.dma_start(bqk[:, 1:2], io["xbk"].rearrange("(p a) -> p a", a=1)).then_inc(xw_in, 16)

            def stack(wk_done, slot):
                sp.wait_ge(wk_free, wk_done)
                for j in range(HPG):
                    r = slice(HD * j, HD * j + HD)
                    sp.dma_start(raw(QS[0:HD, slot, j, :]), raw(qT[0][r, :])).then_inc(stack_in[slot], 16)
                    sp.dma_start(raw(QS[HD:2 * HD, slot, j, :]), raw(qT[0][r, :])).then_inc(stack_in[slot], 16)
                    sp.dma_start(raw(KS[0:HD, slot, j, :]), raw(kT[0][r, :])).then_inc(stack_in[slot], 16)

            stack(WK_START, 0)

            def body(s):
                wk = Tick(s.wk_base)
                for g in range(GROUPS):
                    u = s.b * GROUPS + g
                    if g == 0:
                        if s.main:
                            wk.up(N_V)
                        if s.main and not s.last:
                            sp.wait_ge(xn_ready, (s.b + 1) * NT)
                            sp.dma_start(XL[:], tiles(io["x"], s.b + 1)).then_inc(xl_in, 16)
                        if s.before:
                            sp.wait_ge(wk_free, s.wk_base)
                            sp.dma_start(CX, tiles(io["ctx"], s.b - 1)).then_inc(ctx_in, 16)
                            sp.wait_ge(x2_out, s.b * 16)
                            sp.dma_start(XR[:], tiles(io["x"], s.b - 1)).then_inc(xr_in, 16)
                            wk.up(N_WO + N_CTX)
                    if s.turns(g):
                        wk.up(N_XT)
                    if s.projects(g):
                        wk.up(N_PROJ)
                        stack(wk.now(), (g + 1) % 2)
                    if s.main:
                        sp.wait_ge(sm_free, (u + 1) * N_SM)
                        for i in range(2):
                            sp.dma_start(raw(QS[ROW_MAX + i:ROW_MAX + i + 1, g % 2, :, :]).rearrange(
                                "o j (q n) -> o (j q) n", q=NT), raw(MT[i][:, :])).then_inc(mrow_in[g % 2], 16)
                    if s.before:
                        wk.up()
                if s.before:
                    sp.wait_ge(x2_ready, s.b * NT)
                    sp.dma_start(tiles(x2_dram, s.b - 1), XR[:]).then_inc(x2_out, 16)

            over_batches(sp, body)
            sp.wait_ge(x2_out, (B + 1) * 16)

        @block.gpsimd
        def _(pool):
            nc.gpsimd.memset(ident[:], 0.0).then_inc(pool_c, 1)
            nc.gpsimd.memset(identb[:], 0.0).then_inc(pool_c, 1)
            nc.gpsimd.memset(causal[:], 0.0).then_inc(pool_c, 1)
            nc.gpsimd.memset(causalT[:], 0.0).then_inc(pool_c, 1)
            nc.gpsimd.memset(mhalf[:], -0.5).then_inc(pool_c, 1)
            pool.wait_ge(pool_c, 5)
            for m in (ident, identb):
                nc.gpsimd.affine_select(out=m[:], in_=m[:], compare_op=ALU.not_equal, fill=1.0, base=0,
                                        pattern=[[-1, P]], channel_multiplier=1).then_inc(pool_c, 1)
            nc.gpsimd.affine_select(out=causal[:], in_=causal[:], compare_op=ALU.is_ge, fill=MASKED, base=0,
                                    pattern=[[-1, P]], channel_multiplier=1).then_inc(pool_c, 1)
            nc.gpsimd.affine_select(out=causalT[:], in_=causalT[:], compare_op=ALU.is_ge, fill=MASKED, base=0,
                                    pattern=[[1, P]], channel_multiplier=-1).then_inc(pool_c, 1)

            def rsqrt1(b):
                pool.wait_ge(stat1, b + 1)
                nc.gpsimd.tensor_tensor(rs1[:], rs1[:], mhalf[:], ALU.pow).then_inc(rs1_ready, 1)

            rsqrt1(0)

            def pause():
                if paused.n or not isinstance(paused.base, int) or paused.base:
                    pool.wait_ge(pool_s, paused.now())
                nc.gpsimd.tensor_tensor(idle[:, 0:1], mhalf[:, 0:1], mhalf[:, 0:1], ALU.mult).then_inc(pool_s, 1)
                paused.up()

            paused = Tick(0)
            def stack(wk_done, slot, heads):
                pool.wait_ge(wk_free, wk_done)
                pause()
                pool.dma_start(QS[ROW_ALIBI:ROW_MAX, slot, :, :], io["alq"][:, heads, :]).then_inc(alibi_in[slot], 16)
                pool.dma_start(KS[ROW_ALIBI:ROW_END, slot, :, :], io["alk"][:, heads, :]).then_inc(alibi_in[slot], 16)
                for j in range(HPG):
                    r = slice(HD * j, HD * j + HD)
                    pool.dma_start(raw(QS[2 * HD:3 * HD, slot, j, :]), raw(qT[1][r, :])).then_inc(stack_in2[slot], 16)
                    pool.dma_start(raw(KS[HD:2 * HD, slot, j, :]), raw(kT[1][r, :])).then_inc(stack_in2[slot], 16)
                    pool.dma_start(raw(KS[2 * HD:3 * HD, slot, j, :]), raw(kT[0][r, :])).then_inc(stack_in2[slot], 16)

            stack(WK_START, 0, slice(0, HPG))
            first_pauses, pauses = 1 + GROUPS, 2 * GROUPS
            pool.wait_ge(w_hi, 2 * KT)
            pool.wait_ge(w_lo, 2 * KT)
            nc.gpsimd.memset(V[:, :, :, HD:2 * HD], 1.0).then_inc(ones_ready, 1)

            def body(s):
                nonlocal paused
                if not s.first:
                    paused = Tick(first_pauses + (s.b - 1) * pauses - (1 if s.tail else 0))
                wk = Tick(s.wk_base)
                for g in range(GROUPS):
                    u = s.b * GROUPS + g
                    if g == 0 and s.main:
                        wk.up(N_V)
                    if g == 0 and s.before:
                        wk.up(N_WO + N_CTX)
                        pool.wait_ge(stat2, s.b)
                        nc.gpsimd.tensor_tensor(rs2[:], rs2[:], mhalf[:], ALU.pow).then_inc(rs2_ready, 1)
                    if s.before:
                        if g == 0:
                            pool.wait_ge(mask_ready, B)
                        pool.wait_ge(sc_ready, (s.b - 1) * NT + g + 1)
                        pause()
                        nc.gpsimd.tensor_tensor(AK[:].rearrange("p (o s) -> p o s", o=1), AM[:, g:g + 1, :],
                                                KM[:, bass.ds(s.b - 1, 1), :], ALU.add).then_inc(ak_ready, 1)
                    if s.turns(g):
                        wk.up(N_XT)
                    if s.projects(g):
                        wk.up(N_PROJ)
                        h = HPG * ((g + 1) % GROUPS)
                        stack(wk.now(), (g + 1) % 2, slice(h, h + HPG))
                    if s.before:
                        wk.up()
                    if g == 1 and s.main and not s.last:
                        rsqrt1(s.b + 1)

            over_batches(pool, body)

        @block.tensor
        def _(pe):
            def three(out, pairs):
                terms = [t for (ah, al), (bh, bl) in pairs for t in ((ah, bh), (ah, bl), (al, bh))]
                for i, (a, b) in enumerate(terms):
                    ins = nc.tensor.matmul(out, a, b, start=(i == 0), stop=(i == len(terms) - 1))
                return ins

            def item(wk, free=True):
                n = wk.up()
                if free:
                    pe.wait_ge(wk_free, n - 2)
                return WK[(wk.n - 1) % 2]

            def turn_x(wk, b, start=False):
                for t in range(NT):
                    bank = item(wk, free=not (start and t < 2))
                    pe.wait_ge(xn_ready, b * NT + t + 1)
                    for k in range(KT):
                        ins = nc.tensor.transpose(bank[:, k * P:(k + 1) * P], XN[:, t % 2, k * P:(k + 1) * P], ident[:])
                    ins.then_inc(wk_ready, 1)

            def project(wk, g):
                if g == 0:
                    pe.wait_ge(wk_free, wk.now())
                for i in range(N_PROJ):
                    bank = item(wk)
                    c = slice(i * D + g * P, i * D + g * P + P)
                    three(bank[:], [((Wqk[0][:, k, c], Wqk[1][:, k, c]), (XT[0][:, k, :], XT[1][:, k, :]))
                                    for k in range(KT)]).then_inc(wk_ready, 1)

            def row_maxima(s, g, u):
                pe.wait_ge(stack_in[g % 2], nth(s, g) * STACK_SP * 16)
                pe.wait_ge(stack_in2[g % 2], nth(s, g) * STACK_POOL * 16)
                pe.wait_ge(alibi_in[g % 2], nth(s, g) * 2 * 16)
                for i, (q, j0, nj) in enumerate(SM_PIECES):
                    if not (s.first and g == 0 and i < 2):
                        pe.wait_ge(sm_free, u * N_SM + i - 1)
                    bank, w = SM[i % 2], (q + 1) * P
                    for n in range(nj):
                        nc.tensor.matmul(bank[:, n * w:(n + 1) * w], QS[0:ROW_MAX, g % 2, j0 + n, q * P:(q + 1) * P],
                                         KS[0:ROW_MAX, g % 2, j0 + n, 0:w], start=(n == 0), stop=False,
                                         skip_group_check=True)
                        ins = nc.tensor.matmul(bank[:, (n + 1) * w - P:(n + 1) * w], identb[:], causal[:],
                                               start=False, stop=True, skip_group_check=True)
                    ins.then_inc(sm_ready, 1)

            def turn_maxima(u):
                pe.wait_ge(sm_free, (u + 1) * N_SM - 1)
                nc.tensor.transpose(SM[(N_SM - 1) % 2][0:HPG * NT, 0:P], NM[:], ident[:]).then_inc(sm_ready, 1)

            def scores(s, g, u, j):
                for n, piece in enumerate(ST_PIECES):
                    m = j * len(ST_PIECES) + n
                    if not (s.first and g == 0 and m < 2):
                        pe.wait_ge(p_ready, u * N_ST + m - 1)
                    bank, at = ST[m % 2], 0
                    for kb in piece:
                        w = S - kb * P
                        nc.tensor.matmul(bank[:, at:at + w], KS[0:ROW_END, g % 2, j, kb * P:(kb + 1) * P],
                                         QS[0:ROW_END, g % 2, j, kb * P:S], start=(at == 0), stop=False,
                                         skip_group_check=True)
                        ins = nc.tensor.matmul(bank[:, at:at + P], identb[:], causalT[:], start=False, stop=True,
                                               skip_group_check=True)
                        at += w
                    ins.then_inc(st_ready, 1)

            def values(s, g, u, j):
                i = u * HPG + j
                if not (s.first and g == 0 and j < 2):
                    pe.wait_ge(o_free, i - 1)
                pe.wait_ge(p_ready, (i + 1) * len(ST_PIECES))
                if g == 0 and j == 0:
                    pe.wait_ge(wk_free, s.wk_base + N_V)
                    pe.wait_ge(ones_ready, 1)
                h = g * HPG + j
                a = HD * (h % 2)
                for kb in range(NT):
                    at = P_AT[kb]
                    ins = nc.tensor.matmul(O[j % 2][0:2 * HD, kb * P:S], V[:, kb, h // 2, a:a + 2 * HD],
                                           PT[:, j % 2, at:at + S - kb * P], start=(kb == 0), stop=(kb == NT - 1),
                                           skip_group_check=True)
                ins.then_inc(o_ready, 1)

            wk = Tick(0)
            pe.wait_ge(pool_c, 9)
            turn_x(wk, 0, start=True)
            pe.wait_ge(w_lo, 2 * KT)
            project(wk, 0)

            def body(s):
                wk = Tick(s.wk_base)
                for g in range(GROUPS):
                    u = s.b * GROUPS + g
                    if s.main:
                        row_maxima(s, g, u)
                    if g == 0 and s.main:
                        for t in range(NT):
                            bank, c = item(wk), slice(t * P, (t + 1) * P)
                            three(bank[:], [((XT[0][:, k, c], XT[1][:, k, c]), (Wv[0][:, k, :], Wv[1][:, k, :]))
                                            for k in range(KT)]).then_inc(wk_ready, 1)
                    if g == 0 and s.before:
                        pe.wait_ge(y_done, s.b * GROUPS)
                        for t in range(NT):
                            bank, c = item(wk), slice(t * P, (t + 1) * P)
                            three(bank[:], [((Y[0][:, k, c], Y[1][:, k, c]), (Wo[0][:, k, :], Wo[1][:, k, :]))
                                            for k in range(GROUPS)]).then_inc(wk_ready, 1)
                        bank = item(wk)
                        pe.wait_ge(xw_in, 3 * 16)
                        pe.wait_ge(x2_out, 16)
                        for i in range(2):
                            ins = nc.tensor.transpose(bank[:, i * P:(i + 1) * P], XW[:, i, :], ident[:])
                        ins.then_inc(wk_ready, 1)
                        bank = item(wk)
                        pe.wait_ge(ctx_in, s.b * 16)
                        for t in range(NT):
                            ins = nc.tensor.transpose(bank[:, t * P:(t + 1) * P], CX[:, t, :], ident[:])
                        ins.then_inc(wk_ready, 1)
                        pe.wait_ge(wk_free, wk.now())
                        for i in range(2):
                            nc.tensor.matmul(item(wk)[:], XWT[:, i, :], ctxT[:], start=True, stop=True).then_inc(wk_ready, 1)
                        cross_ready = wk.now()
                    if s.turns(g):
                        turn_x(wk, s.b + 1)
                    if s.projects(g):
                        project(wk, (g + 1) % GROUPS)
                    if s.main:
                        turn_maxima(u)
                    if s.before:
                        bank = item(wk)
                        if g == 0:
                            pe.wait_ge(wk_free, cross_ready)
                        nc.tensor.matmul(bank[:], qpT[:, g * P:(g + 1) * P], kpT[:], start=True, stop=True).then_inc(wk_ready, 1)
                    if s.main:
                        pe.wait_ge(mrow_in[g % 2], nth(s, g) * 2 * 16)
                        scores(s, g, u, 0)
                        for j in range(1, HPG):
                            scores(s, g, u, j)
                            values(s, g, u, j - 1)
                        values(s, g, u, HPG - 1)

            over_batches(pe, body)

        @block.scalar
        def _(act):
            for k in range(KT):
                act.wait_ge(w_in[k % 2], 32 * (k // 2 + 1))
                w = W_STAGE[k % 2]
                nc.scalar.activation(Wqk[0][:, k, :], w[:, 0:2 * D], ACT.Copy).then_inc(w_hi, 1)
                nc.scalar.activation(Wv[0][:, k, :], w[:, 2 * D:3 * D], ACT.Copy).then_inc(w_hi, 1)
                nc.scalar.activation(Wo[0][:, k, :], w[:, 3 * D:4 * D], ACT.Copy).then_inc(w_hi, 1)

            def hi_x(wk):
                for t in range(NT):
                    act.wait_ge(wk_ready, wk.up())
                    nc.scalar.activation(XT[0][:, :, t * P:(t + 1) * P], WK[(wk.n - 1) % 2][:].rearrange(
                        "p (k n) -> p k n", k=KT), ACT.Copy).then_inc(hi_ready, 1)

            def hi_qk(wk, s=None, g=0):
                for i, (dst, scale) in enumerate(((qT[0], ATT_SCALE), (kT[0], 1.0))):
                    act.wait_ge(wk_ready, wk.up())
                    if i == 0 and s:
                        act.wait_ge(stack_in[g % 2], nth(s, g) * STACK_SP * 16)
                        act.wait_ge(stack_in2[g % 2], nth(s, g) * STACK_POOL * 16)
                    nc.scalar.activation(dst[:], WK[(wk.n - 1) % 2][:], ACT.Copy, scale=scale).then_inc(hi_ready, 1)

            wk = Tick(0)
            hi_x(wk)
            hi_qk(wk)

            def exps(s, g, u, j):
                i = u * HPG + j
                for n, piece in enumerate(ST_PIECES):
                    m = j * len(ST_PIECES) + n
                    if n == 0 and not (s.first and g == 0 and j < 2):
                        act.wait_ge(o_ready, i - 1)
                    act.wait_ge(st_ready, u * N_ST + m + 1)
                    w = sum(S - kb * P for kb in piece)
                    at = P_AT[piece[0]]
                    nc.scalar.activation(PT[:, j % 2, at:at + w], ST[m % 2][:, 0:w], ACT.Exp).then_inc(p_ready, 1)

            def outputs(s, g, u, j):
                i, bank = u * HPG + j, O[j % 2]
                act.wait_ge(o_ready, i + 1)
                if j == 0 and not (s.first and g == 0):
                    act.wait_ge(y_done, u)
                r, odd = slice(j * HD, (j + 1) * HD), j % 2
                lower, upper = bank[0:HD, :], bank[HD:2 * HD, :]
                if s.first and g == 0 and j == 0:
                    act.wait_ge(mask_ready, B)
                nc.scalar.activation(Yf[r, :], upper if odd else lower, ACT.Copy)
                nc.scalar.activation(Sf[r, :], lower if odd else upper, ACT.Copy).then_inc(o_free, 1)

            def body(s):
                wk = Tick(s.wk_base)
                for g in range(GROUPS):
                    u = s.b * GROUPS + g
                    if g == 0 and s.main:
                        wk.up(N_V)
                    if g == 0 and s.before:
                        wk.up(N_WO + N_CTX)
                    if s.turns(g):
                        hi_x(wk)
                    if s.projects(g):
                        hi_qk(wk, s, g)
                    if s.before:
                        wk.up()
                        act.wait_ge(nm_ready, (s.b - 1) * NT + g + 1)
                        nc.scalar.activation(SC[:], SC[:], ACT.Exp, bias=col[:, 1:2], accum_out=col[:, 2:3]).then_inc(ex_ready, 1)
                    if s.main:
                        exps(s, g, u, 0)
                        exps(s, g, u, 1)
                        for j in range(2, HPG):
                            outputs(s, g, u, j - 2)
                            exps(s, g, u, j)
                        outputs(s, g, u, HPG - 2)
                        outputs(s, g, u, HPG - 1)

            over_batches(act, body)

        @block.vector
        def _(dve):
            d = Tick(0)

            def pause():
                nc.vector.memset(idle[:, 1:2], 0.0)

            def statistics(b):
                dve.wait_ge(xl_in, (b + 1) * 16)
                for t in range(NT):
                    nc.vector.bn_stats(stats[:, t, :], XL[:, t, :]).then_inc(dv, 1)
                dve.wait_ge(dv, d.up(NT))
                pause()
                for t in range(NT):
                    nc.vector.bn_aggr(mv1[:, t, :], stats[:, t, :]).then_inc(dv, 1)
                dve.wait_ge(dv, d.up(NT))
                nc.vector.tensor_scalar(rs1[:], mv1[:, :, 1], LN_EPS, None, ALU.add).then_inc(stat1, 1)

            def normalise(b, t):
                nc.vector.tensor_scalar(XN[:, t % 2, :], XL[:, t, :], mv1[:, t, 0:1], rs1[:, t:t + 1],
                                        ALU.subtract, ALU.mult).then_inc(xn_ready, 1)

            def lo_x(wk, hi, b):
                dve.wait_ge(rs1_ready, b + 1)
                normalise(b, 0)
                normalise(b, 1)
                for t in range(NT):
                    dve.wait_ge(wk_ready, wk.up())
                    dve.wait_ge(hi_ready, hi.up())
                    c = slice(t * P, (t + 1) * P)
                    nc.vector.tensor_tensor(XT[1][:, :, c], WK[(wk.n - 1) % 2][:].rearrange("p (k n) -> p k n", k=KT),
                                            XT[0][:, :, c].bitcast(F32), ALU.subtract).then_inc(wk_free, 1)
                    if t + 2 < NT:
                        normalise(b, t + 2)

            def lo_qk(wk, hi):
                for i, (pr, scale) in enumerate(((qT, ATT_SCALE), (kT, 1.0))):
                    dve.wait_ge(wk_ready, wk.up())
                    dve.wait_ge(hi_ready, hi.up())
                    nc.vector.scalar_tensor_tensor(out=pr[1][:], in0=WK[(wk.n - 1) % 2][:], scalar=scale,
                                                   in1=pr[0][:].bitcast(F32), op0=ALU.mult,
                                                   op1=ALU.subtract).then_inc(wk_free, 1)

            statistics(0)
            for k in range(KT):
                dve.wait_ge(w_hi, 3 * (k + 1))
                w = W_STAGE[k % 2]
                for n, (pr, c) in enumerate(((Wqk, slice(0, 2 * D)), (Wv, slice(2 * D, 3 * D)), (Wo, slice(3 * D, 4 * D)))):
                    ins = nc.vector.tensor_tensor(pr[1][:, k, :], w[:, c], pr[0][:, k, :].bitcast(F32), ALU.subtract)
                    if n:
                        ins.then_inc(w_lo, 1)
            wk, hi = Tick(0), Tick(0)
            lo_x(wk, hi, 0)
            lo_qk(wk, hi)
            dve.wait_ge(am_in, 16)
            nc.vector.tensor_scalar(AM[:], AM_U8, MASK, None, ALU.mult).then_inc(sc_ready, 1)
            dve.wait_ge(km_in, 16 * B)
            for b in range(B):
                nc.vector.tensor_scalar(KM[:, b, :], KM_U8[:, b, :], MASK, None, ALU.mult).then_inc(mask_ready, 1)

            def maxima(s, g, u):
                for i, (q, j0, nj) in enumerate(SM_PIECES):
                    dve.wait_ge(sm_ready, u * N_SM + i + 1)
                    w = (q + 1) * P
                    c = slice(j0 * NT + q, (j0 + nj - 1) * NT + q + 1, NT)
                    nc.vector.tensor_reduce(NM[:, c], SM[i % 2][:, 0:nj * w].rearrange("p (j n) -> p j n", j=nj), AX_X,
                                            ALU.max, negate=True).then_inc(sm_free, 1)

            def split_maxima(s, g, u):
                dve.wait_ge(sm_ready, (u + 1) * N_SM)
                if g:
                    dve.wait_ge(mrow_in[(g - 1) % 2], nth(s, g - 1) * 2 * 16)
                elif not s.first:
                    dve.wait_ge(mrow_in[(g - 1) % 2], s.b * (GROUPS // 2) * 2 * 16)
                bank = SM[(N_SM - 1) % 2]
                nc.vector.tensor_copy(MT[0][:], bank[0:HPG * NT, 0:P]).then_inc(dv, 1)
                dve.wait_ge(dv, d.up())
                nc.vector.tensor_tensor(MT[1][:], bank[0:HPG * NT, 0:P], MT[0][:].bitcast(F32),
                                        ALU.subtract).then_inc(sm_free, 1)

            def finish_unit(u, g):
                dve.wait_ge(o_free, (u + 1) * HPG)
                nc.vector.reciprocal(Sf[:], Sf[:]).then_inc(dv, 1)
                dve.wait_ge(dv, d.up())
                nc.vector.tensor_tensor(Yf[:], Yf[:], Sf[:], ALU.mult).then_inc(dv, 1)
                dve.wait_ge(dv, d.up())
                nc.vector.tensor_copy(Y[0][:, g, :], Yf[:]).then_inc(dv, 1)
                dve.wait_ge(dv, d.up())
                nc.vector.tensor_tensor(Y[1][:, g, :], Yf[:], Y[0][:, g, :].bitcast(F32), ALU.subtract).then_inc(y_done, 1)

            def residual(wk, b):
                for t in range(NT):
                    dve.wait_ge(wk_ready, wk.up())
                    if t == 0:
                        dve.wait_ge(xr_in, (b + 1) * 16)
                    xt = XR[:, t, :]
                    nc.vector.tensor_tensor(xt, WK[(wk.n - 1) % 2][:], xt, ALU.add).then_inc(wk_free, 1)
                    dve.wait_ge(wk_free, wk.now())
                    nc.vector.bn_stats(stats[:, t, :], xt).then_inc(dv, 1)
                dve.wait_ge(dv, d.up(NT))
                pause()
                for t in range(NT):
                    nc.vector.bn_aggr(mv2[:, t, :], stats[:, t, :]).then_inc(dv, 1)
                dve.wait_ge(dv, d.up(NT))
                nc.vector.tensor_scalar(rs2[:], mv2[:, :, 1], LN_EPS, None, ALU.add).then_inc(stat2, 1)

            def context(wk):
                dve.wait_ge(wk_ready, wk.up())
                nc.vector.tensor_copy(XWT[:], WK[(wk.n - 1) % 2][:, 0:2 * P].rearrange("p (a n) -> p a n", a=2)).then_inc(wk_free, 1)
                dve.wait_ge(wk_ready, wk.up())
                nc.vector.tensor_copy(ctxT[:], WK[(wk.n - 1) % 2][:]).then_inc(wk_free, 1)
                for i, dst in enumerate((qpT, kpT)):
                    dve.wait_ge(wk_ready, wk.up())
                    nc.vector.tensor_scalar(dst[:], WK[(wk.n - 1) % 2][:], bqk[:, i:i + 1], None, ALU.add).then_inc(wk_free, 1)

            def cross(wk, b, g):
                if g == 0:
                    dve.wait_ge(rs2_ready, b + 1)
                tile = XR[:, g, :]
                nc.vector.tensor_scalar(Z[:], tile, mv2[:, g, 0:1], rs2[:, g:g + 1], ALU.subtract, ALU.mult).then_inc(dv, 1)
                dve.wait_ge(dv, d.up())
                dve.wait_ge(wk_ready, wk.up())
                nc.vector.scalar_tensor_tensor(out=SC[:], in0=WK[(wk.n - 1) % 2][:], scalar=X_SCALE, in1=Z[:], op0=ALU.mult,
                                               op1=ALU.mult).then_inc(wk_free, 1)
                dve.wait_ge(wk_free, wk.now())
                dve.wait_ge(ak_ready, b * NT + g + 1)
                pause()
                nc.vector.tensor_tensor_reduce(out=SC[:], in0=SC[:], in1=AK[:], scale=1.0, scalar=LEAST, op0=ALU.add,
                                               op1=ALU.max, accum_out=col[:, 0:1]).then_inc(sc_ready, 1)
                dve.wait_ge(sc_ready, b * NT + g + 2)
                nc.vector.tensor_scalar(col[:, 1:2], col[:, 0:1], -1.0, None, ALU.mult).then_inc(nm_ready, 1)
                dve.wait_ge(ex_ready, b * NT + g + 1)
                nc.vector.reciprocal(col[:, 3:4], col[:, 2:3]).then_inc(dv, 1)
                dve.wait_ge(dv, d.up())
                nc.vector.scalar_tensor_tensor(out=tile, in0=SC[:], scalar=col[:, 3:4], in1=tile, op0=ALU.mult,
                                               op1=ALU.add).then_inc(x2_ready, 1)

            marks = []

            def body(s):
                nonlocal d
                if isinstance(s.b, int):
                    d = Tick(0 if s.first and not marks else marks[-1])
                    if s.first:
                        d = Tick(start)
                else:
                    d = Tick(marks[-1] + (s.b - 1) * DV_PER)
                wk = Tick(s.wk_base)
                hi = Tick(HI_PER * s.b + WK_START)
                for g in range(GROUPS):
                    u = s.b * GROUPS + g
                    if s.main:
                        maxima(s, g, u)
                    if not (s.first and g == 0) and not (s.tail and g):
                        finish_unit(u - 1, (g - 1) % GROUPS)
                    if g == 0 and s.main:
                        for t in range(NT):
                            dve.wait_ge(wk_ready, wk.up())
                            if s.first and t == 0:
                                dve.wait_ge(ones_ready, 1)
                            nc.vector.tensor_copy(V[:, t, :, :].rearrange("p m (c d) -> p m c d", c=3)[:, :, 0:3:2, :],
                                                  WK[(wk.n - 1) % 2][:].rearrange("p (m c d) -> p m c d", c=2, d=HD)
                                                  ).then_inc(wk_free, 1)
                    if g == 0 and s.before:
                        residual(wk, s.b - 1)
                        context(wk)
                    if s.turns(g):
                        lo_x(wk, hi, s.b + 1)
                    if s.projects(g):
                        lo_qk(wk, hi)
                    if s.main:
                        split_maxima(s, g, u)
                    if s.before:
                        cross(wk, s.b - 1, g)
                    if g == 1 and s.main and not s.last:
                        statistics(s.b + 1)
                if not isinstance(s.b, int):
                    assert d.n == DV_PER, d.n
                    marks.append(marks[-1] + (B - 2) * DV_PER)
                else:
                    marks.append(d.base + d.n)

            DV_PER = GROUPS * 3 + 2 * NT + 2 * NT + GROUPS + 2 * GROUPS
            start = d.base + d.n
            over_batches(dve, body)


def routing_constants():
    expert = np.arange(E, dtype=np.float32)
    full = np.arange(TILES, dtype=np.float32) * P
    before = (expert[None, :] < expert[:, None]).astype(np.float32)
    tile = np.arange(SLOT_TILES, dtype=np.float32)
    row = np.concatenate([expert, full, before.ravel(), tile])
    return np.ascontiguousarray(np.broadcast_to(row, (P, row.size)))


def router_and_shared(nc, io, x2_dram, slots_dram, HR, G, SL, EID):
    with ExitStack() as st:
        sb = lambda name, shape, dt=F32: st.enter_context(nc.sbuf_tensor(name, shape, dt))
        bank = lambda name: st.enter_context(nc.psum_tensor(name, [P, 512], F32))
        sem = lambda name: st.enter_context(nc.semaphore(name))
        pair = lambda name, shape: [sb(f"{name}_{p}", shape, F32R) for p in ("hi", "lo")]

        WS, WSD, RW = pair("WS", [P, KT, 2 * FF]), pair("WSD", [P, FT, D]), pair("RW", [P, KT, E])
        HT = pair("HT", [P, KT, S])
        AT = pair("AT", [P, FT, S])
        XB = sb("XB", [P, NT, D])
        SG = sb("SG", [P, FT, S])
        rms = sb("rms_b", [P, D])
        RWf = sb("RWf", [P, KT, E])
        L = sb("L", [P, TILES, E])
        M8, I8, I8f = sb("M8", [P, TILES, E]), sb("I8", [P, TILES, E], mybir.dt.uint32), sb("I8f", [P, TILES, E])
        OH = [sb(f"OH{k}", [P, TILES, E]) for k in range(TOP)]
        OHb = sb("OHb", [P, TILES, E], BF16)
        RK, TMP = sb("RK", [P, TILES, E]), sb("TMP", [P, TILES, E])
        cnt, ntl, base, gt = sb("cnt", [P, E]), sb("ntl", [P, E]), sb("base", [P, E]), sb("gt", [P, E, TILES])
        cst = sb("cst_sb", [P, E + TILES + E * E + SLOT_TILES])
        c_expert, c_full = cst[:, 0:E], cst[:, E:E + TILES]
        c_before = cst[:, E + TILES:E + TILES + E * E].rearrange("p (e f) -> p e f", e=E)
        c_tile = cst[:, E + TILES + E * E:]
        le = sb("le", [P, SLOT_TILES, E - 1])
        eidf = sb("eidf", [P, SLOT_TILES])
        slf = sb("slf", [P, TILES])
        ident, lower, ones = sb("ident2", [P, P]), sb("lower", [P, P], BF16), sb("ones2", [P, P], BF16)
        stats, mv = sb("stats2", [P, 2, 6]), sb("mv3", [P, NT, 2])
        rs, rt = sb("rs3", [P, NT]), sb("rt3", [P, NT])
        idle = sb("idle3", [P, 1])
        mhalf, lneps, rmseps = sb("mhalf3", [P, NT]), sb("lneps", [P, NT]), sb("rmseps", [P, NT])

        WK = [bank(f"WKb{i}") for i in range(2)]
        GU = [bank(f"GUb{i}") for i in range(2 * FT)]
        LG = bank("LG")
        RB = GU[0]
        CB = GU[1]

        x_in = [sem(f"f_x_in{t}") for t in range(NT)]
        w_in, w_hi, w_lo = [sem(f"f_w_in{i}") for i in range(2)], sem("f_w_hi"), sem("f_w_lo")
        c_in, rw_in, rms_in = sem("f_c_in"), sem("f_rw_in"), sem("f_rms_in")
        pc, pl = sem("f_pc"), sem("f_pl")
        var_ready, rs_ready = sem("f_var"), sem("f_rs")
        h0_ready, h_ready = sem("f_h0"), sem("f_h")
        wk_ready, wk_free, hi_ready = sem("f_wk"), sem("f_wkf"), sem("f_hi")
        lg_ready, lg_free = sem("f_lg"), sem("f_lgf")
        e2_in, e2_out = sem("f_e2i"), sem("f_e2o")
        oh_ready, rk_ready, sl_ready = sem("f_oh"), sem("f_rk"), sem("f_sl")
        zero_out, scat = sem("f_zero"), sem("f_scat")
        gu_ready, sg_ready, at0_ready, at_hi, at_ready = [sem(f"f_{n}") for n in ("gu", "sg", "at0", "at_hi", "at")]
        dv = sem("f_dv")
        block = st.enter_context(nc.Block())

        SPIECES = KT + FT

        def down_at(b):
            return TILES + NT + b * 2 * NT + (NT if b < B - 1 else 0)

        def tile(dram, i):
            return dram.rearrange("b (t p) d -> (b t) p d", p=P)[bass.ds(i, 1)].rearrange("o p d -> p (o d)")

        @block.sync
        def _(sp):
            sp.dma_start(cst[:], io["cst"]).then_inc(c_in, 16)
            sp.dma_start(RWf[:], io["router"].rearrange("(k p) e -> p k e", p=P)).then_inc(rw_in, 16)
            sp.dma_start(rms[:], io["rms"].rearrange("(a d) -> a d", a=1).broadcast_to([P, D])).then_inc(rms_in, 16)
            for t in range(NT):
                sp.dma_start(XB[:, t, :], tile(x2_dram, t)).then_inc(x_in[t], 16)
            for k in range(SPIECES):
                if k >= 2:
                    sp.wait_ge(w_hi, k)
                    sp.wait_ge(w_lo, k)
                if k < KT:
                    r = slice(k * P, (k + 1) * P)
                    sp.dma_start(SG[:, k % 2, 0:FF], io["swg"][r, :]).then_inc(w_in[k % 2], 16)
                    sp.dma_start(SG[:, k % 2, FF:2 * FF], io["swu"][r, :]).then_inc(w_in[k % 2], 16)
                else:
                    r = slice((k - KT) * P, (k - KT + 1) * P)
                    sp.dma_start(SG[:, k % 2, :], io["swd"][r, :]).then_inc(w_in[k % 2], 32 if 0 else 16)
            with sp.Fori(1, B) as b:
                for t in range(NT):
                    sp.wait_ge(h0_ready, (b - 1) * NT + t + 1)
                    sp.dma_start(XB[:, t, :], tile(x2_dram, b * NT + t)).then_inc(x_in[t], 16)
            for t in range(NT):
                sp.wait_ge(h0_ready, (B - 1) * NT + t + 1)
                sp.dma_start(XB[:, t, :], tile(x2_dram, t)).then_inc(x_in[t], 16)
            for b in range(1, B):
                for t in range(NT):
                    sp.wait_ge(wk_free, down_at(b - 1) + t + 1)
                    sp.dma_start(XB[:, t, :], tile(x2_dram, b * NT + t)).then_inc(x_in[t], 16)

        @block.gpsimd
        def _(pool):
            nc.gpsimd.memset(mhalf[:], -0.5).then_inc(pc, 1)
            nc.gpsimd.memset(lneps[:], LN_EPS).then_inc(pc, 1)
            nc.gpsimd.memset(rmseps[:], RMS_EPS).then_inc(pc, 1)
            nc.gpsimd.memset(ident[:], 0.0).then_inc(pc, 1)
            nc.gpsimd.memset(lower[:], 1.0).then_inc(pc, 1)
            nc.gpsimd.memset(ones[:], 1.0).then_inc(pc, 1)
            pool.wait_ge(pc, 6)
            nc.gpsimd.affine_select(out=ident[:], in_=ident[:], compare_op=ALU.not_equal, fill=1.0, base=0,
                                    pattern=[[-1, P]], channel_multiplier=1).then_inc(pc, 1)
            nc.gpsimd.affine_select(out=lower[:], in_=lower[:], compare_op=ALU.is_gt, fill=0.0, base=0,
                                    pattern=[[1, P]], channel_multiplier=-1).then_inc(pc, 1)
            pool.wait_ge(rms_in, 16)

            steps = ((rt, mv[:, :, 1], lneps, ALU.add), (rs, rt[:], mhalf, ALU.pow), (rt, rs[:], rs, ALU.mult),
                     (rt, rt[:], mv[:, :, 1], ALU.mult), (rt, rt[:], rmseps, ALU.add), (rt, rt[:], mhalf, ALU.pow),
                     (rs, rs[:], rt, ALU.mult))

            with pool.Fori(0, B) as b:
                pool.wait_ge(var_ready, b + 1)
                for n, (dst, x, y, op) in enumerate(steps):
                    ins = nc.gpsimd.tensor_tensor(dst[:], x, y if op == ALU.mult and n == 3 else y[:], op)
                    if n < len(steps) - 1:
                        ins.then_inc(pl, 1)
                        pool.wait_ge(pl, b * (len(steps) - 1 + NT) + n + 1)
                    else:
                        ins.then_inc(rs_ready, 1)
                for t in range(NT):
                    pool.wait_ge(h0_ready, b * NT + t + 1)
                    nc.gpsimd.tensor_tensor(idle[:], mhalf[:, 0:1], mhalf[:, 0:1], ALU.mult).then_inc(pl, 1)
                    pool.wait_ge(pl, b * (len(steps) - 1 + NT) + len(steps) + t)
                    h = HR[:, bass.ds(b * NT + t, 1), :].rearrange("p o d -> p (o d)")
                    nc.gpsimd.tensor_tensor(h, h, rms[:], ALU.mult).then_inc(h_ready, 1)
            pool.wait_ge(sl_ready, TOP)
            for t in range(TILES):
                for k in range(TOP):
                    pool.indirect_dma_start(out=slots_dram, out_offset=bass.IndirectOffsetOnAxis(ap=SL[k][:, t:t + 1], axis=0),
                                            in_=HR[:, t, :], in_offset=None).then_inc(scat, 16)
            pool.wait_ge(scat, TILES * TOP * 16)

        @block.tensor
        def _(pe):
            def three(out, pairs):
                terms = [t for (ah, al), (bh, bl) in pairs for t in ((ah, bh), (ah, bl), (al, bh))]
                for i, (a, b) in enumerate(terms):
                    ins = nc.tensor.matmul(out, a, b, start=(i == 0), stop=(i == len(terms) - 1))
                return ins

            pe.wait_ge(pc, 8)
            pe.wait_ge(w_lo, SPIECES + 1)
            for b in range(B):
                for t in range(NT):
                    i = b * NT + t
                    if i >= 2:
                        pe.wait_ge(wk_free, i - 1)
                    pe.wait_ge(h_ready, i + 1)
                    for k in range(KT):
                        ins = nc.tensor.transpose(WK[i % 2][:, k * P:(k + 1) * P], HR[:, i, k * P:(k + 1) * P], ident[:])
                    ins.then_inc(wk_ready, 1)
                if b:
                    pe.wait_ge(lg_free, b)
                for t in range(NT):
                    pe.wait_ge(wk_free, b * NT + t + 1)
                    c = slice(t * P, (t + 1) * P)
                    ins = three(LG[:, t * E:(t + 1) * E], [((HT[0][:, k, c], HT[1][:, k, c]), (RW[0][:, k, :], RW[1][:, k, :]))
                                                           for k in range(KT)])
                ins.then_inc(lg_ready, 1)
            pe.wait_ge(oh_ready, 1)
            flat = lambda ap: ap.rearrange("p t e -> p (t e)")
            nc.tensor.matmul(RB[:, 0:TILES * E], lower[:], flat(OHb[:]), start=True, stop=False, skip_group_check=True)
            for t in range(TILES - 1):
                n = TILES - 1 - t
                ins = nc.tensor.matmul(RB[:, (t + 1) * E:TILES * E].rearrange("p (t e) -> p t e", e=E), ones[:],
                                       OHb[:, t:t + 1, :].broadcast_to([P, n, E]), start=False, stop=(n == 1),
                                       skip_group_check=True)
            for t in range(TILES):
                ins = nc.tensor.matmul(CB[:, 0:E], ones[:], OHb[:, t, :], start=(t == 0), stop=(t == TILES - 1))
            ins.then_inc(rk_ready, 1)

            W0 = TILES
            for b in range(B):
                base = W0 + b * 2 * NT
                def transposes(b, base):
                    for t in range(NT):
                        pe.wait_ge(wk_free, base + t - 1)
                        for k in range(KT):
                            ins = nc.tensor.transpose(WK[t % 2][:, k * P:(k + 1) * P], HR[:, b * NT + t, k * P:(k + 1) * P], ident[:])
                        ins.then_inc(wk_ready, 1)
                if b == 0:
                    transposes(0, W0)
                    pe.wait_ge(wk_free, W0 + NT)
                else:
                    pe.wait_ge(wk_free, W0 + b * 2 * NT)
                for f in range(FT):
                    for i, c0 in enumerate((0, FF)):
                        n = 2 * f + i
                        if b:
                            pe.wait_ge(at0_ready, (b - 1) * FT + f + 1)
                        elif n < 2:
                            pe.wait_ge(sl_ready, 1)
                        c = slice(c0 + f * P, c0 + (f + 1) * P)
                        three(GU[n][:], [((WS[0][:, k, c], WS[1][:, k, c]), (HT[0][:, k, :], HT[1][:, k, :]))
                                         for k in range(KT)]).then_inc(gu_ready, 1)
                if b < B - 1:
                    transposes(b + 1, W0 + NT + b * 2 * NT)
                at = down_at(b)
                for t in range(NT):
                    pe.wait_ge(wk_free, at + t - 1)
                    if t == 0:
                        pe.wait_ge(at_ready, FT * (b + 1))
                    c = slice(t * P, (t + 1) * P)
                    three(WK[t % 2][:], [((AT[0][:, f, c], AT[1][:, f, c]), (WSD[0][:, f, :], WSD[1][:, f, :]))
                                         for f in range(FT)]).then_inc(wk_ready, 1)

        @block.scalar
        def _(act):
            act.wait_ge(rw_in, 16)
            nc.scalar.activation(RW[0][:], RWf[:], ACT.Copy).then_inc(w_hi, 1)
            for k in range(SPIECES):
                act.wait_ge(w_in[k % 2], 32 * (k // 2 + 1) if k < KT else 32 * (KT // 2) + 16)
                dst = WS[0][:, k, :] if k < KT else WSD[0][:, k - KT, :]
                nc.scalar.activation(dst, SG[:, k % 2, :], ACT.Copy).then_inc(w_hi, 1)

            def hi_h(base, hi):
                for t in range(NT):
                    act.wait_ge(wk_ready, base + t + 1)
                    if hi and t == 0:
                        act.wait_ge(*hi)
                    nc.scalar.activation(HT[0][:, :, t * P:(t + 1) * P], WK[t % 2][:].rearrange("p (k n) -> p k n", k=KT),
                                         ACT.Copy).then_inc(hi_ready, 1)

            for b in range(B):
                hi_h(b * NT, (lg_ready, b) if b else None)
            act.wait_ge(e2_in, 1)
            nc.scalar.activation(G[1][:], G[1][:], ACT.Exp).then_inc(e2_out, 1)
            hi_h(TILES, (lg_ready, B))

            for b in range(B):
                for f in range(FT):
                    act.wait_ge(gu_ready, (b * FT + f) * 2 + 1)
                    if b:
                        act.wait_ge(at_ready, (b - 1) * FT + f + 1)
                    nc.scalar.activation(SG[:, f, :], GU[2 * f][:], ACT.Silu).then_inc(sg_ready, 1)
                if b < B - 1:
                    hi_h(TILES + NT + b * 2 * NT, (gu_ready, (b + 1) * 2 * FT))
                for f in range(FT):
                    act.wait_ge(at0_ready, b * FT + f + 1)
                    if b and f == 0:
                        act.wait_ge(wk_ready, down_at(b - 1) + NT)
                    nc.scalar.activation(AT[0][:, f, :], SG[:, f, :], ACT.Copy).then_inc(at_hi, 1)

        @block.vector
        def _(dve):
            d = Tick(0)

            def lo_h(base, hi):
                for t in range(NT):
                    dve.wait_ge(wk_ready, base + t + 1)
                    dve.wait_ge(hi_ready, hi + t + 1)
                    c = slice(t * P, (t + 1) * P)
                    nc.vector.tensor_tensor(HT[1][:, :, c], WK[t % 2][:].rearrange("p (k n) -> p k n", k=KT),
                                            HT[0][:, :, c].bitcast(F32), ALU.subtract).then_inc(wk_free, 1)

            def statistics(b):
                for t in range(NT):
                    dve.wait_ge(x_in[t], 16 * (b + 1))
                    nc.vector.bn_stats(stats[:, t % 2, :], XB[:, t, :]).then_inc(dv, 1)
                    dve.wait_ge(dv, d.up())
                    if t == 0 and b:
                        dve.wait_ge(h0_ready, b * NT)
                    ins = nc.vector.bn_aggr(mv[:, t, :], stats[:, t % 2, :])
                ins.then_inc(var_ready, 1)

            dve.wait_ge(w_hi, 1)
            nc.vector.tensor_tensor(RW[1][:], RWf[:], RW[0][:].bitcast(F32), ALU.subtract).then_inc(w_lo, 1)
            statistics(0)
            for k in range(SPIECES):
                dve.wait_ge(w_hi, k + 2)
                pr, n = (WS, k) if k < KT else (WSD, k - KT)
                nc.vector.tensor_tensor(pr[1][:, n, :], SG[:, k % 2, :], pr[0][:, n, :].bitcast(F32), ALU.subtract).then_inc(w_lo, 1)
            for b in range(B):
                dve.wait_ge(rs_ready, b + 1)
                for t in range(NT):
                    nc.vector.tensor_scalar(HR[:, b * NT + t, :], XB[:, t, :], mv[:, t, 0:1], rs[:, t:t + 1], ALU.subtract,
                                            ALU.mult).then_inc(h0_ready, 1)
                if b < B - 1:
                    statistics(b + 1)
                lo_h(b * NT, b * NT)
                dve.wait_ge(lg_ready, b + 1)
                nc.vector.tensor_copy(L[:, b * NT:(b + 1) * NT, :], LG[:, 0:NT * E].rearrange("p (t e) -> p t e", e=E)
                                      ).then_inc(lg_free, 1)
            dve.wait_ge(lg_free, B)
            for t in range(TILES):
                nc.vector.max(M8[:, t, :], L[:, t, :]).then_inc(dv, 1)
            dve.wait_ge(dv, d.up(TILES))
            for t in range(TILES):
                nc.vector.max_index(I8[:, t, :], M8[:, t, :], L[:, t, :]).then_inc(dv, 1)
            nc.vector.tensor_tensor(G[1][:], M8[:, :, 1], M8[:, :, 0], ALU.subtract).then_inc(e2_in, 1)
            dve.wait_ge(dv, d.up(TILES))
            nc.vector.tensor_copy(I8f[:], I8[:]).then_inc(dv, 1)
            dve.wait_ge(dv, d.up())
            dve.wait_ge(c_in, 16)
            experts = c_expert.unsqueeze(1).broadcast_to([P, TILES, E])
            for k in range(TOP):
                nc.vector.tensor_tensor(OH[k][:], I8f[:, :, k:k + 1].broadcast_to([P, TILES, E]), experts, ALU.is_equal
                                        ).then_inc(dv, 1)
            dve.wait_ge(dv, d.up(TOP))
            nc.vector.tensor_tensor(OHb[:], OH[0][:], OH[1][:], ALU.add).then_inc(oh_ready, 1)
            dve.wait_ge(e2_out, 1)
            nc.vector.tensor_scalar(G[0][:], G[1][:], 1.0, None, ALU.add).then_inc(dv, 1)
            dve.wait_ge(dv, d.up())
            nc.vector.reciprocal(G[0][:], G[0][:]).then_inc(dv, 1)
            dve.wait_ge(dv, d.up())
            nc.vector.tensor_tensor(G[1][:], G[1][:], G[0][:], ALU.mult).then_inc(dv, 1)
            dve.wait_ge(dv, d.up())
            dve.wait_ge(rk_ready, 1)
            nc.vector.tensor_copy(cnt[:], CB[:, 0:E]).then_inc(dv, 1)
            dve.wait_ge(dv, d.up())
            nc.vector.tensor_tensor(gt[:], cnt[:].unsqueeze(2).broadcast_to([P, E, TILES]),
                                    c_full.unsqueeze(1).broadcast_to([P, E, TILES]), ALU.is_gt).then_inc(dv, 1)
            dve.wait_ge(dv, d.up())
            nc.vector.tensor_reduce(ntl[:], gt[:], AX_X, ALU.add).then_inc(dv, 1)
            dve.wait_ge(dv, d.up())
            nc.vector.tensor_tensor(gt[:, :, 0:E], ntl[:].unsqueeze(1).broadcast_to([P, E, E]), c_before, ALU.mult).then_inc(dv, 1)
            dve.wait_ge(dv, d.up())
            nc.vector.tensor_reduce(base[:], gt[:, :, 0:E], AX_X, ALU.add).then_inc(dv, 1)
            dve.wait_ge(dv, d.up())
            nc.vector.tensor_scalar(cnt[:], base[:], float(P), None, ALU.mult).then_inc(dv, 1)
            dve.wait_ge(dv, d.up())
            nc.vector.tensor_tensor(RK[:], RB[:, 0:TILES * E].rearrange("p (t e) -> p t e", e=E),
                                    cnt[:].unsqueeze(1).broadcast_to([P, TILES, E]), ALU.add).then_inc(dv, 1)
            dve.wait_ge(dv, d.up())
            for k in range(TOP):
                nc.vector.tensor_tensor(TMP[:], RK[:], OH[k][:], ALU.mult).then_inc(dv, 1)
                dve.wait_ge(dv, d.up())
                nc.vector.tensor_reduce(slf[:], TMP[:], AX_X, ALU.add).then_inc(dv, 1)
                dve.wait_ge(dv, d.up())
                nc.vector.tensor_copy(SL[k][:], slf[:]).then_inc(sl_ready, 1)
                dve.wait_ge(sl_ready, k + 1)
            nc.vector.tensor_tensor(base[:], base[:], ntl[:], ALU.add).then_inc(dv, 1)
            dve.wait_ge(dv, d.up())
            nc.vector.tensor_tensor(le[:], base[:, 0:E - 1].unsqueeze(1).broadcast_to([P, SLOT_TILES, E - 1]),
                                    c_tile.unsqueeze(2).broadcast_to([P, SLOT_TILES, E - 1]), ALU.is_le).then_inc(dv, 1)
            dve.wait_ge(dv, d.up())
            nc.vector.tensor_reduce(eidf[:], le[:], AX_X, ALU.add).then_inc(dv, 1)
            dve.wait_ge(dv, d.up())
            nc.vector.tensor_copy(EID[:], eidf[:]).then_inc(dv, 1)
            dve.wait_ge(dv, d.up())

            lo_h(TILES, TILES)
            for b in range(B):
                for f in range(FT):
                    dve.wait_ge(gu_ready, (b * FT + f) * 2 + 2)
                    dve.wait_ge(sg_ready, b * FT + f + 1)
                    nc.vector.tensor_tensor(SG[:, f, :], GU[2 * f + 1][:], SG[:, f, :], ALU.mult).then_inc(at0_ready, 1)
                if b < B - 1:
                    lo_h(TILES + NT + b * 2 * NT, TILES + (b + 1) * NT)
                for f in range(FT):
                    dve.wait_ge(at_hi, b * FT + f + 1)
                    nc.vector.tensor_tensor(AT[1][:, f, :], SG[:, f, :], AT[0][:, f, :].bitcast(F32), ALU.subtract).then_inc(at_ready, 1)
                at = down_at(b)
                for t in range(NT):
                    dve.wait_ge(wk_ready, at + t + 1)
                    dve.wait_ge(x_in[t], 16 * (B + b + 1))
                    i = b * NT + t
                    if i == 0:
                        dve.wait_ge(scat, TILES * TOP * 16)
                    nc.vector.tensor_tensor(HR[:, i, :], WK[t % 2][:], XB[:, t, :], ALU.add).then_inc(wk_free, 1)


def routed(nc, slots_dram, y_dram, WGU, WD, EID, w_in):
    with ExitStack() as st:
        sb = lambda name, shape, dt=F32: st.enter_context(nc.sbuf_tensor(name, shape, dt))
        banks = lambda name: [st.enter_context(nc.psum_tensor(f"{name}{i}", [P, 512], F32)) for i in range(2)]
        sem = lambda name: st.enter_context(nc.semaphore(name))
        XG, XT, YO = sb("XG", [P, 2, D]), sb("XTs", [P, 2, KT, P]), sb("YO", [P, 2, D])
        SGt, HH, HT = sb("SGt", [P, 2, FF]), sb("HH", [P, 2, FF]), sb("HTs", [P, 2, FT, P])
        ident = sb("ident3", [P, P])
        PX, PG, PH, PD = banks("PX"), banks("PG"), banks("PH"), banks("PD")
        pc = sem("r_pc")
        xg_in, y_out = [sem(f"r_xg{i}") for i in range(2)], [sem(f"r_yo{i}") for i in range(2)]
        px_ready, xt_ready, gu_ready, sg_ready, h_ready, ph_ready, ht_ready, pd_ready, yo_ready = [
            sem(f"r_{n}") for n in ("px", "xt", "gu", "sg", "h", "ph", "ht", "pd", "yo")]
        block = st.enter_context(nc.Block())
        N = SLOT_TILES
        FIRST, PAIRS = 3, (N - 5) // 2
        LAST = FIRST + 2 * PAIRS
        rows = lambda dram, i: dram[bass.ds(i * P, P), :]

        def over_tiles(eng, step):
            for i in range(FIRST):
                step(i, i % 2)
            with eng.Fori(0, PAIRS) as p:
                step(FIRST + 2 * p, 1)
                step(FIRST + 1 + 2 * p, 0)
            for i in range(LAST, N + 1):
                step(i, i % 2)

        @block.sync
        def _(sp):
            for i in range(2):
                sp.dma_start(XG[:, i, :], rows(slots_dram, i)).then_inc(xg_in[i], 16)

            def step(i, s):
                k = isinstance(i, int)
                if not (k and i < 1):
                    sp.wait_ge(yo_ready, i)
                    sp.dma_start(rows(y_dram, i - 1), YO[:, 1 - s, :]).then_inc(y_out[1 - s], 16)
                if not (k and i + 2 >= N):
                    sp.wait_ge(px_ready, i + 1)
                    sp.dma_start(XG[:, s, :], rows(slots_dram, i + 2)).then_inc(xg_in[s], 16)

            over_tiles(sp, step)
            for s in range(2):
                sp.wait_ge(y_out[s], 16 * ((N + 1 - s) // 2))

        @block.gpsimd
        def _(pool):
            nc.gpsimd.memset(ident[:], 0.0).then_inc(pc, 1)
            pool.wait_ge(pc, 1)
            nc.gpsimd.affine_select(out=ident[:], in_=ident[:], compare_op=ALU.not_equal, fill=1.0, base=0,
                                    pattern=[[-1, P]], channel_multiplier=1).then_inc(pc, 1)

        @block.tensor
        def _(pe):
            pe.wait_ge(pc, 2)
            pe.wait_ge(w_in, 16 * 3 * E)

            def turn(i, s, n_before):
                pe.wait_ge(xg_in[s], 16 * (n_before + 1))
                if not (isinstance(i, int) and i < 2):
                    pe.wait_ge(xt_ready, i - 1)
                for k in range(KT):
                    ins = nc.tensor.transpose(PX[s][:, k * P:(k + 1) * P], XG[:, s, k * P:(k + 1) * P], ident[:])
                ins.then_inc(px_ready, 1)

            turn(0, 0, 0)

            def step(i, s, e_before, of_parity):
                k0, e = isinstance(i, int), None
                if not (k0 and i >= N):
                    e = load(i)
                    pe.wait_ge(xt_ready, i + 1)
                    if not (k0 and i < 2):
                        pe.wait_ge(h_ready, i - 1)
                    for k in range(KT):
                        ins = nc.tensor.matmul(PG[s][:], XT[:, s, k, :], WGU[:, bass.ds(e, 1), k, :].rearrange("p o n -> p (o n)"),
                                               start=(k == 0), stop=(k == KT - 1))
                    ins.then_inc(gu_ready, 1)
                if not (k0 and i < 1):
                    pe.wait_ge(ht_ready, i)
                    if not (k0 and i < 3):
                        pe.wait_ge(yo_ready, i - 2)
                    for f in range(FT):
                        ins = nc.tensor.matmul(PD[1 - s][:], HT[:, 1 - s, f, :],
                                               WD[:, bass.ds(e_before, 1), f, :].rearrange("p o n -> p (o n)"),
                                               start=(f == 0), stop=(f == FT - 1))
                    ins.then_inc(pd_ready, 1)
                if not (k0 and i + 1 >= N):
                    turn(i + 1, 1 - s, of_parity)
                if not (k0 and i >= N):
                    pe.wait_ge(h_ready, i + 1)
                    for f in range(FT):
                        ins = nc.tensor.transpose(PH[s][:, f * P:(f + 1) * P], HH[:, s, f * P:(f + 1) * P], ident[:])
                    ins.then_inc(ph_ready, 1)
                return e

            def load(i):
                return nc.tensor.value_load(EID[0:1, i:i + 1] if isinstance(i, int) else EID[0:1, bass.ds(i, 1)],
                                            min_val=0, max_val=E - 1)

            e = None
            for i in range(FIRST):
                e = step(i, i % 2, e, i // 2 + (i % 2))
            with pe.Fori(0, PAIRS) as p:
                e = step(FIRST + 2 * p, 1, load(FIRST - 1 + 2 * p), p + 2)
                step(FIRST + 1 + 2 * p, 0, e, p + 2)
            e = load(LAST - 1)
            for i in range(LAST, N + 1):
                e = step(i, i % 2, e, i // 2 + (i % 2))

        @block.scalar
        def _(act):
            def turned(i, s):
                act.wait_ge(px_ready, i + 1)
                if not (isinstance(i, int) and i < 2):
                    act.wait_ge(gu_ready, i - 1)
                nc.scalar.activation(XT[:, s, :, :], PX[s][:].rearrange("p (k n) -> p k n", k=KT), ACT.Copy).then_inc(xt_ready, 1)

            turned(0, 0)

            def step(i, s):
                k = isinstance(i, int)
                if not (k and i >= N):
                    act.wait_ge(gu_ready, i + 1)
                    if not (k and i < 2):
                        act.wait_ge(h_ready, i - 1)
                    nc.scalar.activation(SGt[:, s, :], PG[s][:, 0:FF], ACT.Silu).then_inc(sg_ready, 1)
                if not (k and i + 1 >= N):
                    turned(i + 1, 1 - s)

            over_tiles(act, step)

        @block.vector
        def _(dve):
            def step(i, s, stored):
                k = isinstance(i, int)
                if not (k and i >= N):
                    dve.wait_ge(sg_ready, i + 1)
                    if not (k and i < 2):
                        dve.wait_ge(ph_ready, i - 1)
                    nc.vector.tensor_tensor(HH[:, s, :], PG[s][:, FF:2 * FF], SGt[:, s, :], ALU.mult).then_inc(h_ready, 1)
                if not (k and i < 1):
                    dve.wait_ge(pd_ready, i)
                    if not (k and i < 3):
                        dve.wait_ge(y_out[1 - s], 16 * stored)
                    nc.vector.tensor_copy(YO[:, 1 - s, :], PD[1 - s][:]).then_inc(yo_ready, 1)
                if not (k and i >= N):
                    dve.wait_ge(ph_ready, i + 1)
                    if not (k and i < 2):
                        dve.wait_ge(pd_ready, i - 1)
                    nc.vector.tensor_copy(HT[:, s, :, :], PH[s][:, 0:FF].rearrange("p (f n) -> p f n", f=FT)).then_inc(ht_ready, 1)

            for i in range(FIRST):
                step(i, i % 2, (i - 1) // 2)
            with dve.Fori(0, PAIRS) as p:
                step(FIRST + 2 * p, 1, p + 1)
                step(FIRST + 1 + 2 * p, 0, p + 1)
            for i in range(LAST, N + 1):
                step(i, i % 2, (i - 1) // 2)


def combine(nc, y_dram, out, ACC, G, SL):
    R = 4
    with ExitStack() as st:
        Y = [st.enter_context(nc.sbuf_tensor(f"Yc{k}", [P, R, D], F32)) for k in range(TOP)]
        y_in = [[st.enter_context(nc.semaphore(f"c_in{k}{r}")) for r in range(R)] for k in range(TOP)]
        a, done, o = [st.enter_context(nc.semaphore(f"c_{n}")) for n in ("a", "done", "o")]
        block = st.enter_context(nc.Block())

        @block.gpsimd
        def _(pool):
            for t in range(TILES):
                if t >= R:
                    pool.wait_ge(done, t - R + 1)
                for k in range(TOP):
                    pool.indirect_dma_start(out=Y[k][:, t % R, :], out_offset=None, in_=y_dram,
                                            in_offset=bass.IndirectOffsetOnAxis(ap=SL[k][:, t:t + 1], axis=0)
                                            ).then_inc(y_in[k][t % R], 16)

        @block.vector
        def _(dve):
            for t in range(TILES):
                for k in range(TOP):
                    dve.wait_ge(y_in[k][t % R], 16 * (t // R + 1))
                    if k:
                        dve.wait_ge(a, t + 1)
                    nc.vector.scalar_tensor_tensor(out=ACC[:, t, :], in0=Y[k][:, t % R, :], scalar=G[k][:, t:t + 1],
                                                   in1=ACC[:, t, :], op0=ALU.mult, op1=ALU.add).then_inc(done if k else a, 1)

        @block.sync
        def _(sp):
            ov = out.rearrange("b (t p) d -> (b t) p d", p=P)
            for t in range(TILES):
                sp.wait_ge(done, t + 1)
                sp.dma_start(ov[t], ACC[:, t, :]).then_inc(o, 16)
            sp.wait_ge(o, 16 * TILES)


def build(nc, io, out):
    x2 = nc.dram_tensor("x2_dram", [B, S, D], F32, kind="Internal").ap()
    slots = nc.dram_tensor("slots_dram", [SLOT_TILES * P, D], F32, kind="Internal").ap()
    y = nc.dram_tensor("y_dram", [SLOT_TILES * P, D], F32, kind="Internal").ap()
    attention_part(nc, io, x2)
    with ExitStack() as st:
        sb = lambda name, shape, dt=F32: st.enter_context(nc.sbuf_tensor(name, shape, dt))
        HR = sb("HR", [P, TILES, D])
        G = [sb(f"G{k}", [P, TILES]) for k in range(TOP)]
        SL = [sb(f"SL{k}", [P, TILES], mybir.dt.int32) for k in range(TOP)]
        EID = sb("EID", [P, SLOT_TILES], mybir.dt.int32)
        WGU, WD = sb("WGU", [P, E, KT, 2 * FF]), sb("WDn", [P, E, FT, D])
        w_in, z_out = st.enter_context(nc.semaphore("exp_w_in")), st.enter_context(nc.semaphore("z_out"))
        zr = st.enter_context(nc.semaphore("zr"))
        with nc.Block() as block:
            @block.gpsimd
            def _(pool):
                nc.gpsimd.memset(HR[:, 0, :], 0.0).then_inc(zr, 1)

            @block.sync
            def _(sp):
                sp.wait_ge(zr, 1)
                for i in range(SLOT_TILES):
                    sp.dma_start(slots[i * P:(i + 1) * P, :], HR[:, 0, :]).then_inc(z_out, 16)
                sp.wait_ge(z_out, 16 * SLOT_TILES)

            @block.scalar
            def _(act):
                for e in range(E):
                    act.dma_start(WGU[:, e, :, 0:FF], io["wg"][e].rearrange("(k p) f -> p k f", p=P)).then_inc(w_in, 16)
                    act.dma_start(WGU[:, e, :, FF:2 * FF], io["wu"][e].rearrange("(k p) f -> p k f", p=P)).then_inc(w_in, 16)
                    act.dma_start(WD[:, e, :, :], io["wd"][e].rearrange("(f p) d -> p f d", p=P)).then_inc(w_in, 16)
        router_and_shared(nc, io, x2, slots, HR, G, SL, EID)
        routed(nc, slots, y, WGU, WD, EID, w_in)
        combine(nc, y, out, HR, G, SL)


NAMES = {"x": "x", "ctx_512": "ctx", "mask_SxS2_bk1": "am", "mask_BxS2_bf0": "km", "L0_attn_W_qkv": "wqkv",
         "L0_attn_W_o": "wo", "L0_xattn_Wq": "xwq", "L0_xattn_bq": "xbq", "L0_xattn_Wk": "xwk",
         "L0_xattn_bk": "xbk", "L0_ffn_rms_weight": "rms", "L0_ffn_router_w": "router", "L0_ffn_w_gate": "wg",
         "L0_ffn_w_up": "wu", "L0_ffn_w_down": "wd", "L0_ffn_sw_gate": "swg", "L0_ffn_sw_up": "swu",
         "L0_ffn_sw_down": "swd"}


def extra():
    return {"cst": routing_constants()}


def kernel(**inputs):
    import concourse.bacc as bacc
    from concourse.bass_utils import run_bass_kernel_spmd

    nc = bacc.Bacc("TRN2", target_bir_lowering=False, num_devices=1)
    alibi_q, alibi_k = alibi_rows()
    arrays = {NAMES[name]: np.ascontiguousarray(a) for name, a in inputs.items()}
    arrays.update(alq=alibi_q, alk=alibi_k, cst=routing_constants())
    io = {n: nc.dram_tensor(n, a.shape, mybir.dt.from_np(a.dtype), kind="ExternalInput").ap() for n, a in arrays.items()}
    out = nc.dram_tensor("out", (B, S, D), F32, kind="ExternalOutput").ap()
    build(nc, io, out)
    result = run_bass_kernel_spmd(nc, [arrays], core_ids=[0])
    return result.results[0]["out"]
```

```python
from contextlib import ExitStack

import numpy as np

import concourse.bass as bass
from concourse import mybir

F32 = mybir.dt.float32
F32R = mybir.dt.float32r
BF16 = mybir.dt.bfloat16
U8 = mybir.dt.uint8
ALU = mybir.AluOpType
ACT = mybir.ActivationFunctionType
AX_X = mybir.AxisListType.X

P = 128
B, S, D = 4, 512, 512
HEADS, HD = 16, 32
CTX = 128
NT = S // P
KT = D // P
GROUPS = 4
HPG = HEADS // GROUPS
E, FF = 8, 256
FT = FF // P
TILES = B * NT
TOP = 2
SLOT_TILES = (TOP * TILES * P + E * (P - 1)) // P
LN_EPS, RMS_EPS = 1e-5, 1e-6
ATT_SCALE = HD ** -0.5
X_SCALE = CTX ** -0.5
MASK = -1.5e38
LEAST = -1.0e37
MASKED = -1e30
ROW_ALIBI, ROW_MAX, ROW_END = 3 * HD, 3 * HD + 4, 3 * HD + 6
SM_PIECES = [(0, 0, 4), (1, 0, 2), (1, 2, 2)] + [(q, j, 1) for q in (2, 3) for j in range(HPG)]
N_SM = len(SM_PIECES) + 1
SM_GROUPS = ((0, 1, 2), (3, 4, 5), (6, 7, 8), (9, 10))
PROJ_PARTS = (range(0, KT // 2), range(KT // 2, KT))
ST_PIECES = ((0,), (1, 3), (2,))
N_ST = len(ST_PIECES) * HPG
P_AT = {0: 0, 1: 512, 3: 896, 2: 1024}
N_V, N_WO, N_CTX, N_PROJ, N_XT = NT, NT, 4, 2, NT
ZERO_PARTS = GROUPS
WK_START = N_XT + N_PROJ
WK_BEFORE = N_WO + N_CTX + GROUPS
WK_PER = N_V + GROUPS * N_PROJ + N_XT + WK_BEFORE
HI_PER = GROUPS * N_PROJ + N_XT
STACK_SP, STACK_POOL = 4 * HPG, 2 * HPG


def alibi_rows():
    slope = (2.0 ** (-8.0 / np.arange(1, HEADS + 1, dtype=np.float32))).astype(np.float32)
    hi = (slope.view(np.uint32) & np.uint32(0xFFFFF000)).view(np.float32)
    lo = slope - hi
    pos = np.arange(S, dtype=np.float32) - S // 2
    q = np.zeros((ROW_MAX - ROW_ALIBI, HEADS, S), np.float32)
    k = np.zeros((ROW_END - ROW_ALIBI, HEADS, S), np.float32)
    q[0], q[1], q[2], q[3] = hi[:, None], lo[:, None], pos, pos
    k[0], k[1], k[2], k[3] = pos, pos, -hi[:, None], -lo[:, None]
    k[4:] = 1.0
    return q, k


def raw(ap):
    return ap.bitcast(F32)


class Tick:

    def __init__(self, base=0):
        self.base, self.n = base, 0

    def up(self, k=1):
        self.n += k
        return self.base + self.n

    def now(self):
        return self.base + self.n


def nth(s, g):
    return s.b * (GROUPS // 2) + g // 2 + 1


class Step:

    def __init__(self, b, first=False, last=False, tail=False):
        self.b, self.first, self.last, self.tail = b, first, last, tail
        self.main = not tail
        self.before = not first
        self.wk_base = WK_START + b * WK_PER - (0 if first else WK_BEFORE) - (WK_START if tail else 0)

    def projects(self, g):
        return self.main and not (self.last and g == GROUPS - 1)

    def turns(self, g):
        return self.main and not self.last and g == GROUPS - 1


def over_batches(eng, body):
    body(Step(0, first=True))
    with eng.Fori(1, B - 1) as b:
        body(Step(b))
    body(Step(B - 1, last=True))
    body(Step(B, tail=True))


def attention_part(nc, io, x2_dram, mv_dram, slots_dram):
    with ExitStack() as st:
        sb = lambda name, shape, dt=F32: st.enter_context(nc.sbuf_tensor(name, shape, dt))
        banks = lambda name: [st.enter_context(nc.psum_tensor(f"{name}{i}", [P, 512], F32)) for i in range(2)]
        sem = lambda name: st.enter_context(nc.semaphore(name))
        pair = lambda name, shape: [sb(f"{name}_{p}", shape, F32R) for p in ("hi", "lo")]

        Wqk, Wv, Wo = pair("Wqk", [P, KT, 2 * D]), pair("Wv", [P, KT, D]), pair("Wo", [P, KT, D])
        XT = pair("XT", [P, KT, S])
        QS, KS = sb("QS", [P, 2, HPG, S], F32R), sb("KS", [P, 2, HPG, S], F32R)
        qT, kT = pair("qT", [P, S]), pair("kT", [P, S])
        V = sb("V", [P, NT, HEADS // 2, 3 * HD])
        PT = sb("PT", [P, 2, 1280])
        Yf, Sf = sb("Yf", [P, S]), sb("Sf", [P, S])
        Y = pair("Y", [P, GROUPS, S])
        NM = sb("NM", [P, HPG * NT])
        MT = pair("MT", [HPG * NT, P])
        XN = sb("XN", [P, 2, D])
        XL, XR = sb("XL", [P, NT, D]), sb("XR", [P, NT, D])
        Z, SC, AK = sb("Z", [P, D]), sb("SC", [P, D]), sb("AK", [P, D], BF16)
        CX = Z[:].rearrange("p (t c) -> p t c", t=NT)
        ctxT, qpT, kpT = sb("ctxT", [P, S]), sb("qpT", [P, S]), sb("kpT", [P, S])
        XW, XWT, bqk = sb("XW", [P, 2, P]), sb("XWT", [P, 2, P]), sb("bqk", [P, 2])
        AM, KM = sb("AM", [P, NT, S], BF16), sb("KM", [P, B, S], BF16)
        ident, identb = sb("ident", [P, P]), sb("identb", [P, P], BF16)
        causal, causalT = sb("causal", [P, P], BF16), sb("causalT", [P, P], BF16)
        stats = sb("stats", [P, NT, 6])
        mv1, rs1 = sb("mv1", [P, NT, 2]), sb("rs1", [P, NT])
        mv2, rs2 = sb("mv2", [P, NT, 2]), sb("rs2", [P, NT])
        mv3 = sb("mv3a", [P, NT, 2])
        mhalf = sb("mhalf", [P, NT])
        idle = sb("idle", [P, 2])
        col = sb("col", [P, 4])
        W_STAGE = [PT[:, :, :].rearrange("p a n -> p (a n)"), V[:, :, :, :].rearrange("p t m n -> p (t m n)")]
        AM_U8 = Yf[:].bitcast(U8).rearrange("p (t s) -> p t s", t=NT)
        KM_U8 = Sf[:].bitcast(U8).rearrange("p (t s) -> p t s", t=B)

        SM, ST, O, WK = banks("SM"), banks("ST"), banks("O"), banks("WK")

        xl_in, xr_in, x2_out = sem("xl_in"), sem("xr_in"), sem("x2_out")
        x2_ready = sem("x2_ready")
        mv_ready = sem("mv_ready")
        zero_out = sem("zero_out")
        w_in = [sem(f"w_in{k}") for k in range(2)]
        am_in, km_in, xw_in = sem("am_in"), sem("km_in"), sem("xw_in")
        ctx_in = sem("ctx_in")
        alibi_in = [sem(f"alibi_in{i}") for i in range(2)]
        stack_in, stack_in2 = [[sem(f"stack_in_{q}{i}") for i in range(2)] for q in ("sp", "pool")]
        mrow_in = [sem(f"mrow_in{i}") for i in range(2)]
        pool_c = sem("pool_c")
        pool_s = sem("pool_s")
        ones_ready = sem("ones_ready")
        stat1, rs1_ready = sem("stat1"), sem("rs1_ready")
        stat2, rs2_ready = sem("stat2"), sem("rs2_ready")
        ak_ready = sem("ak_ready")
        w_hi, w_lo = sem("w_hi"), sem("w_lo")
        mask_ready = sem("mask_ready")
        xn_ready = sem("xn_ready")
        wk_ready, wk_free = sem("wk_ready"), sem("wk_free")
        hi_ready = sem("hi_ready")
        sm_ready, sm_free = sem("sm_ready"), sem("sm_free")
        st_ready, p_ready = sem("st_ready"), sem("p_ready")
        o_ready, o_free = sem("o_ready"), sem("o_free")
        y_done = sem("y_done")
        sc_ready, nm_ready, ex_ready = sem("sc_ready"), sem("nm_ready"), sem("ex_ready")
        dv = sem("dv")
        block = st.enter_context(nc.Block())

        @block.sync
        def _(sp):
            def tiles(dram, b):
                return dram[bass.ds(b, 1)].rearrange("o (t p) d -> p (o t) d", p=P)

            wv = io["wqkv"].rearrange("(k p) n -> k p n", p=P)
            wov = io["wo"].rearrange("(k p) n -> k p n", p=P)
            sp.dma_start(XL[:], tiles(io["x"], 0)).then_inc(xl_in, 16)
            for k in range(KT):
                if k >= 2:
                    sp.wait_ge(w_hi, 2 * (k - 1))
                    sp.wait_ge(w_lo, 2 * (k - 1))
                sp.dma_start(W_STAGE[k % 2][:, 0:3 * D], wv[k]).then_inc(w_in[k % 2], 16)
                sp.dma_start(W_STAGE[k % 2][:, 3 * D:4 * D], wov[k]).then_inc(w_in[k % 2], 16)
            sp.dma_start(AM_U8, io["am"].rearrange("(t p) s -> p t s", p=P)).then_inc(am_in, 16)
            for b in range(B):
                sp.dma_start(KM_U8[:, b, :], io["km"][b:b + 1, :].broadcast_to([P, S])).then_inc(km_in, 16)
            sp.dma_start(XW[:, 0, :], io["xwq"]).then_inc(xw_in, 16)
            sp.dma_start(XW[:, 1, :], io["xwk"]).then_inc(x2_out, 16)
            sp.dma_start(bqk[:, 0:1], io["xbq"].rearrange("(p a) -> p a", a=1)).then_inc(xw_in, 16)
            sp.dma_start(bqk[:, 1:2], io["xbk"].rearrange("(p a) -> p a", a=1)).then_inc(xw_in, 16)

            def stack(wk_done, slot):
                sp.wait_ge(wk_free, wk_done)
                for j in range(HPG):
                    r = slice(HD * j, HD * j + HD)
                    sp.dma_start(raw(QS[0:HD, slot, j, :]), raw(qT[0][r, :])).then_inc(stack_in[slot], 16)
                    sp.dma_start(raw(QS[HD:2 * HD, slot, j, :]), raw(qT[0][r, :])).then_inc(stack_in[slot], 16)
                    sp.dma_start(raw(KS[0:HD, slot, j, :]), raw(kT[0][r, :])).then_inc(stack_in[slot], 16)
                    sp.dma_start(raw(KS[2 * HD:3 * HD, slot, j, :]), raw(kT[0][r, :])).then_inc(stack_in[slot], 16)

            stack(WK_START, 0)

            def body(s):
                wk = Tick(s.wk_base)
                for g in range(GROUPS):
                    u = s.b * GROUPS + g
                    if g == 0:
                        if s.main:
                            wk.up(N_V)
                        if s.main and not s.last:
                            sp.wait_ge(xn_ready, (s.b + 1) * NT)
                            sp.dma_start(XL[:], tiles(io["x"], s.b + 1)).then_inc(xl_in, 16)
                        if s.before:
                            sp.wait_ge(wk_free, s.wk_base)
                            sp.dma_start(CX, tiles(io["ctx"], s.b - 1)).then_inc(ctx_in, 16)
                            sp.wait_ge(x2_out, s.b * 32 - 16)
                            sp.dma_start(XR[:], tiles(io["x"], s.b - 1)).then_inc(xr_in, 16)
                    if s.turns(g):
                        wk.up(N_XT)
                    if s.main:
                        sp.wait_ge(sm_free, (u + 1) * N_SM)
                        for i in range(2):
                            sp.dma_start(raw(QS[ROW_MAX + i:ROW_MAX + i + 1, g % 2, :, :]).rearrange(
                                "o j (q n) -> o (j q) n", q=NT), raw(MT[i][:, :])).then_inc(mrow_in[g % 2], 16)
                    if s.projects(g):
                        wk.up(N_PROJ)
                        stack(wk.now(), (g + 1) % 2)
                    if s.before:
                        wk.up(N_WO + N_CTX + 1 if g == 0 else 1)
                    if s.first:
                        n = SLOT_TILES // ZERO_PARTS
                        c = slice(g * n * P, (g + 1) * n * P if g < ZERO_PARTS - 1 else SLOT_TILES * P)
                        sp.dma_start(slots_dram[c, :].rearrange("(i p) d -> p i d", p=P),
                                     Z[:].unsqueeze(1).broadcast_to([P, (c.stop - c.start) // P, D])).then_inc(zero_out, 16)
                if s.first:
                    sp.wait_ge(zero_out, ZERO_PARTS * 16)
                if s.before:
                    sp.wait_ge(x2_ready, s.b * NT)
                    sp.dma_start(tiles(x2_dram, s.b - 1), XR[:]).then_inc(x2_out, 16)
                    sp.wait_ge(mv_ready, s.b * NT)
                    sp.dma_start(mv_dram[bass.ds(s.b - 1, 1)].rearrange("o p n -> p (o n)"),
                                 mv3[:].rearrange("p t n -> p (t n)")).then_inc(x2_out, 16)

            over_batches(sp, body)
            sp.wait_ge(x2_out, 16 + B * 32)

        @block.gpsimd
        def _(pool):
            nc.gpsimd.memset(ident[:], 0.0).then_inc(pool_c, 1)
            nc.gpsimd.memset(identb[:], 0.0).then_inc(pool_c, 1)
            nc.gpsimd.memset(causal[:], 0.0).then_inc(pool_c, 1)
            nc.gpsimd.memset(causalT[:], 0.0).then_inc(pool_c, 1)
            nc.gpsimd.memset(mhalf[:], -0.5).then_inc(pool_c, 1)
            nc.gpsimd.memset(Z[:], 0.0).then_inc(pool_c, 1)
            pool.wait_ge(pool_c, 6)
            for m in (ident, identb):
                nc.gpsimd.affine_select(out=m[:], in_=m[:], compare_op=ALU.not_equal, fill=1.0, base=0,
                                        pattern=[[-1, P]], channel_multiplier=1).then_inc(pool_c, 1)
            nc.gpsimd.affine_select(out=causal[:], in_=causal[:], compare_op=ALU.is_ge, fill=MASKED, base=0,
                                    pattern=[[-1, P]], channel_multiplier=1).then_inc(pool_c, 1)
            nc.gpsimd.affine_select(out=causalT[:], in_=causalT[:], compare_op=ALU.is_ge, fill=MASKED, base=0,
                                    pattern=[[1, P]], channel_multiplier=-1).then_inc(pool_c, 1)

            def rsqrt1(b):
                pool.wait_ge(stat1, b + 1)
                nc.gpsimd.tensor_tensor(rs1[:], rs1[:], mhalf[:], ALU.pow).then_inc(rs1_ready, 1)

            rsqrt1(0)

            def pause():
                if paused.n or not isinstance(paused.base, int) or paused.base:
                    pool.wait_ge(pool_s, paused.now())
                nc.gpsimd.tensor_tensor(idle[:, 0:1], mhalf[:, 0:1], mhalf[:, 0:1], ALU.mult).then_inc(pool_s, 1)
                paused.up()

            paused = Tick(0)
            def alibi(slot, heads):
                pool.dma_start(QS[ROW_ALIBI:ROW_MAX, slot, :, :], io["alq"][:, heads, :]).then_inc(alibi_in[slot], 16)
                pool.dma_start(KS[ROW_ALIBI:ROW_END, slot, :, :], io["alk"][:, heads, :]).then_inc(alibi_in[slot], 16)

            def stack(wk_done, slot):
                pool.wait_ge(wk_free, wk_done)
                pause()
                for j in range(HPG):
                    r = slice(HD * j, HD * j + HD)
                    pool.dma_start(raw(QS[2 * HD:3 * HD, slot, j, :]), raw(qT[1][r, :])).then_inc(stack_in2[slot], 16)
                    pool.dma_start(raw(KS[HD:2 * HD, slot, j, :]), raw(kT[1][r, :])).then_inc(stack_in2[slot], 16)

            alibi(0, slice(0, HPG))
            stack(WK_START, 0)
            first_pauses, pauses = 2 * GROUPS, 3 * GROUPS
            pool.wait_ge(w_hi, 2 * KT)
            pool.wait_ge(w_lo, 2 * KT)
            nc.gpsimd.memset(V[:, :, :, HD:2 * HD], 1.0).then_inc(ones_ready, 1)

            def body(s):
                nonlocal paused
                if not s.first:
                    paused = Tick(first_pauses + (s.b - 1) * pauses - (2 if s.tail else 0))
                wk = Tick(s.wk_base)
                for g in range(GROUPS):
                    u = s.b * GROUPS + g
                    if g == 0 and s.main:
                        wk.up(N_V)
                    if s.before:
                        if g == 0:
                            pool.wait_ge(mask_ready, B)
                        pool.wait_ge(sc_ready, (s.b - 1) * NT + g + 1)
                        pause()
                        nc.gpsimd.tensor_tensor(AK[:].rearrange("p (o s) -> p o s", o=1), AM[:, g:g + 1, :],
                                                KM[:, bass.ds(s.b - 1, 1), :], ALU.add).then_inc(ak_ready, 1)
                    if s.turns(g):
                        wk.up(N_XT)
                    if s.projects(g):
                        if not (s.first and g == 0):
                            pool.wait_ge(st_ready, u * N_ST)
                            pause()
                        h = HPG * ((g + 1) % GROUPS)
                        alibi((g + 1) % 2, slice(h, h + HPG))
                        wk.up(N_PROJ)
                        stack(wk.now(), (g + 1) % 2)
                    if g == 0 and s.before:
                        wk.up(N_WO + N_CTX)
                        pool.wait_ge(stat2, s.b)
                        nc.gpsimd.tensor_tensor(rs2[:], rs2[:], mhalf[:], ALU.pow).then_inc(rs2_ready, 1)
                    if s.before:
                        wk.up()
                    if g == 1 and s.main and not s.last:
                        rsqrt1(s.b + 1)

            over_batches(pool, body)

        @block.tensor
        def _(pe):
            def three(out, pairs, start=True, stop=True):
                terms = [t for (ah, al), (bh, bl) in pairs for t in ((ah, bh), (ah, bl), (al, bh))]
                for i, (a, b) in enumerate(terms):
                    ins = nc.tensor.matmul(out, a, b, start=start and i == 0, stop=stop and i == len(terms) - 1,
                                           skip_group_check=True)
                return ins

            def item(wk, free=True):
                n = wk.up()
                if free:
                    pe.wait_ge(wk_free, n - 2)
                return WK[(wk.n - 1) % 2]

            def turn_x(wk, b, tiles, start=False):
                for t in tiles:
                    bank = item(wk, free=not (start and t < 2))
                    pe.wait_ge(xn_ready, b * NT + t + 1)
                    for k in range(KT):
                        ins = nc.tensor.transpose(bank[:, k * P:(k + 1) * P], XN[:, t % 2, k * P:(k + 1) * P], ident[:])
                    ins.then_inc(wk_ready, 1)

            def project(wk, g, i, ks=range(KT)):
                if g == 0 and i == 0:
                    pe.wait_ge(wk_free, wk.now())
                bank = item(wk) if ks[0] == 0 else WK[(wk.n - 1) % 2]
                c = slice(i * D + g * P, i * D + g * P + P)
                ins = three(bank[:], [((Wqk[0][:, k, c], Wqk[1][:, k, c]), (XT[0][:, k, :], XT[1][:, k, :])) for k in ks],
                            start=ks[0] == 0, stop=ks[-1] == KT - 1)
                if ks[-1] == KT - 1:
                    ins.then_inc(wk_ready, 1)

            def row_maxima(s, g, u, pieces):
                if pieces[0] == 0:
                    pe.wait_ge(stack_in[g % 2], nth(s, g) * STACK_SP * 16)
                    pe.wait_ge(stack_in2[g % 2], nth(s, g) * STACK_POOL * 16)
                    pe.wait_ge(alibi_in[g % 2], nth(s, g) * 2 * 16)
                for i in pieces:
                    q, j0, nj = SM_PIECES[i]
                    if not (s.first and g == 0 and i < 2):
                        pe.wait_ge(sm_free, u * N_SM + i - 1)
                    bank, w = SM[i % 2], (q + 1) * P
                    for n in range(nj):
                        nc.tensor.matmul(bank[:, n * w:(n + 1) * w], QS[0:ROW_MAX, g % 2, j0 + n, q * P:(q + 1) * P],
                                         KS[0:ROW_MAX, g % 2, j0 + n, 0:w], start=(n == 0), stop=False,
                                         skip_group_check=True)
                        ins = nc.tensor.matmul(bank[:, (n + 1) * w - P:(n + 1) * w], identb[:], causal[:],
                                               start=False, stop=True, skip_group_check=True)
                    ins.then_inc(sm_ready, 1)

            def turn_maxima(u):
                pe.wait_ge(sm_free, (u + 1) * N_SM - 1)
                nc.tensor.transpose(SM[(N_SM - 1) % 2][0:HPG * NT, 0:P], NM[:], ident[:]).then_inc(sm_ready, 1)

            def scores(s, g, u, j):
                for n, piece in enumerate(ST_PIECES):
                    m = j * len(ST_PIECES) + n
                    if not (s.first and g == 0 and m < 2):
                        pe.wait_ge(p_ready, u * N_ST + m - 1)
                    bank, at = ST[m % 2], 0
                    for kb in piece:
                        w = S - kb * P
                        nc.tensor.matmul(bank[:, at:at + w], KS[0:ROW_END, g % 2, j, kb * P:(kb + 1) * P],
                                         QS[0:ROW_END, g % 2, j, kb * P:S], start=(at == 0), stop=False,
                                         skip_group_check=True)
                        ins = nc.tensor.matmul(bank[:, at:at + P], identb[:], causalT[:], start=False, stop=True,
                                               skip_group_check=True)
                        at += w
                    ins.then_inc(st_ready, 1)

            def values(s, g, u, j):
                i = u * HPG + j
                if not (s.first and g == 0 and j < 2):
                    pe.wait_ge(o_free, i - 1)
                pe.wait_ge(p_ready, (i + 1) * len(ST_PIECES))
                if g == 0 and j == 0:
                    pe.wait_ge(wk_free, s.wk_base + N_V)
                    pe.wait_ge(ones_ready, 1)
                h = g * HPG + j
                a = HD * (h % 2)
                for kb in range(NT):
                    at = P_AT[kb]
                    ins = nc.tensor.matmul(O[j % 2][0:2 * HD, kb * P:S], V[:, kb, h // 2, a:a + 2 * HD],
                                           PT[:, j % 2, at:at + S - kb * P], start=(kb == 0), stop=(kb == NT - 1),
                                           skip_group_check=True)
                ins.then_inc(o_ready, 1)

            wk = Tick(0)
            pe.wait_ge(pool_c, 10)
            turn_x(wk, 0, range(NT), start=True)
            pe.wait_ge(w_lo, 2 * KT)
            for i in range(N_PROJ):
                project(wk, 0, i)

            def body(s):
                wk = Tick(s.wk_base)
                for g in range(GROUPS):
                    u = s.b * GROUPS + g
                    for n in range(len(SM_GROUPS) if s.main else 0):
                        row_maxima(s, g, u, SM_GROUPS[n])
                        if g == 0:
                            bank, c = item(wk), slice(n * P, (n + 1) * P)
                            three(bank[:], [((XT[0][:, k, c], XT[1][:, k, c]), (Wv[0][:, k, :], Wv[1][:, k, :]))
                                            for k in range(KT)]).then_inc(wk_ready, 1)
                        elif s.turns(g):
                            turn_x(wk, s.b + 1, (n,))
                        elif s.projects(g) and n < 3:
                            project(wk, g + 1, n // 2, PROJ_PARTS[n % 2])
                    if s.main:
                        turn_maxima(u)
                    if s.projects(g):
                        if g == 0 or s.turns(g):
                            project(wk, (g + 1) % GROUPS, 0)
                            project(wk, (g + 1) % GROUPS, 1)
                        else:
                            project(wk, g + 1, 1, PROJ_PARTS[1])
                    if s.main:
                        pe.wait_ge(mrow_in[g % 2], nth(s, g) * 2 * 16)
                        scores(s, g, u, 0)
                        scores(s, g, u, 1)
                        values(s, g, u, 0)
                    if g == 0 and s.before:
                        bank = item(wk)
                        pe.wait_ge(xw_in, 3 * 16)
                        pe.wait_ge(x2_out, 16)
                        for i in range(2):
                            ins = nc.tensor.transpose(bank[:, i * P:(i + 1) * P], XW[:, i, :], ident[:])
                        ins.then_inc(wk_ready, 1)
                        bank = item(wk)
                        pe.wait_ge(ctx_in, s.b * 16)
                        for t in range(NT):
                            ins = nc.tensor.transpose(bank[:, t * P:(t + 1) * P], CX[:, t, :], ident[:])
                        ins.then_inc(wk_ready, 1)
                        ctx_ready = wk.now()
                        pe.wait_ge(y_done, s.b * GROUPS)
                        for t in range(NT):
                            bank, c = item(wk), slice(t * P, (t + 1) * P)
                            three(bank[:], [((Y[0][:, k, c], Y[1][:, k, c]), (Wo[0][:, k, :], Wo[1][:, k, :]))
                                            for k in range(GROUPS)]).then_inc(wk_ready, 1)
                        for i in range(2):
                            bank = item(wk)
                            if i == 0:
                                pe.wait_ge(wk_free, ctx_ready)
                            nc.tensor.matmul(bank[:], XWT[:, i, :], ctxT[:], start=True, stop=True).then_inc(wk_ready, 1)
                        cross_ready = wk.now()
                    if s.main:
                        scores(s, g, u, 2)
                        values(s, g, u, 1)
                    if s.before:
                        bank = item(wk)
                        if g == 0:
                            pe.wait_ge(wk_free, cross_ready)
                        nc.tensor.matmul(bank[:], qpT[:, g * P:(g + 1) * P], kpT[:], start=True, stop=True).then_inc(wk_ready, 1)
                    if s.main:
                        scores(s, g, u, 3)
                        values(s, g, u, 2)
                        values(s, g, u, 3)

            over_batches(pe, body)

        @block.scalar
        def _(act):
            for k in range(KT):
                act.wait_ge(w_in[k % 2], 32 * (k // 2 + 1))
                w = W_STAGE[k % 2]
                nc.scalar.activation(Wqk[0][:, k, :], w[:, 0:2 * D], ACT.Copy).then_inc(w_hi, 1)
                nc.scalar.activation(Wv[0][:, k, :], w[:, 2 * D:3 * D], ACT.Copy).then_inc(w_hi, 1)
                nc.scalar.activation(Wo[0][:, k, :], w[:, 3 * D:4 * D], ACT.Copy).then_inc(w_hi, 1)

            def hi_x(wk):
                for t in range(NT):
                    act.wait_ge(wk_ready, wk.up())
                    nc.scalar.activation(XT[0][:, :, t * P:(t + 1) * P], WK[(wk.n - 1) % 2][:].rearrange(
                        "p (k n) -> p k n", k=KT), ACT.Copy).then_inc(hi_ready, 1)

            def hi_qk(wk, s=None, g=0):
                for i, (dst, scale) in enumerate(((qT[0], ATT_SCALE), (kT[0], 1.0))):
                    act.wait_ge(wk_ready, wk.up())
                    if i == 0 and s:
                        act.wait_ge(stack_in[g % 2], nth(s, g) * STACK_SP * 16)
                        act.wait_ge(stack_in2[g % 2], nth(s, g) * STACK_POOL * 16)
                    nc.scalar.activation(dst[:], WK[(wk.n - 1) % 2][:], ACT.Copy, scale=scale).then_inc(hi_ready, 1)

            wk = Tick(0)
            hi_x(wk)
            hi_qk(wk)

            def exps(s, g, u, j):
                i = u * HPG + j
                for n, piece in enumerate(ST_PIECES):
                    m = j * len(ST_PIECES) + n
                    if n == 0 and not (s.first and g == 0 and j < 2):
                        act.wait_ge(o_ready, i - 1)
                    act.wait_ge(st_ready, u * N_ST + m + 1)
                    w = sum(S - kb * P for kb in piece)
                    at = P_AT[piece[0]]
                    nc.scalar.activation(PT[:, j % 2, at:at + w], ST[m % 2][:, 0:w], ACT.Exp).then_inc(p_ready, 1)

            def outputs(s, g, u, j):
                i, bank = u * HPG + j, O[j % 2]
                act.wait_ge(o_ready, i + 1)
                if j == 0 and not (s.first and g == 0):
                    act.wait_ge(y_done, u)
                r, odd = slice(j * HD, (j + 1) * HD), j % 2
                lower, upper = bank[0:HD, :], bank[HD:2 * HD, :]
                if s.first and g == 0 and j == 0:
                    act.wait_ge(mask_ready, B)
                nc.scalar.activation(Yf[r, :], upper if odd else lower, ACT.Copy)
                nc.scalar.activation(Sf[r, :], lower if odd else upper, ACT.Copy).then_inc(o_free, 1)

            def body(s):
                wk = Tick(s.wk_base)
                for g in range(GROUPS):
                    u = s.b * GROUPS + g
                    if g == 0 and s.main:
                        wk.up(N_V)
                    if s.turns(g):
                        hi_x(wk)
                    if s.projects(g):
                        hi_qk(wk, s, g)
                    if s.before:
                        wk.up(N_WO + N_CTX + 1 if g == 0 else 1)
                    if s.main:
                        exps(s, g, u, 0)
                        exps(s, g, u, 1)
                        for j in range(2, HPG):
                            outputs(s, g, u, j - 2)
                            exps(s, g, u, j)
                    if s.before:
                        act.wait_ge(nm_ready, (s.b - 1) * NT + g + 1)
                        nc.scalar.activation(SC[:], SC[:], ACT.Exp, bias=col[:, 1:2], accum_out=col[:, 2:3]).then_inc(ex_ready, 1)
                    if s.main:
                        outputs(s, g, u, HPG - 2)
                        outputs(s, g, u, HPG - 1)

            over_batches(act, body)

        @block.vector
        def _(dve):
            d = Tick(0)

            def pause():
                nc.vector.memset(idle[:, 1:2], 0.0)

            def statistics(b):
                dve.wait_ge(xl_in, (b + 1) * 16)
                for t in range(NT):
                    nc.vector.bn_stats(stats[:, t, :], XL[:, t, :]).then_inc(dv, 1)
                dve.wait_ge(dv, d.up(NT))
                pause()
                for t in range(NT):
                    nc.vector.bn_aggr(mv1[:, t, :], stats[:, t, :]).then_inc(dv, 1)
                dve.wait_ge(dv, d.up(NT))
                nc.vector.tensor_scalar(rs1[:], mv1[:, :, 1], LN_EPS, None, ALU.add).then_inc(stat1, 1)

            def normalise(b, t):
                nc.vector.tensor_scalar(XN[:, t % 2, :], XL[:, t, :], mv1[:, t, 0:1], rs1[:, t:t + 1],
                                        ALU.subtract, ALU.mult).then_inc(xn_ready, 1)

            def first_tiles(b):
                dve.wait_ge(rs1_ready, b + 1)
                normalise(b, 0)
                normalise(b, 1)

            def lo_x(wk, hi, b, tiles):
                for t in tiles:
                    dve.wait_ge(wk_ready, wk.up())
                    dve.wait_ge(hi_ready, hi.up())
                    c = slice(t * P, (t + 1) * P)
                    nc.vector.tensor_tensor(XT[1][:, :, c], WK[(wk.n - 1) % 2][:].rearrange("p (k n) -> p k n", k=KT),
                                            XT[0][:, :, c].bitcast(F32), ALU.subtract).then_inc(wk_free, 1)
                    if t + 2 < NT:
                        normalise(b, t + 2)

            def lo_qk(wk, hi):
                for i, (pr, scale) in enumerate(((qT, ATT_SCALE), (kT, 1.0))):
                    dve.wait_ge(wk_ready, wk.up())
                    dve.wait_ge(hi_ready, hi.up())
                    nc.vector.scalar_tensor_tensor(out=pr[1][:], in0=WK[(wk.n - 1) % 2][:], scalar=scale,
                                                   in1=pr[0][:].bitcast(F32), op0=ALU.mult,
                                                   op1=ALU.subtract).then_inc(wk_free, 1)

            statistics(0)
            for k in range(KT):
                dve.wait_ge(w_hi, 3 * (k + 1))
                w = W_STAGE[k % 2]
                for n, (pr, c) in enumerate(((Wqk, slice(0, 2 * D)), (Wv, slice(2 * D, 3 * D)), (Wo, slice(3 * D, 4 * D)))):
                    ins = nc.vector.tensor_tensor(pr[1][:, k, :], w[:, c], pr[0][:, k, :].bitcast(F32), ALU.subtract)
                    if n:
                        ins.then_inc(w_lo, 1)
            wk, hi = Tick(0), Tick(0)
            first_tiles(0)
            lo_x(wk, hi, 0, range(NT))
            lo_qk(wk, hi)
            dve.wait_ge(am_in, 16)
            nc.vector.tensor_scalar(AM[:], AM_U8, MASK, None, ALU.mult).then_inc(sc_ready, 1)
            dve.wait_ge(km_in, 16 * B)
            for b in range(B):
                nc.vector.tensor_scalar(KM[:, b, :], KM_U8[:, b, :], MASK, None, ALU.mult).then_inc(mask_ready, 1)

            def maxima(s, g, u, pieces):
                for i in pieces:
                    q, j0, nj = SM_PIECES[i]
                    dve.wait_ge(sm_ready, u * N_SM + i + 1)
                    w = (q + 1) * P
                    c = slice(j0 * NT + q, (j0 + nj - 1) * NT + q + 1, NT)
                    nc.vector.tensor_reduce(NM[:, c], SM[i % 2][:, 0:nj * w].rearrange("p (j n) -> p j n", j=nj), AX_X,
                                            ALU.max, negate=True).then_inc(sm_free, 1)

            def split_maxima(s, g, u):
                dve.wait_ge(sm_ready, (u + 1) * N_SM)
                if g:
                    dve.wait_ge(mrow_in[(g - 1) % 2], nth(s, g - 1) * 2 * 16)
                elif not s.first:
                    dve.wait_ge(mrow_in[(g - 1) % 2], s.b * (GROUPS // 2) * 2 * 16)
                bank = SM[(N_SM - 1) % 2]
                nc.vector.tensor_copy(MT[0][:], bank[0:HPG * NT, 0:P]).then_inc(dv, 1)
                dve.wait_ge(dv, d.up())
                nc.vector.tensor_tensor(MT[1][:], bank[0:HPG * NT, 0:P], MT[0][:].bitcast(F32),
                                        ALU.subtract).then_inc(sm_free, 1)

            def finish_unit(u, g):
                dve.wait_ge(o_free, (u + 1) * HPG)
                nc.vector.reciprocal(Sf[:], Sf[:]).then_inc(dv, 1)
                dve.wait_ge(dv, d.up())
                nc.vector.tensor_tensor(Yf[:], Yf[:], Sf[:], ALU.mult).then_inc(dv, 1)
                dve.wait_ge(dv, d.up())
                nc.vector.tensor_copy(Y[0][:, g, :], Yf[:]).then_inc(dv, 1)
                dve.wait_ge(dv, d.up())
                nc.vector.tensor_tensor(Y[1][:, g, :], Yf[:], Y[0][:, g, :].bitcast(F32), ALU.subtract).then_inc(y_done, 1)

            def residual(wk, b):
                for t in range(NT):
                    dve.wait_ge(wk_ready, wk.up())
                    if t == 0:
                        dve.wait_ge(xr_in, (b + 1) * 16)
                    xt = XR[:, t, :]
                    nc.vector.tensor_tensor(xt, WK[(wk.n - 1) % 2][:], xt, ALU.add).then_inc(wk_free, 1)
                    dve.wait_ge(wk_free, wk.now())
                    nc.vector.bn_stats(stats[:, t, :], xt).then_inc(dv, 1)
                dve.wait_ge(dv, d.up(NT))
                pause()
                for t in range(NT):
                    nc.vector.bn_aggr(mv2[:, t, :], stats[:, t, :]).then_inc(dv, 1)
                dve.wait_ge(dv, d.up(NT))
                nc.vector.tensor_scalar(rs2[:], mv2[:, :, 1], LN_EPS, None, ALU.add).then_inc(stat2, 1)

            def turn_context(wk):
                dve.wait_ge(wk_ready, wk.up())
                nc.vector.tensor_copy(XWT[:], WK[(wk.n - 1) % 2][:, 0:2 * P].rearrange("p (a n) -> p a n", a=2)).then_inc(wk_free, 1)
                dve.wait_ge(wk_ready, wk.up())
                nc.vector.tensor_copy(ctxT[:], WK[(wk.n - 1) % 2][:]).then_inc(wk_free, 1)

            def context(wk):
                for i, dst in enumerate((qpT, kpT)):
                    dve.wait_ge(wk_ready, wk.up())
                    nc.vector.tensor_scalar(dst[:], WK[(wk.n - 1) % 2][:], bqk[:, i:i + 1], None, ALU.add).then_inc(wk_free, 1)

            def cross(wk, b, g):
                if g == 0:
                    dve.wait_ge(rs2_ready, b + 1)
                tile = XR[:, g, :]
                nc.vector.tensor_scalar(Z[:], tile, mv2[:, g, 0:1], rs2[:, g:g + 1], ALU.subtract, ALU.mult).then_inc(dv, 1)
                dve.wait_ge(dv, d.up())
                dve.wait_ge(wk_ready, wk.up())
                nc.vector.scalar_tensor_tensor(out=SC[:], in0=WK[(wk.n - 1) % 2][:], scalar=X_SCALE, in1=Z[:], op0=ALU.mult,
                                               op1=ALU.mult).then_inc(wk_free, 1)
                dve.wait_ge(wk_free, wk.now())
                dve.wait_ge(ak_ready, b * NT + g + 1)
                pause()
                nc.vector.tensor_tensor_reduce(out=SC[:], in0=SC[:], in1=AK[:], scale=1.0, scalar=LEAST, op0=ALU.add,
                                               op1=ALU.max, accum_out=col[:, 0:1]).then_inc(sc_ready, 1)
                dve.wait_ge(sc_ready, b * NT + g + 2)
                nc.vector.tensor_scalar(col[:, 1:2], col[:, 0:1], -1.0, None, ALU.mult).then_inc(nm_ready, 1)
                dve.wait_ge(ex_ready, b * NT + g + 1)
                nc.vector.reciprocal(col[:, 3:4], col[:, 2:3]).then_inc(dv, 1)
                dve.wait_ge(dv, d.up())
                nc.vector.scalar_tensor_tensor(out=tile, in0=SC[:], scalar=col[:, 3:4], in1=tile, op0=ALU.mult,
                                               op1=ALU.add).then_inc(x2_ready, 1)
                dve.wait_ge(x2_ready, b * NT + g + 1)
                nc.vector.bn_stats(stats[:, g, :], tile).then_inc(dv, 1)
                dve.wait_ge(dv, d.up())
                pause()
                nc.vector.bn_aggr(mv3[:, g, :], stats[:, g, :]).then_inc(mv_ready, 1)
                dve.wait_ge(mv_ready, b * NT + g + 1)
                pause()

            marks = []

            def body(s):
                nonlocal d
                if isinstance(s.b, int):
                    d = Tick(0 if s.first and not marks else marks[-1])
                    if s.first:
                        d = Tick(start)
                else:
                    d = Tick(marks[-1] + (s.b - 1) * DV_PER)
                wk = Tick(s.wk_base)
                hi = Tick(HI_PER * s.b + WK_START)
                for g in range(GROUPS):
                    u = s.b * GROUPS + g
                    if s.turns(g):
                        first_tiles(s.b + 1)
                    for n in range(len(SM_GROUPS) if s.main else 0):
                        maxima(s, g, u, SM_GROUPS[n])
                        if g == 0:
                            dve.wait_ge(wk_ready, wk.up())
                            if s.first and n == 0:
                                dve.wait_ge(ones_ready, 1)
                            nc.vector.tensor_copy(V[:, n, :, :].rearrange("p m (c d) -> p m c d", c=3)[:, :, 0:3:2, :],
                                                  WK[(wk.n - 1) % 2][:].rearrange("p (m c d) -> p m c d", c=2, d=HD)
                                                  ).then_inc(wk_free, 1)
                        elif s.turns(g):
                            lo_x(wk, hi, s.b + 1, (n,))
                    if s.main:
                        split_maxima(s, g, u)
                    if s.projects(g):
                        lo_qk(wk, hi)
                    if not (s.first and g == 0) and not (s.tail and g):
                        finish_unit(u - 1, (g - 1) % GROUPS)
                    if g == 0 and s.before:
                        turn_context(wk)
                        residual(wk, s.b - 1)
                        context(wk)
                    if s.before:
                        cross(wk, s.b - 1, g)
                    if g == 1 and s.main and not s.last:
                        statistics(s.b + 1)
                if not isinstance(s.b, int):
                    assert d.n == DV_PER, d.n
                    marks.append(marks[-1] + (B - 2) * DV_PER)
                else:
                    marks.append(d.base + d.n)

            DV_PER = GROUPS * 3 + 2 * NT + 2 * NT + GROUPS + 3 * GROUPS
            start = d.base + d.n
            over_batches(dve, body)


def routing_constants():
    expert = np.arange(E, dtype=np.float32)
    full = np.arange(TILES, dtype=np.float32) * P
    before = (expert[None, :] < expert[:, None]).astype(np.float32)
    tile = np.arange(SLOT_TILES, dtype=np.float32)
    row = np.concatenate([expert, full, before.ravel(), tile])
    return np.ascontiguousarray(np.broadcast_to(row, (P, row.size)))


def router_and_shared(nc, io, x2_dram, mv_dram, slots_dram, HR, G, SL, EID, load_experts):
    with ExitStack() as st:
        sb = lambda name, shape, dt=F32: st.enter_context(nc.sbuf_tensor(name, shape, dt))
        bank = lambda name: st.enter_context(nc.psum_tensor(name, [P, 512], F32))
        sem = lambda name: st.enter_context(nc.semaphore(name))
        pair = lambda name, shape: [sb(f"{name}_{p}", shape, F32R) for p in ("hi", "lo")]

        WS, WSD, RW = pair("WS", [P, KT, 2 * FF]), pair("WSD", [P, FT, D]), pair("RW", [P, KT, E])
        HT = pair("HT", [P, KT, S])
        AT = pair("AT", [P, FT, S])
        XB = sb("XB", [P, NT, D])
        SG = sb("SG", [P, FT, S])
        rms = sb("rms_b", [P, D])
        RWf = sb("RWf", [P, KT, E])
        L = sb("L", [P, TILES, E])
        M8, I8, I8f = sb("M8", [P, TILES, E]), sb("I8", [P, TILES, E], mybir.dt.uint32), sb("I8f", [P, TILES, E])
        OH = [sb(f"OH{k}", [P, TILES, E]) for k in range(TOP)]
        OHb = sb("OHb", [P, TILES, E], BF16)
        RK, TMP = sb("RK", [P, TILES, E]), sb("TMP", [P, TILES, E])
        cnt, ntl, base, gt = sb("cnt", [P, E]), sb("ntl", [P, E]), sb("base", [P, E]), sb("gt", [P, E, TILES])
        cst = sb("cst_sb", [P, E + TILES + E * E + SLOT_TILES])
        c_expert, c_full = cst[:, 0:E], cst[:, E:E + TILES]
        c_before = cst[:, E + TILES:E + TILES + E * E].rearrange("p (e f) -> p e f", e=E)
        c_tile = cst[:, E + TILES + E * E:]
        le = sb("le", [P, SLOT_TILES, E - 1])
        eidf = sb("eidf", [P, SLOT_TILES])
        slf = sb("slf", [P, TILES])
        ident, lower, ones = sb("ident2", [P, P]), sb("lower", [P, P], BF16), sb("ones2", [P, P], BF16)
        mv = sb("mv3", [P, TILES, 2])
        rs, rt = sb("rs3", [P, TILES]), sb("rt3", [P, TILES])
        mhalf, lneps, rmseps = sb("mhalf3", [P, TILES]), sb("lneps", [P, TILES]), sb("rmseps", [P, TILES])

        WK = [bank(f"WKb{i}") for i in range(2)]
        GU = [bank(f"GUb{i}") for i in range(2 * FT)]
        LG = bank("LG")
        RB = bank("RB")

        x_in = [sem(f"f_x_in{b}") for b in range(B)]
        xb_in = [sem(f"f_xb_in{t}") for t in range(NT)]
        w_in, w_hi, w_lo = [sem(f"f_w_in{i}") for i in range(2)], sem("f_w_hi"), sem("f_w_lo")
        c_in, rw_in, rms_in, mv_in = sem("f_c_in"), sem("f_rw_in"), sem("f_rms_in"), sem("f_mv_in")
        pc, pl = sem("f_pc"), sem("f_pl")
        rs_ready = sem("f_rs")
        h0_ready, h_ready = sem("f_h0"), sem("f_h")
        wk_ready, wk_free, hi_ready = sem("f_wk"), sem("f_wkf"), sem("f_hi")
        lg_ready = sem("f_lg")
        e2_in, e2_out = sem("f_e2i"), sem("f_e2o")
        oh_ready, rk_ready, sl_ready = sem("f_oh"), sem("f_rk"), sem("f_sl")
        scat = [sem(f"f_scat{b}") for b in range(B)]
        gu_ready, sg_ready, at0_ready, at_hi, at_ready = [sem(f"f_{n}") for n in ("gu", "sg", "at0", "at_hi", "at")]
        dv = sem("f_dv")
        block = st.enter_context(nc.Block())

        SPIECES = KT + FT
        ORDER = (B - 1,) + tuple(range(B - 1))

        def turned_at(n):
            return TILES + (n - 1) * 2 * NT

        def down_at(n):
            return TILES + n * 2 * NT + (NT if n < B - 1 else 0)

        @block.sync
        def _(sp):
            x2 = x2_dram.rearrange("b (t p) d -> b p t d", p=P)
            sp.dma_start(mv[:].rearrange("p (b t) c -> p b (t c)", b=B), mv_dram.rearrange("b p n -> p b n")).then_inc(mv_in, 16)
            sp.dma_start(HR[:, 0:NT, :], x2[0]).then_inc(x_in[0], 16)
            sp.dma_start(rms[:], io["rms"].rearrange("(a d) -> a d", a=1).broadcast_to([P, D])).then_inc(rms_in, 16)
            sp.dma_start(RWf[:], io["router"].rearrange("(k p) e -> p k e", p=P)).then_inc(rw_in, 16)
            for b in range(1, B):
                sp.dma_start(HR[:, b * NT:(b + 1) * NT, :], x2[b]).then_inc(x_in[b], 16)
            sp.dma_start(cst[:], io["cst"]).then_inc(c_in, 16)
            for k in range(SPIECES):
                if k >= 2:
                    sp.wait_ge(w_hi, k)
                    sp.wait_ge(w_lo, k)
                if k < KT:
                    r = slice(k * P, (k + 1) * P)
                    sp.dma_start(SG[:, k % 2, 0:FF], io["swg"][r, :]).then_inc(w_in[k % 2], 16)
                    sp.dma_start(SG[:, k % 2, FF:2 * FF], io["swu"][r, :]).then_inc(w_in[k % 2], 16)
                else:
                    r = slice((k - KT) * P, (k - KT + 1) * P)
                    sp.dma_start(SG[:, k % 2, :], io["swd"][r, :]).then_inc(w_in[k % 2], 16)
            for n, b in enumerate(ORDER):
                for t in range(NT):
                    if n:
                        sp.wait_ge(wk_free, down_at(n - 1) + t + 1)
                    sp.dma_start(XB[:, t, :], x2[b][:, t, :]).then_inc(xb_in[t], 16)
                if n == 0:
                    load_experts(sp)

        @block.gpsimd
        def _(pool):
            nc.gpsimd.memset(mhalf[:], -0.5).then_inc(pc, 1)
            nc.gpsimd.memset(lneps[:], LN_EPS).then_inc(pc, 1)
            nc.gpsimd.memset(rmseps[:], RMS_EPS).then_inc(pc, 1)
            nc.gpsimd.memset(ident[:], 0.0).then_inc(pc, 1)
            nc.gpsimd.memset(lower[:], 1.0).then_inc(pc, 1)
            nc.gpsimd.memset(ones[:], 1.0).then_inc(pc, 1)
            pool.wait_ge(pc, 6)
            nc.gpsimd.affine_select(out=ident[:], in_=ident[:], compare_op=ALU.not_equal, fill=1.0, base=0,
                                    pattern=[[-1, P]], channel_multiplier=1).then_inc(pc, 1)
            nc.gpsimd.affine_select(out=lower[:], in_=lower[:], compare_op=ALU.is_gt, fill=0.0, base=0,
                                    pattern=[[1, P]], channel_multiplier=-1).then_inc(pc, 1)

            steps = ((rt, mv[:, :, 1], lneps, ALU.add), (rs, rt[:], mhalf, ALU.pow), (rt, rs[:], rs, ALU.mult),
                     (rt, rt[:], mv[:, :, 1], ALU.mult), (rt, rt[:], rmseps, ALU.add), (rt, rt[:], mhalf, ALU.pow),
                     (rs, rs[:], rt, ALU.mult))
            pool.wait_ge(mv_in, 16)
            for n, (dst, x, y, op) in enumerate(steps):
                ins = nc.gpsimd.tensor_tensor(dst[:], x, y if n == 3 else y[:], op)
                if n < len(steps) - 1:
                    ins.then_inc(pl, 1)
                    pool.wait_ge(pl, n + 1)
                else:
                    ins.then_inc(rs_ready, 1)
            pool.wait_ge(sl_ready, TOP)
            for b in ORDER:
                for t in range(b * NT, (b + 1) * NT):
                    for k in range(TOP):
                        pool.indirect_dma_start(out=slots_dram, out_offset=bass.IndirectOffsetOnAxis(ap=SL[k][:, t:t + 1], axis=0),
                                                in_=HR[:, t, :], in_offset=None).then_inc(scat[b], 16)
            for b in range(B):
                pool.wait_ge(scat[b], NT * TOP * 16)

        @block.tensor
        def _(pe):
            def three(out, pairs):
                terms = [t for (ah, al), (bh, bl) in pairs for t in ((ah, bh), (ah, bl), (al, bh))]
                for i, (a, b) in enumerate(terms):
                    ins = nc.tensor.matmul(out, a, b, start=(i == 0), stop=(i == len(terms) - 1))
                return ins

            pe.wait_ge(pc, 8)
            pe.wait_ge(w_lo, 1)

            def turn(i, at):
                pe.wait_ge(wk_free, at - 1)
                for k in range(KT):
                    ins = nc.tensor.transpose(WK[at % 2][:, k * P:(k + 1) * P], HR[:, i, k * P:(k + 1) * P], ident[:])
                ins.then_inc(wk_ready, 1)

            for i in range(TILES + 1):
                if i < TILES:
                    pe.wait_ge(h_ready, i + 1)
                    if i >= 2:
                        turn(i, i)
                    else:
                        for k in range(KT):
                            ins = nc.tensor.transpose(WK[i][:, k * P:(k + 1) * P], HR[:, i, k * P:(k + 1) * P], ident[:])
                        ins.then_inc(wk_ready, 1)
                if i:
                    pe.wait_ge(wk_free, i)
                    c = slice((i - 1) % NT * P, ((i - 1) % NT + 1) * P)
                    three(LG[:, (i - 1) * E:i * E], [((HT[0][:, k, c], HT[1][:, k, c]), (RW[0][:, k, :], RW[1][:, k, :]))
                                                     for k in range(KT)]).then_inc(lg_ready, 1)

            def ranks():
                pe.wait_ge(oh_ready, 1)
                nc.tensor.matmul(RB[:, 0:TILES * E], lower[:], OHb[:].rearrange("p t e -> p (t e)"), start=True, stop=False,
                                 skip_group_check=True)
                for t in range(TILES - 1):
                    n = TILES - 1 - t
                    nc.tensor.matmul(RB[:, (t + 1) * E:TILES * E].rearrange("p (t e) -> p t e", e=E), ones[:],
                                     OHb[:, t:t + 1, :].broadcast_to([P, n, E]), start=False, stop=(n == 1),
                                     skip_group_check=True)
                for t in range(TILES):
                    ins = nc.tensor.matmul(RB[:, TILES * E:(TILES + 1) * E], ones[:], OHb[:, t, :], start=(t == 0),
                                           stop=(t == TILES - 1), skip_group_check=True)
                ins.then_inc(rk_ready, 1)

            pe.wait_ge(w_lo, SPIECES + 1)
            for n, b in enumerate(ORDER):
                if n:
                    pe.wait_ge(wk_free, turned_at(n) + NT)
                for f in range(FT):
                    for i, c0 in enumerate((0, FF)):
                        if n:
                            pe.wait_ge(at0_ready, (n - 1) * FT + f + 1)
                        c = slice(c0 + f * P, c0 + (f + 1) * P)
                        three(GU[2 * f + i][:], [((WS[0][:, k, c], WS[1][:, k, c]), (HT[0][:, k, :], HT[1][:, k, :]))
                                                 for k in range(KT)]).then_inc(gu_ready, 1)
                if n == 0:
                    ranks()
                if n < B - 1:
                    for t in range(NT):
                        turn(ORDER[n + 1] * NT + t, turned_at(n + 1) + t)
                at = down_at(n)
                for t in range(NT):
                    pe.wait_ge(wk_free, at + t - 1)
                    if t == 0:
                        pe.wait_ge(at_ready, FT * (n + 1))
                    c = slice(t * P, (t + 1) * P)
                    three(WK[t % 2][:], [((AT[0][:, f, c], AT[1][:, f, c]), (WSD[0][:, f, :], WSD[1][:, f, :]))
                                         for f in range(FT)]).then_inc(wk_ready, 1)

        @block.scalar
        def _(act):
            act.wait_ge(rw_in, 16)
            nc.scalar.activation(RW[0][:], RWf[:], ACT.Copy).then_inc(w_hi, 1)

            def hi_w(k):
                act.wait_ge(w_in[k % 2], 32 * (k // 2 + 1) if k < KT else 32 * (KT // 2) + 16)
                dst = WS[0][:, k, :] if k < KT else WSD[0][:, k - KT, :]
                nc.scalar.activation(dst, SG[:, k % 2, :], ACT.Copy).then_inc(w_hi, 1)

            def hi_h(t, at):
                act.wait_ge(wk_ready, at + 1)
                nc.scalar.activation(HT[0][:, :, t * P:(t + 1) * P], WK[at % 2][:].rearrange("p (k n) -> p k n", k=KT),
                                     ACT.Copy).then_inc(hi_ready, 1)

            def scaled(i):
                act.wait_ge(h0_ready, i + 1)
                nc.scalar.activation(HR[:, i, :], HR[:, i, :], ACT.Copy, scale=rs[:, i:i + 1]).then_inc(h_ready, 1)

            act.wait_ge(rs_ready, 1)
            scaled(0)
            scaled(1)
            for i in range(TILES):
                if i >= NT:
                    act.wait_ge(lg_ready, i - NT + 1)
                hi_h(i % NT, i)
                if i + 2 < TILES:
                    scaled(i + 2)
                if i % 2 and i // 2 < SPIECES:
                    hi_w(i // 2)
            act.wait_ge(e2_in, 1)
            nc.scalar.activation(G[1][:], G[1][:], ACT.Exp).then_inc(e2_out, 1)

            for n in range(B):
                for f in range(FT):
                    act.wait_ge(gu_ready, (n * FT + f) * 2 + 1)
                    if n:
                        act.wait_ge(at_ready, (n - 1) * FT + f + 1)
                    nc.scalar.activation(SG[:, f, :], GU[2 * f][:], ACT.Silu).then_inc(sg_ready, 1)
                if n < B - 1:
                    act.wait_ge(gu_ready, (n + 1) * 2 * FT)
                    for t in range(NT):
                        hi_h(t, turned_at(n + 1) + t)
                for f in range(FT):
                    act.wait_ge(at0_ready, n * FT + f + 1)
                    if n and f == 0:
                        act.wait_ge(wk_ready, down_at(n - 1) + NT)
                    nc.scalar.activation(AT[0][:, f, :], SG[:, f, :], ACT.Copy).then_inc(at_hi, 1)

        @block.vector
        def _(dve):
            d = Tick(0)

            def lo_h(t, at, hi):
                dve.wait_ge(wk_ready, at + 1)
                dve.wait_ge(hi_ready, hi + 1)
                c = slice(t * P, (t + 1) * P)
                nc.vector.tensor_tensor(HT[1][:, :, c], WK[at % 2][:].rearrange("p (k n) -> p k n", k=KT),
                                        HT[0][:, :, c].bitcast(F32), ALU.subtract).then_inc(wk_free, 1)

            def lo_w(k):
                dve.wait_ge(w_hi, k + 2)
                pr, n = (WS, k) if k < KT else (WSD, k - KT)
                nc.vector.tensor_tensor(pr[1][:, n, :], SG[:, k % 2, :], pr[0][:, n, :].bitcast(F32), ALU.subtract).then_inc(w_lo, 1)

            def centred(i):
                if i % NT == 0:
                    dve.wait_ge(x_in[i // NT], 16)
                nc.vector.scalar_tensor_tensor(out=HR[:, i, :], in0=HR[:, i, :], scalar=mv[:, i, 0:1], in1=rms[:],
                                               op0=ALU.subtract, op1=ALU.mult).then_inc(h0_ready, 1)

            dve.wait_ge(mv_in, 16)
            dve.wait_ge(rms_in, 16)
            centred(0)
            dve.wait_ge(w_hi, 1)
            nc.vector.tensor_tensor(RW[1][:], RWf[:], RW[0][:].bitcast(F32), ALU.subtract).then_inc(w_lo, 1)
            for i in range(1, NT):
                centred(i)
            for i in range(TILES):
                lo_h(i % NT, i, i)
                if i + NT < TILES:
                    centred(i + NT)
                if i % 2 and i // 2 < SPIECES:
                    lo_w(i // 2)
            dve.wait_ge(lg_ready, TILES)
            nc.vector.tensor_copy(L[:], LG[:, 0:TILES * E].rearrange("p (t e) -> p t e", e=E)).then_inc(dv, 1)
            dve.wait_ge(dv, d.up())
            for t in range(TILES):
                nc.vector.max(M8[:, t, :], L[:, t, :]).then_inc(dv, 1)
            dve.wait_ge(dv, d.up(TILES))
            for t in range(TILES):
                nc.vector.max_index(I8[:, t, :], M8[:, t, :], L[:, t, :]).then_inc(dv, 1)
            nc.vector.tensor_tensor(G[1][:], M8[:, :, 1], M8[:, :, 0], ALU.subtract).then_inc(e2_in, 1)
            dve.wait_ge(dv, d.up(TILES))
            nc.vector.tensor_copy(I8f[:], I8[:]).then_inc(dv, 1)
            dve.wait_ge(dv, d.up())
            dve.wait_ge(c_in, 16)
            experts = c_expert.unsqueeze(1).broadcast_to([P, TILES, E])
            for k in range(TOP):
                nc.vector.tensor_tensor(OH[k][:], I8f[:, :, k:k + 1].broadcast_to([P, TILES, E]), experts, ALU.is_equal
                                        ).then_inc(dv, 1)
            dve.wait_ge(dv, d.up(TOP))
            nc.vector.tensor_tensor(OHb[:], OH[0][:], OH[1][:], ALU.add).then_inc(oh_ready, 1)
            dve.wait_ge(e2_out, 1)
            nc.vector.tensor_scalar(G[0][:], G[1][:], 1.0, None, ALU.add).then_inc(dv, 1)
            dve.wait_ge(dv, d.up())
            nc.vector.reciprocal(G[0][:], G[0][:]).then_inc(dv, 1)
            dve.wait_ge(dv, d.up())
            nc.vector.tensor_tensor(G[1][:], G[1][:], G[0][:], ALU.mult).then_inc(dv, 1)
            dve.wait_ge(dv, d.up())
            dve.wait_ge(rk_ready, 1)
            nc.vector.tensor_copy(cnt[:], RB[:, TILES * E:(TILES + 1) * E]).then_inc(dv, 1)
            dve.wait_ge(dv, d.up())
            nc.vector.tensor_tensor(gt[:], cnt[:].unsqueeze(2).broadcast_to([P, E, TILES]),
                                    c_full.unsqueeze(1).broadcast_to([P, E, TILES]), ALU.is_gt).then_inc(dv, 1)
            dve.wait_ge(dv, d.up())
            nc.vector.tensor_reduce(ntl[:], gt[:], AX_X, ALU.add).then_inc(dv, 1)
            dve.wait_ge(dv, d.up())
            nc.vector.tensor_tensor(gt[:, :, 0:E], ntl[:].unsqueeze(1).broadcast_to([P, E, E]), c_before, ALU.mult).then_inc(dv, 1)
            dve.wait_ge(dv, d.up())
            nc.vector.tensor_reduce(base[:], gt[:, :, 0:E], AX_X, ALU.add).then_inc(dv, 1)
            dve.wait_ge(dv, d.up())
            nc.vector.tensor_scalar(cnt[:], base[:], float(P), None, ALU.mult).then_inc(dv, 1)
            dve.wait_ge(dv, d.up())
            nc.vector.tensor_tensor(RK[:], RB[:, 0:TILES * E].rearrange("p (t e) -> p t e", e=E),
                                    cnt[:].unsqueeze(1).broadcast_to([P, TILES, E]), ALU.add).then_inc(dv, 1)
            dve.wait_ge(dv, d.up())
            for k in range(TOP):
                nc.vector.tensor_tensor(TMP[:], RK[:], OH[k][:], ALU.mult).then_inc(dv, 1)
                dve.wait_ge(dv, d.up())
                nc.vector.tensor_reduce(slf[:], TMP[:], AX_X, ALU.add).then_inc(dv, 1)
                dve.wait_ge(dv, d.up())
                nc.vector.tensor_copy(SL[k][:], slf[:]).then_inc(sl_ready, 1)
                dve.wait_ge(sl_ready, k + 1)
            nc.vector.tensor_tensor(base[:], base[:], ntl[:], ALU.add).then_inc(dv, 1)
            dve.wait_ge(dv, d.up())
            nc.vector.tensor_tensor(le[:], base[:, 0:E - 1].unsqueeze(1).broadcast_to([P, SLOT_TILES, E - 1]),
                                    c_tile.unsqueeze(2).broadcast_to([P, SLOT_TILES, E - 1]), ALU.is_le).then_inc(dv, 1)
            dve.wait_ge(dv, d.up())
            nc.vector.tensor_reduce(eidf[:], le[:], AX_X, ALU.add).then_inc(dv, 1)
            dve.wait_ge(dv, d.up())
            nc.vector.tensor_copy(EID[:], eidf[:]).then_inc(dv, 1)
            dve.wait_ge(dv, d.up())

            for n, b in enumerate(ORDER):
                for f in range(FT):
                    dve.wait_ge(gu_ready, (n * FT + f) * 2 + 2)
                    dve.wait_ge(sg_ready, n * FT + f + 1)
                    nc.vector.tensor_tensor(SG[:, f, :], GU[2 * f + 1][:], SG[:, f, :], ALU.mult).then_inc(at0_ready, 1)
                if n < B - 1:
                    for t in range(NT):
                        lo_h(t, turned_at(n + 1) + t, TILES + n * NT + t)
                for f in range(FT):
                    dve.wait_ge(at_hi, n * FT + f + 1)
                    nc.vector.tensor_tensor(AT[1][:, f, :], SG[:, f, :], AT[0][:, f, :].bitcast(F32), ALU.subtract).then_inc(at_ready, 1)
                at = down_at(n)
                dve.wait_ge(scat[b], NT * TOP * 16)
                for t in range(NT):
                    dve.wait_ge(wk_ready, at + t + 1)
                    dve.wait_ge(xb_in[t], 16 * (n + 1))
                    nc.vector.tensor_tensor(HR[:, b * NT + t, :], WK[t % 2][:], XB[:, t, :], ALU.add).then_inc(wk_free, 1)


def routed(nc, slots_dram, y_dram, WGU, WD, EID, w_in):
    with ExitStack() as st:
        sb = lambda name, shape, dt=F32: st.enter_context(nc.sbuf_tensor(name, shape, dt))
        banks = lambda name: [st.enter_context(nc.psum_tensor(f"{name}{i}", [P, 512], F32)) for i in range(2)]
        sem = lambda name: st.enter_context(nc.semaphore(name))
        XG, XT, YO = sb("XG", [P, 2, D]), sb("XTs", [P, 2, KT, P]), sb("YO", [P, 2, D])
        SGt, HH, HT = sb("SGt", [P, 2, FF]), sb("HH", [P, 2, FF]), sb("HTs", [P, 2, FT, P])
        ident = sb("ident3", [P, P])
        PX, PG, PH, PD = banks("PX"), banks("PG"), banks("PH"), banks("PD")
        pc = sem("r_pc")
        xg_in, y_out = [sem(f"r_xg{i}") for i in range(2)], [sem(f"r_yo{i}") for i in range(2)]
        px_ready, xt_ready, gu_ready, sg_ready, h_ready, ph_ready, ht_ready, pd_ready, yo_ready = [
            sem(f"r_{n}") for n in ("px", "xt", "gu", "sg", "h", "ph", "ht", "pd", "yo")]
        block = st.enter_context(nc.Block())
        N = SLOT_TILES
        FIRST, PAIRS = 3, (N - 5) // 2
        LAST = FIRST + 2 * PAIRS
        rows = lambda dram, i: dram[bass.ds(i * P, P), :]

        def over_tiles(eng, step):
            for i in range(FIRST):
                step(i, i % 2)
            with eng.Fori(0, PAIRS) as p:
                step(FIRST + 2 * p, 1)
                step(FIRST + 1 + 2 * p, 0)
            for i in range(LAST, N + 1):
                step(i, i % 2)

        @block.sync
        def _(sp):
            for i in range(2):
                sp.dma_start(XG[:, i, :], rows(slots_dram, i)).then_inc(xg_in[i], 16)

            def step(i, s):
                k = isinstance(i, int)
                if not (k and i < 1):
                    sp.wait_ge(yo_ready, i)
                    sp.dma_start(rows(y_dram, i - 1), YO[:, 1 - s, :]).then_inc(y_out[1 - s], 16)
                if not (k and i + 2 >= N):
                    sp.wait_ge(px_ready, i + 1)
                    sp.dma_start(XG[:, s, :], rows(slots_dram, i + 2)).then_inc(xg_in[s], 16)

            over_tiles(sp, step)
            for s in range(2):
                sp.wait_ge(y_out[s], 16 * ((N + 1 - s) // 2))

        @block.gpsimd
        def _(pool):
            nc.gpsimd.memset(ident[:], 0.0).then_inc(pc, 1)
            pool.wait_ge(pc, 1)
            nc.gpsimd.affine_select(out=ident[:], in_=ident[:], compare_op=ALU.not_equal, fill=1.0, base=0,
                                    pattern=[[-1, P]], channel_multiplier=1).then_inc(pc, 1)

        @block.tensor
        def _(pe):
            pe.wait_ge(pc, 2)
            pe.wait_ge(w_in, 16 * 3 * E)

            def turn(i, s, n_before):
                pe.wait_ge(xg_in[s], 16 * (n_before + 1))
                if not (isinstance(i, int) and i < 2):
                    pe.wait_ge(xt_ready, i - 1)
                for k in range(KT):
                    ins = nc.tensor.transpose(PX[s][:, k * P:(k + 1) * P], XG[:, s, k * P:(k + 1) * P], ident[:])
                ins.then_inc(px_ready, 1)

            turn(0, 0, 0)

            def step(i, s, e_before, of_parity):
                k0, e = isinstance(i, int), None
                if not (k0 and i >= N):
                    e = load(i)
                    pe.wait_ge(xt_ready, i + 1)
                    if not (k0 and i < 2):
                        pe.wait_ge(h_ready, i - 1)
                    for k in range(KT):
                        ins = nc.tensor.matmul(PG[s][:], XT[:, s, k, :], WGU[:, bass.ds(e, 1), k, :].rearrange("p o n -> p (o n)"),
                                               start=(k == 0), stop=(k == KT - 1))
                    ins.then_inc(gu_ready, 1)
                if not (k0 and i < 1):
                    pe.wait_ge(ht_ready, i)
                    if not (k0 and i < 3):
                        pe.wait_ge(yo_ready, i - 2)
                    for f in range(FT):
                        ins = nc.tensor.matmul(PD[1 - s][:], HT[:, 1 - s, f, :],
                                               WD[:, bass.ds(e_before, 1), f, :].rearrange("p o n -> p (o n)"),
                                               start=(f == 0), stop=(f == FT - 1))
                    ins.then_inc(pd_ready, 1)
                if not (k0 and i + 1 >= N):
                    turn(i + 1, 1 - s, of_parity)
                if not (k0 and i >= N):
                    pe.wait_ge(h_ready, i + 1)
                    for f in range(FT):
                        ins = nc.tensor.transpose(PH[s][:, f * P:(f + 1) * P], HH[:, s, f * P:(f + 1) * P], ident[:])
                    ins.then_inc(ph_ready, 1)
                return e

            def load(i):
                return nc.tensor.value_load(EID[0:1, i:i + 1] if isinstance(i, int) else EID[0:1, bass.ds(i, 1)],
                                            min_val=0, max_val=E - 1)

            e = None
            for i in range(FIRST):
                e = step(i, i % 2, e, i // 2 + (i % 2))
            with pe.Fori(0, PAIRS) as p:
                e = step(FIRST + 2 * p, 1, load(FIRST - 1 + 2 * p), p + 2)
                step(FIRST + 1 + 2 * p, 0, e, p + 2)
            e = load(LAST - 1)
            for i in range(LAST, N + 1):
                e = step(i, i % 2, e, i // 2 + (i % 2))

        @block.scalar
        def _(act):
            def turned(i, s):
                act.wait_ge(px_ready, i + 1)
                if not (isinstance(i, int) and i < 2):
                    act.wait_ge(gu_ready, i - 1)
                nc.scalar.activation(XT[:, s, :, :], PX[s][:].rearrange("p (k n) -> p k n", k=KT), ACT.Copy).then_inc(xt_ready, 1)

            turned(0, 0)

            def step(i, s):
                k = isinstance(i, int)
                if not (k and i >= N):
                    act.wait_ge(gu_ready, i + 1)
                    if not (k and i < 2):
                        act.wait_ge(h_ready, i - 1)
                    nc.scalar.activation(SGt[:, s, :], PG[s][:, 0:FF], ACT.Silu).then_inc(sg_ready, 1)
                if not (k and i + 1 >= N):
                    turned(i + 1, 1 - s)

            over_tiles(act, step)

        @block.vector
        def _(dve):
            def step(i, s, stored):
                k = isinstance(i, int)
                if not (k and i >= N):
                    dve.wait_ge(sg_ready, i + 1)
                    if not (k and i < 2):
                        dve.wait_ge(ph_ready, i - 1)
                    nc.vector.tensor_tensor(HH[:, s, :], PG[s][:, FF:2 * FF], SGt[:, s, :], ALU.mult).then_inc(h_ready, 1)
                if not (k and i < 1):
                    dve.wait_ge(pd_ready, i)
                    if not (k and i < 3):
                        dve.wait_ge(y_out[1 - s], 16 * stored)
                    nc.vector.tensor_copy(YO[:, 1 - s, :], PD[1 - s][:]).then_inc(yo_ready, 1)
                if not (k and i >= N):
                    dve.wait_ge(ph_ready, i + 1)
                    if not (k and i < 2):
                        dve.wait_ge(pd_ready, i - 1)
                    nc.vector.tensor_copy(HT[:, s, :, :], PH[s][:, 0:FF].rearrange("p (f n) -> p f n", f=FT)).then_inc(ht_ready, 1)

            for i in range(FIRST):
                step(i, i % 2, (i - 1) // 2)
            with dve.Fori(0, PAIRS) as p:
                step(FIRST + 2 * p, 1, p + 1)
                step(FIRST + 1 + 2 * p, 0, p + 1)
            for i in range(LAST, N + 1):
                step(i, i % 2, (i - 1) // 2)


def combine(nc, y_dram, out, ACC, G, SL):
    R = 4
    with ExitStack() as st:
        Y = [st.enter_context(nc.sbuf_tensor(f"Yc{k}", [P, R, D], F32)) for k in range(TOP)]
        y_in = [[st.enter_context(nc.semaphore(f"c_in{k}{r}")) for r in range(R)] for k in range(TOP)]
        a, done, o = [st.enter_context(nc.semaphore(f"c_{n}")) for n in ("a", "done", "o")]
        block = st.enter_context(nc.Block())

        @block.gpsimd
        def _(pool):
            for t in range(TILES):
                if t >= R:
                    pool.wait_ge(done, t - R + 1)
                for k in range(TOP):
                    pool.indirect_dma_start(out=Y[k][:, t % R, :], out_offset=None, in_=y_dram,
                                            in_offset=bass.IndirectOffsetOnAxis(ap=SL[k][:, t:t + 1], axis=0)
                                            ).then_inc(y_in[k][t % R], 16)

        @block.vector
        def _(dve):
            for t in range(TILES):
                for k in range(TOP):
                    dve.wait_ge(y_in[k][t % R], 16 * (t // R + 1))
                    if k:
                        dve.wait_ge(a, t + 1)
                    nc.vector.scalar_tensor_tensor(out=ACC[:, t, :], in0=Y[k][:, t % R, :], scalar=G[k][:, t:t + 1],
                                                   in1=ACC[:, t, :], op0=ALU.mult, op1=ALU.add).then_inc(done if k else a, 1)

        @block.sync
        def _(sp):
            ov = out.rearrange("b (t p) d -> (b t) p d", p=P)
            for t in range(TILES):
                sp.wait_ge(done, t + 1)
                sp.dma_start(ov[t], ACC[:, t, :]).then_inc(o, 16)
            sp.wait_ge(o, 16 * TILES)


def build(nc, io, out):
    x2 = nc.dram_tensor("x2_dram", [B, S, D], F32, kind="Internal").ap()
    slots = nc.dram_tensor("slots_dram", [SLOT_TILES * P, D], F32, kind="Internal").ap()
    y = nc.dram_tensor("y_dram", [SLOT_TILES * P, D], F32, kind="Internal").ap()
    mv = nc.dram_tensor("mv_dram", [B, P, NT * 2], F32, kind="Internal").ap()
    attention_part(nc, io, x2, mv, slots)
    with ExitStack() as st:
        sb = lambda name, shape, dt=F32: st.enter_context(nc.sbuf_tensor(name, shape, dt))
        HR = sb("HR", [P, TILES, D])
        G = [sb(f"G{k}", [P, TILES]) for k in range(TOP)]
        SL = [sb(f"SL{k}", [P, TILES], mybir.dt.int32) for k in range(TOP)]
        EID = sb("EID", [P, SLOT_TILES], mybir.dt.int32)
        WGU, WD = sb("WGU", [P, E, KT, 2 * FF]), sb("WDn", [P, E, FT, D])
        w_in = st.enter_context(nc.semaphore("exp_w_in"))

        def load_experts(sp):
            for e in range(E):
                sp.dma_start(WGU[:, e, :, 0:FF], io["wg"][e].rearrange("(k p) f -> p k f", p=P)).then_inc(w_in, 16)
                sp.dma_start(WGU[:, e, :, FF:2 * FF], io["wu"][e].rearrange("(k p) f -> p k f", p=P)).then_inc(w_in, 16)
                sp.dma_start(WD[:, e, :, :], io["wd"][e].rearrange("(f p) d -> p f d", p=P)).then_inc(w_in, 16)

        router_and_shared(nc, io, x2, mv, slots, HR, G, SL, EID, load_experts)
        routed(nc, slots, y, WGU, WD, EID, w_in)
        combine(nc, y, out, HR, G, SL)


NAMES = {"x": "x", "ctx_512": "ctx", "mask_SxS2_bk1": "am", "mask_BxS2_bf0": "km", "L0_attn_W_qkv": "wqkv",
         "L0_attn_W_o": "wo", "L0_xattn_Wq": "xwq", "L0_xattn_bq": "xbq", "L0_xattn_Wk": "xwk",
         "L0_xattn_bk": "xbk", "L0_ffn_rms_weight": "rms", "L0_ffn_router_w": "router", "L0_ffn_w_gate": "wg",
         "L0_ffn_w_up": "wu", "L0_ffn_w_down": "wd", "L0_ffn_sw_gate": "swg", "L0_ffn_sw_up": "swu",
         "L0_ffn_sw_down": "swd"}


def extra():
    return {"cst": routing_constants()}


def kernel(**inputs):
    import concourse.bacc as bacc
    from concourse.bass_utils import run_bass_kernel_spmd

    nc = bacc.Bacc("TRN2", target_bir_lowering=False, num_devices=1)
    alibi_q, alibi_k = alibi_rows()
    arrays = {NAMES[name]: np.ascontiguousarray(a) for name, a in inputs.items()}
    arrays.update(alq=alibi_q, alk=alibi_k, cst=routing_constants())
    io = {n: nc.dram_tensor(n, a.shape, mybir.dt.from_np(a.dtype), kind="ExternalInput").ap() for n, a in arrays.items()}
    out = nc.dram_tensor("out", (B, S, D), F32, kind="ExternalOutput").ap()
    build(nc, io, out)
    result = run_bass_kernel_spmd(nc, [arrays], core_ids=[0])
    return result.results[0]["out"]
```

```python
from contextlib import ExitStack

import numpy as np

import concourse.bass as bass
from concourse import mybir

F32 = mybir.dt.float32
F32R = mybir.dt.float32r
BF16 = mybir.dt.bfloat16
U8 = mybir.dt.uint8
ALU = mybir.AluOpType
ACT = mybir.ActivationFunctionType
AX_X = mybir.AxisListType.X

P = 128
B, S, D = 4, 512, 512
HEADS, HD = 16, 32
CTX = 128
NT = S // P
KT = D // P
GROUPS = 4
HPG = HEADS // GROUPS
E, FF = 8, 256
FT = FF // P
TILES = B * NT
TOP = 2
SLOT_TILES = (TOP * TILES * P + E * (P - 1)) // P
LN_EPS, RMS_EPS = 1e-5, 1e-6
ATT_SCALE = HD ** -0.5
X_SCALE = CTX ** -0.5
MASK = -1.5e38
LEAST = -1.0e37
MASKED = -1e30
ROW_ALIBI, ROW_MAX, ROW_END = 3 * HD, 3 * HD + 4, 3 * HD + 6
SM_PIECES = [(0, 0, 4), (1, 0, 2), (1, 2, 2)] + [(q, j, 1) for q in (2, 3) for j in range(HPG)]
N_SM = len(SM_PIECES) + 1
VALUES_FIRST = {1: (2, (0,)), 2: (2, (1,)), 3: (2, (2, 3)), 4: (3, (0,)), 5: (3, (1,)), 6: (3, (2, 3))}
VALUES_AFTER = {1: (2, (0,)), 3: (2, (1,)), 4: (2, (2, 3)), 6: (3, (0,)), 7: (3, (1,)), 8: (3, (2,)), 9: (3, (3,))}
VALUES_LATE = {1: (2, (0,)), 3: (2, (1,)), 5: (2, (2,)), 7: (2, (3,))}
V_AFTER = (7, 9)
ST_PIECES = ((0,), (1, 3), (2,))
DVE_SLICES = KT // 2
N_ST = len(ST_PIECES) * HPG
P_AT = {0: 0, 1: 512, 3: 896, 2: 1024}
N_V, N_WO, N_CTX, N_PROJ, N_XT = NT, NT, 4, 2, NT
ZERO_PARTS = GROUPS
WK_START = N_XT + 2 * N_PROJ
WK_BEFORE = N_WO + N_CTX + GROUPS
WK_PER = N_V + GROUPS * N_PROJ + N_XT + WK_BEFORE
HI_PER = GROUPS * N_PROJ + N_XT
STACK_SP, STACK_POOL = 4 * HPG, 2 * HPG


def alibi_rows():
    slope = (2.0 ** (-8.0 / np.arange(1, HEADS + 1, dtype=np.float32))).astype(np.float32)
    hi = (slope.view(np.uint32) & np.uint32(0xFFFFF000)).view(np.float32)
    lo = slope - hi
    pos = np.arange(S, dtype=np.float32) - S // 2
    q = np.zeros((ROW_MAX - ROW_ALIBI, HEADS, S), np.float32)
    k = np.zeros((ROW_END - ROW_ALIBI, HEADS, S), np.float32)
    q[0], q[1], q[2], q[3] = hi[:, None], lo[:, None], pos, pos
    k[0], k[1], k[2], k[3] = pos, pos, -hi[:, None], -lo[:, None]
    k[4:] = 1.0
    return q, k


def raw(ap):
    return ap.bitcast(F32)


class Tick:

    def __init__(self, base=0):
        self.base, self.n = base, 0

    def up(self, k=1):
        self.n += k
        return self.base + self.n

    def now(self):
        return self.base + self.n


def nth(s, g):
    return s.b * (GROUPS // 2) + g // 2 + 1


FIRST_PAUSES, PAUSES = 2 * GROUPS, 3 * GROUPS


def slot_open(s, g):
    return 2 + 2 * g if s.first else FIRST_PAUSES + (s.b - 1) * PAUSES + 3 * g + 2


class Step:

    def __init__(self, b, first=False, last=False, tail=False):
        self.b, self.first, self.last, self.tail = b, first, last, tail
        self.main = not tail
        self.before = not first
        self.v = self.main and not first
        self.wk_base = WK_START + b * WK_PER - (-N_V if first else WK_BEFORE) - (WK_START if tail else 0)

    def projects(self, g):
        return self.main and not (self.last and g >= GROUPS - 2)

    def stacks(self, g):
        return self.main and not (self.last and g == GROUPS - 1)

    def turns(self, g):
        return self.main and not self.last and g == 1


def over_batches(eng, body):
    body(Step(0, first=True))
    with eng.Fori(1, B - 1) as b:
        body(Step(b))
    body(Step(B - 1, last=True))
    body(Step(B, tail=True))


def attention_part(nc, io, x2_dram, mv_dram, slots_dram):
    with ExitStack() as st:
        sb = lambda name, shape, dt=F32: st.enter_context(nc.sbuf_tensor(name, shape, dt))
        banks = lambda name: [st.enter_context(nc.psum_tensor(f"{name}{i}", [P, 512], F32)) for i in range(2)]
        sem = lambda name: st.enter_context(nc.semaphore(name))
        pair = lambda name, shape: [sb(f"{name}_{p}", shape, F32R) for p in ("hi", "lo")]

        Wqk, Wv, Wo = pair("Wqk", [P, KT, 2 * D]), pair("Wv", [P, KT, D]), pair("Wo", [P, KT, D])
        XT = pair("XT", [P, KT, S])
        QS, KS = sb("QS", [P, 2, HPG, S], F32R), sb("KS", [P, 2, HPG, S], F32R)
        qT, kT = pair("qT", [P, S]), pair("kT", [P, S])
        V = sb("V", [P, NT, HEADS // 2, 3 * HD])
        PT = sb("PT", [P, 2, 1280])
        Yf, Sf = sb("Yf", [P, S]), sb("Sf", [P, S])
        Y = pair("Y", [P, GROUPS, S])
        NM = sb("NM", [P, HPG * NT])
        MT = pair("MT", [HPG * NT, P])
        XN = sb("XN", [P, 2, D])
        XL, XR = sb("XL", [P, NT, D]), sb("XR", [P, NT, D])
        Z, SC, AK = sb("Z", [P, D]), sb("SC", [P, D]), sb("AK", [P, D], BF16)
        CX = Z[:].rearrange("p (t c) -> p t c", t=NT)
        ctxT, qpT, kpT = sb("ctxT", [P, S]), sb("qpT", [P, S]), sb("kpT", [P, S])
        XW, XWT, bqk = sb("XW", [P, 2, P]), sb("XWT", [P, 2, P]), sb("bqk", [P, 2])
        AM, KM = sb("AM", [P, NT, S], BF16), sb("KM", [P, B, S], BF16)
        ident, identb = sb("ident", [P, P]), sb("identb", [P, P], BF16)
        causal, causalT = sb("causal", [P, P], BF16), sb("causalT", [P, P], BF16)
        stats = sb("stats", [P, NT, 6])
        mv1, rs1 = sb("mv1", [P, NT, 2]), sb("rs1", [P, NT])
        mv2, rs2 = sb("mv2", [P, NT, 2]), sb("rs2", [P, NT])
        mv3 = sb("mv3a", [P, NT, 2])
        mhalf = sb("mhalf", [P, NT])
        idle = sb("idle", [P, 2])
        cols = sb("cols", [P, 2, 4])
        CROSS = ((SC[:], cols[:, 0, :]), (PT[:, 0, 0:D], cols[:, 1, :]))
        W_STAGE = [(buf[:, 0:2 * D], buf[:, 2 * D:4 * D]) for buf in (
            PT[:].rearrange("p a n -> p (a n)"), V[:].rearrange("p t m n -> p (t m n)"), XR[:].rearrange("p t d -> p (t d)"))]
        W_STAGE.append((raw(AM[:].rearrange("p t s -> p (t s)")), raw(KM[:].rearrange("p t s -> p (t s)"))))
        AM_U8 = Yf[:].bitcast(U8).rearrange("p (t s) -> p t s", t=NT)
        KM_U8 = Sf[:].bitcast(U8).rearrange("p (t s) -> p t s", t=B)

        SM, ST, O, WK = banks("SM"), banks("ST"), banks("O"), banks("WK")

        xl_in, xr_in, x2_out = sem("xl_in"), sem("xr_in"), sem("x2_out")
        x2_ready = sem("x2_ready")
        mv_ready = sem("mv_ready")
        zero_out = sem("zero_out")
        w_in, vo_in = [[sem(f"{n}_in{k}") for k in range(KT)] for n in ("w", "vo")]
        am_in, km_in = sem("am_in"), sem("km_in")
        xw_in = sem("xw_in")
        ctx_in = sem("ctx_in")
        alibi_in = [sem(f"alibi_in{i}") for i in range(2)]
        stack_in, stack_in2 = [[sem(f"stack_in_{q}{i}") for i in range(2)] for q in ("sp", "pool")]
        mrow_in = [sem(f"mrow_in{i}") for i in range(2)]
        pool_c = sem("pool_c")
        pool_s = sem("pool_s")
        ones_ready = sem("ones_ready")
        stat1, rs1_ready = sem("stat1"), sem("rs1_ready")
        stat2, rs2_ready = sem("stat2"), sem("rs2_ready")
        ak_ready = sem("ak_ready")
        w_hi, w_lo = sem("w_hi"), sem("w_lo")
        vo_hi, vo_lo = sem("vo_hi"), sem("vo_lo")
        mask_ready = sem("mask_ready")
        xn_ready = sem("xn_ready")
        wk_ready, wk_free = sem("wk_ready"), sem("wk_free")
        hi_ready = sem("hi_ready")
        sm_ready, sm_free = sem("sm_ready"), sem("sm_free")
        st_ready, p_ready = sem("st_ready"), sem("p_ready")
        o_ready, o_free = sem("o_ready"), sem("o_free")
        y_done = sem("y_done")
        y_half = sem("y_half")
        sc_ready, nm_ready, ex_ready = sem("sc_ready"), sem("nm_ready"), sem("ex_ready")
        dv = sem("dv")
        block = st.enter_context(nc.Block())

        @block.sync
        def _(sp):
            def tiles(dram, b):
                return dram[bass.ds(b, 1)].rearrange("o (t p) d -> p (o t) d", p=P)

            wv = io["wqkv"].rearrange("(k p) n -> k p n", p=P)
            wov = io["wo"].rearrange("(k p) n -> k p n", p=P)
            sp.dma_start(XL[:], tiles(io["x"], 0)).then_inc(xl_in, 16)
            for k in range(KT):
                sp.dma_start(W_STAGE[k][0], wv[k][:, 0:2 * D]).then_inc(w_in[k], 16)
            for k in range(KT):
                vo = W_STAGE[k][1]
                sp.dma_start(vo[:, 0:D], wv[k][:, 2 * D:3 * D]).then_inc(vo_in[k], 16)
                sp.dma_start(vo[:, D:2 * D], wov[k]).then_inc(vo_in[k], 16)
            sp.dma_start(AM_U8, io["am"].rearrange("(t p) s -> p t s", p=P)).then_inc(am_in, 16)
            for b in range(B):
                sp.dma_start(KM_U8[:, b, :], io["km"][b:b + 1, :].broadcast_to([P, S])).then_inc(km_in, 16)
            sp.dma_start(XW[:, 0, :], io["xwq"]).then_inc(xw_in, 16)
            sp.dma_start(XW[:, 1, :], io["xwk"]).then_inc(x2_out, 16)
            sp.dma_start(bqk[:, 0:1], io["xbq"].rearrange("(p a) -> p a", a=1)).then_inc(xw_in, 16)
            sp.dma_start(bqk[:, 1:2], io["xbk"].rearrange("(p a) -> p a", a=1)).then_inc(xw_in, 16)

            def stack(opened, slot):
                sp.wait_ge(pool_s, opened)
                for j in range(HPG):
                    r = slice(HD * j, HD * j + HD)
                    sp.dma_start(raw(QS[0:HD, slot, j, :]), raw(qT[0][r, :])).then_inc(stack_in[slot], 16)
                    sp.dma_start(raw(QS[HD:2 * HD, slot, j, :]), raw(qT[0][r, :])).then_inc(stack_in[slot], 16)
                    sp.dma_start(raw(KS[0:HD, slot, j, :]), raw(kT[0][r, :])).then_inc(stack_in[slot], 16)
                    sp.dma_start(raw(KS[2 * HD:3 * HD, slot, j, :]), raw(kT[0][r, :])).then_inc(stack_in[slot], 16)

            stack(1, 0)

            def body(s):
                wk = Tick(s.wk_base)
                for g in range(GROUPS):
                    u = s.b * GROUPS + g
                    if g == 0 and s.main and not s.last:
                        sp.wait_ge(xn_ready, (s.b + 1) * NT)
                        sp.dma_start(XL[:], tiles(io["x"], s.b + 1)).then_inc(xl_in, 16)
                    if s.stacks(g):
                        stack(slot_open(s, g), (g + 1) % 2)
                    if s.main:
                        sp.wait_ge(sm_free, (u + 1) * N_SM)
                        for i in range(2):
                            sp.dma_start(raw(QS[ROW_MAX + i:ROW_MAX + i + 1, g % 2, :, :]).rearrange(
                                "o j (q n) -> o (j q) n", q=NT), raw(MT[i][:, :])).then_inc(mrow_in[g % 2], 16)
                    if g == 0:
                        if s.v:
                            wk.up(N_V)
                        if s.before:
                            sp.wait_ge(wk_free, s.wk_base)
                            sp.dma_start(CX, tiles(io["ctx"], s.b - 1)).then_inc(ctx_in, 16)
                            sp.wait_ge(x2_out, s.b * 32 - 16)
                            sp.dma_start(XR[:], tiles(io["x"], s.b - 1)).then_inc(xr_in, 16)
                    if s.projects(g):
                        wk.up(N_PROJ)
                    if s.turns(g):
                        wk.up(N_XT)
                    if s.before:
                        wk.up(N_WO + N_CTX + 1 if g == 0 else 1)
                    if s.first:
                        n = SLOT_TILES // ZERO_PARTS
                        c = slice(g * n * P, (g + 1) * n * P if g < ZERO_PARTS - 1 else SLOT_TILES * P)
                        sp.dma_start(slots_dram[c, :].rearrange("(i p) d -> p i d", p=P),
                                     Z[:].unsqueeze(1).broadcast_to([P, (c.stop - c.start) // P, D])).then_inc(zero_out, 16)
                if s.first:
                    sp.wait_ge(zero_out, ZERO_PARTS * 16)
                if s.tail:
                    for g in range(NT):
                        sp.wait_ge(x2_ready, (B - 1) * NT + g + 1)
                        sp.dma_start(x2_dram[B - 1, g * P:(g + 1) * P, :], XR[:, g, :]).then_inc(x2_out, 16)
                elif s.before:
                    sp.wait_ge(x2_ready, s.b * NT)
                    sp.dma_start(tiles(x2_dram, s.b - 1), XR[:]).then_inc(x2_out, 16)
                if s.before:
                    sp.wait_ge(mv_ready, s.b * NT)
                    sp.dma_start(mv_dram[bass.ds(s.b - 1, 1)].rearrange("o p n -> p (o n)"),
                                 mv3[:].rearrange("p t n -> p (t n)")).then_inc(x2_out, 16)

            over_batches(sp, body)
            sp.wait_ge(x2_out, 16 + (B - 1) * 32 + (NT + 1) * 16)

        @block.gpsimd
        def _(pool):
            nc.gpsimd.memset(ident[:], 0.0).then_inc(pool_c, 1)
            nc.gpsimd.memset(identb[:], 0.0).then_inc(pool_c, 1)
            nc.gpsimd.memset(causal[:], 0.0).then_inc(pool_c, 1)
            nc.gpsimd.memset(causalT[:], 0.0).then_inc(pool_c, 1)
            nc.gpsimd.memset(mhalf[:], -0.5).then_inc(pool_c, 1)
            nc.gpsimd.memset(Z[:], 0.0).then_inc(pool_c, 1)
            pool.wait_ge(pool_c, 6)
            for m in (ident, identb):
                nc.gpsimd.affine_select(out=m[:], in_=m[:], compare_op=ALU.not_equal, fill=1.0, base=0,
                                        pattern=[[-1, P]], channel_multiplier=1).then_inc(pool_c, 1)
            nc.gpsimd.affine_select(out=causal[:], in_=causal[:], compare_op=ALU.is_ge, fill=MASKED, base=0,
                                    pattern=[[-1, P]], channel_multiplier=1).then_inc(pool_c, 1)
            nc.gpsimd.affine_select(out=causalT[:], in_=causalT[:], compare_op=ALU.is_ge, fill=MASKED, base=0,
                                    pattern=[[1, P]], channel_multiplier=-1).then_inc(pool_c, 1)

            def rsqrt1(b):
                pool.wait_ge(stat1, b + 1)
                nc.gpsimd.tensor_tensor(rs1[:], rs1[:], mhalf[:], ALU.pow).then_inc(rs1_ready, 1)

            rsqrt1(0)

            def pause():
                if paused.n or not isinstance(paused.base, int) or paused.base:
                    pool.wait_ge(pool_s, paused.now())
                nc.gpsimd.tensor_tensor(idle[:, 0:1], mhalf[:, 0:1], mhalf[:, 0:1], ALU.mult).then_inc(pool_s, 1)
                paused.up()

            paused = Tick(0)

            def stack(slot, heads):
                for j in range(HPG):
                    r = slice(HD * j, HD * j + HD)
                    pool.dma_start(raw(QS[2 * HD:3 * HD, slot, j, :]), raw(qT[1][r, :])).then_inc(stack_in2[slot], 16)
                    pool.dma_start(raw(KS[HD:2 * HD, slot, j, :]), raw(kT[1][r, :])).then_inc(stack_in2[slot], 16)
                pool.dma_start(QS[ROW_ALIBI:ROW_MAX, slot, :, :], io["alq"][:, heads, :]).then_inc(alibi_in[slot], 16)
                pool.dma_start(KS[ROW_ALIBI:ROW_END, slot, :, :], io["alk"][:, heads, :]).then_inc(alibi_in[slot], 16)

            for k in range(DVE_SLICES, KT):
                pool.wait_ge(w_hi, k + 1)
                nc.gpsimd.tensor_tensor(Wqk[1][:, k, :], W_STAGE[k][0], raw(Wqk[0][:, k, :]), ALU.subtract
                                        ).then_inc(w_lo, 1)
            for k in range(KT):
                pool.wait_ge(vo_hi, k + 1)
                nc.gpsimd.tensor_tensor(Wv[1][:, k, :], W_STAGE[k][1][:, 0:D], raw(Wv[0][:, k, :]), ALU.subtract
                                        ).then_inc(vo_lo, 1)
            pool.wait_ge(w_lo, KT)
            pool.wait_ge(vo_lo, 2 * KT)
            nc.gpsimd.memset(V[:, :, :, HD:2 * HD], 1.0).then_inc(ones_ready, 1)
            pool.wait_ge(wk_free, N_XT + N_PROJ)
            pause()
            stack(0, slice(0, HPG))

            def body(s):
                nonlocal paused
                if not s.first:
                    paused = Tick(FIRST_PAUSES + (s.b - 1) * PAUSES - (2 if s.tail else 0))
                wk = Tick(s.wk_base)
                for g in range(GROUPS):
                    u = s.b * GROUPS + g
                    if s.stacks(g):
                        if not (s.first and g == 0):
                            pool.wait_ge(st_ready, u * N_ST)
                            pause()
                        pool.wait_ge(wk_free, wk.now())
                        pause()
                        h = HPG * ((g + 1) % GROUPS)
                        stack((g + 1) % 2, slice(h, h + HPG))
                    if g == 0 and s.v:
                        wk.up(N_V)
                    if s.before:
                        if g == 0:
                            pool.wait_ge(mask_ready, B)
                        pool.wait_ge(sc_ready, (s.b - 1) * NT + g + 1)
                        pause()
                        nc.gpsimd.tensor_tensor(AK[:].rearrange("p (o s) -> p o s", o=1), AM[:, g:g + 1, :],
                                                KM[:, bass.ds(s.b - 1, 1), :], ALU.add).then_inc(ak_ready, 1)
                    if g == 0 and s.main and not s.last:
                        rsqrt1(s.b + 1)
                    if g == 0 and s.before:
                        pool.wait_ge(stat2, s.b)
                        nc.gpsimd.tensor_tensor(rs2[:], rs2[:], mhalf[:], ALU.pow).then_inc(rs2_ready, 1)
                    if s.projects(g):
                        wk.up(N_PROJ)
                    if s.turns(g):
                        wk.up(N_XT)
                    if s.before:
                        wk.up(N_WO + N_CTX + 1 if g == 0 else 1)
            over_batches(pool, body)

        @block.tensor
        def _(pe):
            def three(out, pairs, start=True, stop=True):
                terms = [t for (ah, al), (bh, bl) in pairs for t in ((ah, bh), (ah, bl), (al, bh))]
                for i, (a, b) in enumerate(terms):
                    ins = nc.tensor.matmul(out, a, b, start=start and i == 0, stop=stop and i == len(terms) - 1,
                                           skip_group_check=True)
                return ins

            def item(wk, free=True):
                n = wk.up()
                if free:
                    pe.wait_ge(wk_free, n - 2)
                return WK[(wk.n - 1) % 2]

            def turn_x(wk, b, tiles, start=False):
                for t in tiles:
                    bank = item(wk, free=not (start and t < 2))
                    pe.wait_ge(xn_ready, b * NT + t + 1)
                    for k in range(KT):
                        ins = nc.tensor.transpose(bank[:, k * P:(k + 1) * P], XN[:, t % 2, k * P:(k + 1) * P], ident[:])
                    ins.then_inc(wk_ready, 1)

            def project(wk, g):
                for i in range(N_PROJ):
                    bank = item(wk)
                    c = slice(i * D + g * P, i * D + g * P + P)
                    three(bank[:], [((Wqk[0][:, k, c], Wqk[1][:, k, c]), (XT[0][:, k, :], XT[1][:, k, :]))
                                    for k in range(KT)]).then_inc(wk_ready, 1)

            def token_values(wk, t):
                bank, c = item(wk), slice(t * P, (t + 1) * P)
                three(bank[:], [((XT[0][:, k, c], XT[1][:, k, c]), (Wv[0][:, k, :], Wv[1][:, k, :]))
                                for k in range(KT)]).then_inc(wk_ready, 1)

            def turn_context(wk, b):
                bank = item(wk)
                pe.wait_ge(xw_in, 3 * 16)
                pe.wait_ge(x2_out, 16)
                for i in range(2):
                    ins = nc.tensor.transpose(bank[:, i * P:(i + 1) * P], XW[:, i, :], ident[:])
                ins.then_inc(wk_ready, 1)
                bank = item(wk)
                pe.wait_ge(ctx_in, b * 16)
                for t in range(NT):
                    ins = nc.tensor.transpose(bank[:, t * P:(t + 1) * P], CX[:, t, :], ident[:])
                ins.then_inc(wk_ready, 1)
                return wk.now()

            def cross_projections(wk, ctx_ready):
                for i in range(2):
                    bank = item(wk)
                    if i == 0:
                        pe.wait_ge(wk_free, ctx_ready)
                    nc.tensor.matmul(bank[:], XWT[:, i, :], ctxT[:], start=True, stop=True).then_inc(wk_ready, 1)

            def output(wk, t):
                bank, c = item(wk), slice(t * P, (t + 1) * P)
                three(bank[:], [((Y[0][:, k, c], Y[1][:, k, c]), (Wo[0][:, k, :], Wo[1][:, k, :]))
                                for k in range(GROUPS)]).then_inc(wk_ready, 1)

            def row_maxima(s, g, u, i):
                if i == 0:
                    pe.wait_ge(stack_in[g % 2], nth(s, g) * STACK_SP * 16)
                    pe.wait_ge(stack_in2[g % 2], nth(s, g) * STACK_POOL * 16)
                    pe.wait_ge(alibi_in[g % 2], nth(s, g) * 2 * 16)
                q, j0, nj = SM_PIECES[i]
                if not (s.first and g == 0 and i < 2):
                    pe.wait_ge(sm_free, u * N_SM + i - 1)
                bank, w = SM[i % 2], (q + 1) * P
                for n in range(nj):
                    nc.tensor.matmul(bank[:, n * w:(n + 1) * w], QS[0:ROW_MAX, g % 2, j0 + n, q * P:(q + 1) * P],
                                     KS[0:ROW_MAX, g % 2, j0 + n, 0:w], start=(n == 0), stop=False,
                                     skip_group_check=True)
                    ins = nc.tensor.matmul(bank[:, (n + 1) * w - P:(n + 1) * w], identb[:], causal[:],
                                           start=False, stop=True, skip_group_check=True)
                ins.then_inc(sm_ready, 1)

            def turn_maxima(u):
                pe.wait_ge(sm_free, (u + 1) * N_SM - 1)
                nc.tensor.transpose(SM[(N_SM - 1) % 2][0:HPG * NT, 0:P], NM[:], ident[:]).then_inc(sm_ready, 1)

            def scores(s, g, u, j):
                for n, piece in enumerate(ST_PIECES):
                    m = j * len(ST_PIECES) + n
                    if not (s.first and g == 0 and m < 2):
                        pe.wait_ge(p_ready, u * N_ST + m - 1)
                    bank, at = ST[m % 2], 0
                    for kb in piece:
                        w = S - kb * P
                        nc.tensor.matmul(bank[:, at:at + w], KS[0:ROW_END, g % 2, j, kb * P:(kb + 1) * P],
                                         QS[0:ROW_END, g % 2, j, kb * P:S], start=(at == 0), stop=False,
                                         skip_group_check=True)
                        ins = nc.tensor.matmul(bank[:, at:at + P], identb[:], causalT[:], start=False, stop=True,
                                               skip_group_check=True)
                        at += w
                    ins.then_inc(st_ready, 1)

            def values(s, g, u, j, blocks=range(NT)):
                i = u * HPG + j
                if blocks[0] == 0:
                    if not (s.first and g == 0 and j < 2):
                        pe.wait_ge(o_free, i - 1)
                    pe.wait_ge(p_ready, (i + 1) * len(ST_PIECES))
                    if g == 0 and j == 0:
                        pe.wait_ge(wk_free, s.wk_base + (N_V if s.v else 0))
                        pe.wait_ge(ones_ready, 1)
                h = g * HPG + j
                a = HD * (h % 2)
                for kb in blocks:
                    at = P_AT[kb]
                    ins = nc.tensor.matmul(O[j % 2][0:2 * HD, kb * P:S], V[:, kb, h // 2, a:a + 2 * HD],
                                           PT[:, j % 2, at:at + S - kb * P], start=(kb == 0), stop=(kb == NT - 1),
                                           skip_group_check=True)
                if blocks[-1] == NT - 1:
                    ins.then_inc(o_ready, 1)

            wk = Tick(0)
            pe.wait_ge(pool_c, 10)
            turn_x(wk, 0, range(NT), start=True)
            pe.wait_ge(w_lo, KT)
            pe.wait_ge(wk_free, N_XT)
            project(wk, 0)
            pe.wait_ge(vo_lo, 2 * KT)
            for t in range(NT):
                token_values(wk, t)
            project(wk, 1)

            def body(s):
                wk = Tick(s.wk_base)
                for g in range(GROUPS):
                    u = s.b * GROUPS + g
                    ends = {}
                    if not (s.first and g == 0):
                        ends = VALUES_FIRST if g == 0 else VALUES_AFTER if s.projects(g) else VALUES_LATE
                    for i in range(len(SM_PIECES) if s.main else 0):
                        row_maxima(s, g, u, i)
                        if i in ends:
                            j, blocks = ends[i]
                            values(s, (g - 1) % GROUPS, u - 1, j, blocks)
                        if g == 0 and s.before and i in V_AFTER:
                            token_values(wk, V_AFTER.index(i))
                    if s.main:
                        turn_maxima(u)
                    if s.main and ends is VALUES_LATE:
                        values(s, g - 1, u - 1, HPG - 1)
                    if g == 0 and s.before and s.main:
                        token_values(wk, 2)
                        token_values(wk, 3)
                    if s.tail and g == 0:
                        values(s, GROUPS - 1, u - 1, HPG - 2)
                        values(s, GROUPS - 1, u - 1, HPG - 1)
                    if s.projects(g):
                        if g == 2:
                            pe.wait_ge(wk_free, x_split)
                        project(wk, (g + 2) % GROUPS)
                    if s.main:
                        pe.wait_ge(mrow_in[g % 2], nth(s, g) * 2 * 16)
                        scores(s, g, u, 0)
                        scores(s, g, u, 1)
                        values(s, g, u, 0)
                    if g == 0 and s.before:
                        ctx_ready = turn_context(wk, s.b)
                        if s.tail:
                            cross_projections(wk, ctx_ready)
                            cross_ready = wk.now()
                            for t in range(NT):
                                pe.wait_ge(y_half, t // 2 + 1)
                                output(wk, t)
                        else:
                            pe.wait_ge(y_done, s.b * GROUPS)
                            for t in range(NT):
                                output(wk, t)
                            cross_projections(wk, ctx_ready)
                            cross_ready = wk.now()
                    if s.turns(g):
                        turn_x(wk, s.b + 1, (0, 1))
                    if s.main:
                        scores(s, g, u, 2)
                    if s.turns(g):
                        turn_x(wk, s.b + 1, (2, 3))
                        x_split = wk.now()
                    if s.before:
                        bank = item(wk)
                        if g == 0:
                            pe.wait_ge(wk_free, cross_ready)
                        nc.tensor.matmul(bank[:], qpT[:, g * P:(g + 1) * P], kpT[:], start=True, stop=True).then_inc(wk_ready, 1)
                    if s.main:
                        values(s, g, u, 1)
                        scores(s, g, u, 3)

            over_batches(pe, body)

        @block.scalar
        def _(act):
            def hi_x(wk, tiles=range(NT)):
                for t in tiles:
                    act.wait_ge(wk_ready, wk.up())
                    nc.scalar.activation(XT[0][:, :, t * P:(t + 1) * P], WK[(wk.n - 1) % 2][:].rearrange(
                        "p (k n) -> p k n", k=KT), ACT.Copy).then_inc(hi_ready, 1)

            def hi_qk(wk, before=None, slot=0):
                for i in range(N_PROJ):
                    dst, scale = ((qT[0], ATT_SCALE), (kT[0], 1.0))[i]
                    act.wait_ge(wk_ready, wk.up())
                    if i == 0 and before is not None:
                        act.wait_ge(stack_in[slot], before * STACK_SP * 16)
                        act.wait_ge(stack_in2[slot], before * STACK_POOL * 16)
                    nc.scalar.activation(dst[:], WK[(wk.n - 1) % 2][:], ACT.Copy, scale=scale).then_inc(hi_ready, 1)

            wk = Tick(0)
            for k in range(KT):
                act.wait_ge(w_in[k], 16)
                nc.scalar.activation(Wqk[0][:, k, :], W_STAGE[k][0], ACT.Copy).then_inc(w_hi, 1)
            hi_x(wk)
            for n, W in enumerate((Wv, Wo)):
                for k in range(KT):
                    if n == 0:
                        act.wait_ge(vo_in[k], 32)
                    nc.scalar.activation(W[0][:, k, :], W_STAGE[k][1][:, n * D:(n + 1) * D], ACT.Copy).then_inc(vo_hi, 1)
            hi_qk(wk)
            wk.up(N_V)
            hi_qk(wk, 1, 0)

            def exps(s, g, u, j):
                i = u * HPG + j
                for n, piece in enumerate(ST_PIECES):
                    m = j * len(ST_PIECES) + n
                    if n == 0 and not (s.first and g == 0 and j < 2):
                        act.wait_ge(o_ready, i - 1)
                    act.wait_ge(st_ready, u * N_ST + m + 1)
                    w = sum(S - kb * P for kb in piece)
                    at = P_AT[piece[0]]
                    nc.scalar.activation(PT[:, j % 2, at:at + w], ST[m % 2][:, 0:w], ACT.Exp).then_inc(p_ready, 1)

            def outputs(s, g, u, j):
                i, bank = u * HPG + j, O[j % 2]
                act.wait_ge(o_ready, i + 1)
                if j == 0 and not (s.first and g == 0):
                    act.wait_ge(y_done, u)
                r, odd = slice(j * HD, (j + 1) * HD), j % 2
                lower, upper = bank[0:HD, :], bank[HD:2 * HD, :]
                if s.first and g == 0 and j == 0:
                    act.wait_ge(mask_ready, B)
                nc.scalar.activation(Yf[r, :], upper if odd else lower, ACT.Copy)
                nc.scalar.activation(Sf[r, :], lower if odd else upper, ACT.Copy).then_inc(o_free, 1)

            def body(s):
                wk = Tick(s.wk_base)
                for g in range(GROUPS):
                    u = s.b * GROUPS + g
                    if g == 0 and s.v:
                        wk.up(N_V)
                    if s.projects(g):
                        hi_qk(wk, nth(s, g + 1), (g + 1) % 2)
                    if s.main:
                        exps(s, g, u, 0)
                        exps(s, g, u, 1)
                    if s.turns(g):
                        hi_x(wk, (0, 1))
                    if s.main:
                        exps(s, g, u, 2)
                        outputs(s, g, u, 0)
                    if s.turns(g):
                        hi_x(wk, (2, 3))
                    if s.before:
                        wk.up(N_WO + N_CTX + 1 if g == 0 else 1)
                        act.wait_ge(nm_ready, (s.b - 1) * NT + g + 1)
                        sc, col = CROSS[g % 2 if s.tail else 0]
                        nc.scalar.activation(sc, sc, ACT.Exp, bias=col[:, 1:2], accum_out=col[:, 2:3]).then_inc(ex_ready, 1)
                    if s.main:
                        exps(s, g, u, 3)
                        for j in range(1, HPG):
                            outputs(s, g, u, j)

            over_batches(act, body)

        @block.vector
        def _(dve):
            d = Tick(0)
            DV_PER = 2 * NT + 2 * NT + GROUPS + 3 * GROUPS + 3 * NT

            def pause():
                nc.vector.memset(idle[:, 1:2], 0.0)

            def statistics(b):
                dve.wait_ge(xl_in, (b + 1) * 16)
                for t in range(NT):
                    nc.vector.bn_stats(stats[:, t, :], XL[:, t, :]).then_inc(dv, 1)
                dve.wait_ge(dv, d.up(NT))
                pause()
                for t in range(NT):
                    nc.vector.bn_aggr(mv1[:, t, :], stats[:, t, :]).then_inc(dv, 1)
                dve.wait_ge(dv, d.up(NT))
                nc.vector.tensor_scalar(rs1[:], mv1[:, :, 1], LN_EPS, None, ALU.add).then_inc(stat1, 1)

            def normalise(b, t):
                nc.vector.tensor_scalar(XN[:, t % 2, :], XL[:, t, :], mv1[:, t, 0:1], rs1[:, t:t + 1],
                                        ALU.subtract, ALU.mult).then_inc(xn_ready, 1)

            def first_tiles(b):
                dve.wait_ge(rs1_ready, b + 1)
                normalise(b, 0)
                normalise(b, 1)

            def lo_x(wk, hi, b, tiles):
                for t in tiles:
                    dve.wait_ge(wk_ready, wk.up())
                    dve.wait_ge(hi_ready, hi.up())
                    c = slice(t * P, (t + 1) * P)
                    nc.vector.tensor_tensor(XT[1][:, :, c], WK[(wk.n - 1) % 2][:].rearrange("p (k n) -> p k n", k=KT),
                                            XT[0][:, :, c].bitcast(F32), ALU.subtract).then_inc(wk_free, 1)
                    if t + 2 < NT:
                        normalise(b, t + 2)

            def token_values(wk, t):
                dve.wait_ge(wk_ready, wk.up())
                nc.vector.tensor_copy(V[:, t, :, :].rearrange("p m (c d) -> p m c d", c=3)[:, :, 0:3:2, :],
                                      WK[(wk.n - 1) % 2][:].rearrange("p (m c d) -> p m c d", c=2, d=HD)
                                      ).then_inc(wk_free, 1)

            def lo_qk(wk, hi):
                for i, (pr, scale) in enumerate(((qT, ATT_SCALE), (kT, 1.0))):
                    dve.wait_ge(wk_ready, wk.up())
                    dve.wait_ge(hi_ready, hi.up())
                    nc.vector.scalar_tensor_tensor(out=pr[1][:], in0=WK[(wk.n - 1) % 2][:], scalar=scale,
                                                   in1=pr[0][:].bitcast(F32), op0=ALU.mult,
                                                   op1=ALU.subtract).then_inc(wk_free, 1)

            statistics(0)
            wk, hi = Tick(0), Tick(0)
            for k in range(DVE_SLICES):
                if k == 1:
                    first_tiles(0)
                dve.wait_ge(w_hi, k + 1)
                nc.vector.tensor_tensor(Wqk[1][:, k, :], W_STAGE[k][0], raw(Wqk[0][:, k, :]), ALU.subtract
                                        ).then_inc(w_lo, 1)
            lo_x(wk, hi, 0, range(NT))
            for k in range(KT):
                dve.wait_ge(vo_hi, KT + k + 1)
                nc.vector.tensor_tensor(Wo[1][:, k, :], W_STAGE[k][1][:, D:2 * D], raw(Wo[0][:, k, :]), ALU.subtract
                                        ).then_inc(vo_lo, 1)
            lo_qk(wk, hi)
            dve.wait_ge(ones_ready, 1)
            for t in range(NT):
                token_values(wk, t)
            dve.wait_ge(vo_lo, 2 * KT)
            dve.wait_ge(am_in, 16)
            nc.vector.tensor_scalar(AM[:], AM_U8, MASK, None, ALU.mult).then_inc(sc_ready, 1)
            dve.wait_ge(km_in, 16 * B)
            for b in range(B):
                nc.vector.tensor_scalar(KM[:, b, :], KM_U8[:, b, :], MASK, None, ALU.mult).then_inc(mask_ready, 1)
            lo_qk(wk, hi)

            def maxima(u, i):
                q, j0, nj = SM_PIECES[i]
                dve.wait_ge(sm_ready, u * N_SM + i + 1)
                w = (q + 1) * P
                c = slice(j0 * NT + q, (j0 + nj - 1) * NT + q + 1, NT)
                nc.vector.tensor_reduce(NM[:, c], SM[i % 2][:, 0:nj * w].rearrange("p (j n) -> p j n", j=nj), AX_X,
                                        ALU.max, negate=True).then_inc(sm_free, 1)

            def split_maxima(s, g, u):
                dve.wait_ge(sm_ready, (u + 1) * N_SM)
                if g:
                    dve.wait_ge(mrow_in[(g - 1) % 2], nth(s, g - 1) * 2 * 16)
                elif not s.first:
                    dve.wait_ge(mrow_in[(g - 1) % 2], s.b * (GROUPS // 2) * 2 * 16)
                bank = SM[(N_SM - 1) % 2]
                nc.vector.tensor_copy(MT[0][:], bank[0:HPG * NT, 0:P]).then_inc(dv, 1)
                dve.wait_ge(dv, d.up())
                nc.vector.tensor_tensor(MT[1][:], bank[0:HPG * NT, 0:P], MT[0][:].bitcast(F32),
                                        ALU.subtract).then_inc(sm_free, 1)

            def finish_unit(u, g, cols=slice(0, S), done=y_done):
                dve.wait_ge(o_free, (u + 1) * HPG)
                nc.vector.reciprocal(Sf[:, cols], Sf[:, cols]).then_inc(dv, 1)
                dve.wait_ge(dv, d.up())
                nc.vector.tensor_tensor(Yf[:, cols], Yf[:, cols], Sf[:, cols], ALU.mult).then_inc(dv, 1)
                dve.wait_ge(dv, d.up())
                nc.vector.tensor_copy(Y[0][:, g, cols], Yf[:, cols]).then_inc(dv, 1)
                dve.wait_ge(dv, d.up())
                nc.vector.tensor_tensor(Y[1][:, g, cols], Yf[:, cols], Y[0][:, g, cols].bitcast(F32), ALU.subtract
                                        ).then_inc(done, 1)

            def residual(wk, b):
                for t in range(NT):
                    dve.wait_ge(wk_ready, wk.up())
                    if t == 0:
                        dve.wait_ge(xr_in, (b + 1) * 16)
                    xt = XR[:, t, :]
                    nc.vector.tensor_tensor(xt, WK[(wk.n - 1) % 2][:], xt, ALU.add).then_inc(wk_free, 1)
                    dve.wait_ge(wk_free, wk.now())
                    nc.vector.bn_stats(stats[:, t, :], xt).then_inc(dv, 1)
                dve.wait_ge(dv, d.up(NT))
                pause()
                for t in range(NT):
                    nc.vector.bn_aggr(mv2[:, t, :], stats[:, t, :]).then_inc(dv, 1)
                dve.wait_ge(dv, d.up(NT))
                nc.vector.tensor_scalar(rs2[:], mv2[:, :, 1], LN_EPS, None, ALU.add).then_inc(stat2, 1)

            def turn_context(wk):
                dve.wait_ge(wk_ready, wk.up())
                nc.vector.tensor_copy(XWT[:], WK[(wk.n - 1) % 2][:, 0:2 * P].rearrange("p (a n) -> p a n", a=2)).then_inc(wk_free, 1)
                dve.wait_ge(wk_ready, wk.up())
                nc.vector.tensor_copy(ctxT[:], WK[(wk.n - 1) % 2][:]).then_inc(wk_free, 1)

            def context(wk):
                for i, dst in enumerate((qpT, kpT)):
                    dve.wait_ge(wk_ready, wk.up())
                    nc.vector.tensor_scalar(dst[:], WK[(wk.n - 1) % 2][:], bqk[:, i:i + 1], None, ALU.add).then_inc(wk_free, 1)

            def cross_scores(wk, b, g, slot=0):
                sc, col = CROSS[slot]
                if g == 0:
                    dve.wait_ge(rs2_ready, b + 1)
                tile = XR[:, g, :]
                nc.vector.tensor_scalar(Z[:], tile, mv2[:, g, 0:1], rs2[:, g:g + 1], ALU.subtract, ALU.mult).then_inc(dv, 1)
                dve.wait_ge(dv, d.up())
                dve.wait_ge(wk_ready, wk.up())
                nc.vector.scalar_tensor_tensor(out=sc, in0=WK[(wk.n - 1) % 2][:], scalar=X_SCALE, in1=Z[:], op0=ALU.mult,
                                               op1=ALU.mult).then_inc(wk_free, 1)
                dve.wait_ge(wk_free, wk.now())
                dve.wait_ge(ak_ready, b * NT + g + 1)
                pause()
                nc.vector.tensor_tensor_reduce(out=sc, in0=sc, in1=AK[:], scale=1.0, scalar=LEAST, op0=ALU.add,
                                               op1=ALU.max, accum_out=col[:, 0:1]).then_inc(sc_ready, 1)
                dve.wait_ge(sc_ready, b * NT + g + 2)
                nc.vector.tensor_scalar(col[:, 1:2], col[:, 0:1], -1.0, None, ALU.mult).then_inc(nm_ready, 1)

            def cross_add(b, g, slot=0):
                sc, col = CROSS[slot]
                tile = XR[:, g, :]
                dve.wait_ge(ex_ready, b * NT + g + 1)
                nc.vector.reciprocal(col[:, 3:4], col[:, 2:3]).then_inc(dv, 1)
                dve.wait_ge(dv, d.up())
                nc.vector.scalar_tensor_tensor(out=tile, in0=sc, scalar=col[:, 3:4], in1=tile, op0=ALU.mult,
                                               op1=ALU.add).then_inc(x2_ready, 1)
                dve.wait_ge(x2_ready, b * NT + g + 1)
                nc.vector.bn_stats(stats[:, g, :], tile).then_inc(dv, 1)
                dve.wait_ge(dv, d.up())
                pause()
                nc.vector.bn_aggr(mv3[:, g, :], stats[:, g, :]).then_inc(mv_ready, 1)
                dve.wait_ge(mv_ready, b * NT + g + 1)
                pause()

            def body(s):
                nonlocal d, steps_before
                looped = not isinstance(s.b, int)
                d = Tick(steps_before + (s.b - 1) * DV_PER if looped else steps_before)
                wk = Tick(s.wk_base)
                hi = Tick(HI_PER * s.b + WK_START)
                for g in range(GROUPS):
                    u = s.b * GROUPS + g
                    for i in range(len(SM_PIECES) if s.main else 0):
                        maxima(u, i)
                        if g == 0 and s.before and i in V_AFTER:
                            token_values(wk, V_AFTER.index(i))
                    if s.main:
                        split_maxima(s, g, u)
                    if g == 0 and s.main and not s.last:
                        statistics(s.b + 1)
                    if g == 0 and s.before and s.main:
                        token_values(wk, 2)
                        token_values(wk, 3)
                    if s.tail and g == 0:
                        turn_context(wk)
                        context(wk)
                        for h in range(2):
                            finish_unit(u - 1, GROUPS - 1, slice(h * S // 2, (h + 1) * S // 2), y_half)
                        residual(wk, B - 1)
                    elif s.main and not (s.first and g == 0):
                        finish_unit(u - 1, (g - 1) % GROUPS)
                    if s.turns(g):
                        first_tiles(s.b + 1)
                    if s.projects(g):
                        lo_qk(wk, hi)
                    if g == 0 and s.v:
                        turn_context(wk)
                        residual(wk, s.b - 1)
                        context(wk)
                    if s.turns(g):
                        lo_x(wk, hi, s.b + 1, range(NT))
                    if s.tail:
                        cross_scores(wk, B - 1, g, g % 2)
                        if g:
                            cross_add(B - 1, g - 1, (g - 1) % 2)
                    elif s.before:
                        cross_scores(wk, s.b - 1, g)
                        cross_add(s.b - 1, g)
                if s.tail:
                    cross_add(B - 1, NT - 1, (NT - 1) % 2)
                if looped:
                    assert d.n == DV_PER, d.n
                steps_before = steps_before + (B - 2) * DV_PER if looped else d.now()

            steps_before = d.now()
            over_batches(dve, body)


def routing_constants():
    expert = np.arange(E, dtype=np.float32)
    full = np.arange(TILES, dtype=np.float32) * P
    before = (expert[None, :] < expert[:, None]).astype(np.float32)
    tile = np.arange(SLOT_TILES, dtype=np.float32)
    row = np.concatenate([expert, full, before.ravel(), tile])
    return np.ascontiguousarray(np.broadcast_to(row, (P, row.size)))


def router_and_shared(nc, io, x2_dram, mv_dram, slots_dram, HR, G, SL, EID, load_experts):
    with ExitStack() as st:
        sb = lambda name, shape, dt=F32: st.enter_context(nc.sbuf_tensor(name, shape, dt))
        bank = lambda name: st.enter_context(nc.psum_tensor(name, [P, 512], F32))
        sem = lambda name: st.enter_context(nc.semaphore(name))
        pair = lambda name, shape: [sb(f"{name}_{p}", shape, F32R) for p in ("hi", "lo")]

        WS, WSD, RW = pair("WS", [P, KT, 2 * FF]), pair("WSD", [P, FT, D]), pair("RW", [P, KT, E])
        HT = pair("HT", [P, KT, S])
        AT = pair("AT", [P, 2, FT, S])
        XB = sb("XB", [P, NT, D])
        SG = sb("SG", [P, FT, S])
        rms = sb("rms_b", [P, D])
        RWf = sb("RWf", [P, KT, E])
        LT = sb("LT", [E, 2, 2 * P])
        L = sb("L", [P, TILES, E])
        M8, I8, I8f = sb("M8", [P, TILES, E]), sb("I8", [P, TILES, E], mybir.dt.uint32), sb("I8f", [P, TILES, E])
        OH = [sb(f"OH{k}", [P, TILES, E]) for k in range(TOP)]
        OHb = sb("OHb", [P, TILES, E], BF16)
        RK, TMP = sb("RK", [P, TILES, E]), sb("TMP", [P, TILES, E])
        cnt, ntl, base = sb("cnt", [P, E]), sb("ntl", [P, E]), sb("base", [P, E])
        gt = rms[:, 0:E * TILES].rearrange("p (e t) -> p e t", e=E)
        cst = sb("cst_sb", [P, E + TILES + E * E + SLOT_TILES])
        c_expert, c_full = cst[:, 0:E], cst[:, E:E + TILES]
        c_before = cst[:, E + TILES:E + TILES + E * E].rearrange("p (e f) -> p e f", e=E)
        c_tile = cst[:, E + TILES + E * E:]
        le = rms[:, E * TILES:E * TILES + SLOT_TILES * (E - 1)].rearrange("p (s e) -> p s e", e=E - 1)
        eidf = sb("eidf", [P, SLOT_TILES])
        slf = sb("slf", [P, TILES])
        ident, lower, ones = sb("ident2", [P, P]), sb("lower", [P, P], BF16), sb("ones2", [P, P], BF16)
        mv = sb("mv3", [P, TILES, 2])
        rs, mhalf = sb("rs3", [P, TILES]), sb("mhalf3", [P, TILES])

        WK = [bank(f"WKb{i}") for i in range(3)]
        GU = [bank(f"GUb{i}") for i in range(2 * FT)]
        LR = bank("LR")
        LG, RB = LR[:, 0:TILES * E], LR[:, TILES * E:(2 * TILES + 1) * E]

        x0_in = [sem(f"f_x0_in{t}") for t in range(NT)]
        x_in = [None] + [sem(f"f_x_in{b}") for b in range(1, B)]
        xb_in = [sem(f"f_xb_in{t}") for t in range(NT)]
        w_in, w_hi, w_lo = [sem(f"f_w_in{k}") for k in range(KT + FT)], sem("f_w_hi"), sem("f_w_lo")
        c_in, rw_in, rms_in, mv_in = sem("f_c_in"), sem("f_rw_in"), sem("f_rms_in"), sem("f_mv_in")
        pc = sem("f_pc")
        var_ready, rs_ready = sem("f_var"), sem("f_rs")
        h0_ready, h_ready = sem("f_h0"), sem("f_h")
        wk_ready, wk_free, hi_ready = sem("f_wk"), sem("f_wkf"), sem("f_hi")
        lg_ready, lt_ready, lg_turned = sem("f_lg"), sem("f_lt"), sem("f_lgt")
        e2_in, e2_out = sem("f_e2i"), sem("f_e2o")
        acc_out = sem("f_acc")
        oh_ready, rk_ready, sl_ready = sem("f_oh"), sem("f_rk"), sem("f_sl")
        scat = [sem(f"f_scat{b}") for b in range(B)]
        gu_ready, sg_ready, at0_ready, at_hi, at_ready = [sem(f"f_{n}") for n in ("gu", "sg", "at0", "at_hi", "at")]
        dv = sem("f_dv")
        block = st.enter_context(nc.Block())

        SPIECES = KT + FT
        ORDER = (B - 1,) + tuple(range(B - 1))

        RING, LAG = 2 * FT, 3
        HALVES = TILES // 2

        def h_tile(i):
            return HR[i // NT][:, i % NT, :]

        def work_bank(at):
            return GU[at % RING] if at < TILES else WK[(at - TILES) % len(WK)]

        def bank_free(at):
            return max(at + 1 - len(WK), TILES)

        FILLS = ["T1"] + [fill for n in range(1, B) for fill in ([f"T{n + 1}"] if n < B - 1 else []) + [f"D{n - 1}"]] + [f"D{B - 1}"]

        def stage(k):
            return SG[:, k, :] if k < FT else XB[:, k - FT, :]

        def turned_at(n):
            return TILES + NT * FILLS.index(f"T{n}")

        def down_at(n):
            return TILES + NT * FILLS.index(f"D{n}")

        @block.sync
        def _(sp):
            x2 = x2_dram.rearrange("b (t p) d -> b p t d", p=P)
            sp.dma_start(mv[:].rearrange("p (b t) c -> p b (t c)", b=B), mv_dram.rearrange("b p n -> p b n")).then_inc(mv_in, 16)
            sp.dma_start(rms[:], io["rms"].rearrange("(a d) -> a d", a=1).broadcast_to([P, D])).then_inc(rms_in, 16)
            for t in range(NT):
                sp.dma_start(HR[0][:, t, :], x2[0][:, t, :]).then_inc(x0_in[t], 16)
            sp.dma_start(RWf[:], io["router"].rearrange("(k p) e -> p k e", p=P)).then_inc(rw_in, 16)
            for b in range(1, B):
                sp.dma_start(HR[b][:], x2[b]).then_inc(x_in[b], 16)
            sp.dma_start(cst[:], io["cst"]).then_inc(c_in, 16)
            for k in range(SPIECES):
                if k < KT:
                    r = slice(k * P, (k + 1) * P)
                    sp.dma_start(stage(k)[:, 0:FF], io["swg"][r, :]).then_inc(w_in[k], 16)
                    sp.dma_start(stage(k)[:, FF:2 * FF], io["swu"][r, :]).then_inc(w_in[k], 16)
                else:
                    r = slice((k - KT) * P, (k - KT + 1) * P)
                    sp.dma_start(stage(k), io["swd"][r, :]).then_inc(w_in[k], 16)
            load_experts(sp)
            sp.wait_ge(w_lo, SPIECES + 1)
            for n, b in enumerate(ORDER):
                for t in range(NT):
                    if n:
                        sp.wait_ge(wk_free, down_at(n - 1) + t + 1)
                    sp.dma_start(XB[:, t, :], x2[b][:, t, :]).then_inc(xb_in[t], 16)
            sp.dma_start(x2[ORDER[0]], HR[ORDER[0]][:]).then_inc(acc_out, 16)
            sp.wait_ge(acc_out, 16)

        @block.gpsimd
        def _(pool):
            nc.gpsimd.memset(mhalf[:], -0.5).then_inc(pc, 1)
            nc.gpsimd.memset(ident[:], 0.0).then_inc(pc, 1)
            nc.gpsimd.memset(lower[:], 1.0).then_inc(pc, 1)
            nc.gpsimd.memset(ones[:], 1.0).then_inc(pc, 1)
            pool.wait_ge(pc, 4)
            nc.gpsimd.affine_select(out=ident[:], in_=ident[:], compare_op=ALU.not_equal, fill=1.0, base=0,
                                    pattern=[[-1, P]], channel_multiplier=1).then_inc(pc, 1)
            nc.gpsimd.affine_select(out=lower[:], in_=lower[:], compare_op=ALU.is_gt, fill=0.0, base=0,
                                    pattern=[[1, P]], channel_multiplier=-1).then_inc(pc, 1)

            pool.wait_ge(var_ready, 1)
            for c in (slice(0, NT), slice(NT, TILES)):
                nc.gpsimd.tensor_tensor(rs[:, c], rs[:, c], mhalf[:, c], ALU.pow).then_inc(rs_ready, 1)
            pool.wait_ge(sl_ready, TOP)
            for b in ORDER:
                for t in range(b * NT, (b + 1) * NT):
                    for k in range(TOP):
                        pool.indirect_dma_start(out=slots_dram, out_offset=bass.IndirectOffsetOnAxis(ap=SL[k][:, t:t + 1], axis=0),
                                                in_=HR[b][:, t - b * NT, :], in_offset=None).then_inc(scat[b], 16)
            for b in range(B):
                pool.wait_ge(scat[b], NT * TOP * 16)

        @block.tensor
        def _(pe):
            def three(out, pairs):
                terms = [t for (ah, al), (bh, bl) in pairs for t in ((ah, bh), (ah, bl), (al, bh))]
                for i, (a, b) in enumerate(terms):
                    ins = nc.tensor.matmul(out, a, b, start=(i == 0), stop=(i == len(terms) - 1))
                return ins

            pe.wait_ge(pc, 6)

            def turn(i, at):
                bank = work_bank(at)
                for k in range(KT):
                    ins = nc.tensor.transpose(bank[:, k * P:(k + 1) * P], h_tile(i)[:, k * P:(k + 1) * P], ident[:])
                ins.then_inc(wk_ready, 1)

            def turn_logits(j):
                pe.wait_ge(lt_ready, j + 1)
                for i in range(2):
                    c = slice((2 * j + i) * E, (2 * j + i + 1) * E)
                    ins = nc.tensor.transpose(LG[:, c], LT[:, j % 2, i * P:(i + 1) * P], ident[0:E, 0:E])
                ins.then_inc(lg_turned, 1)

            for i in range(TILES + LAG + 2):
                if i < TILES:
                    pe.wait_ge(h_ready, i + 1)
                    if i >= RING:
                        pe.wait_ge(wk_free, i - RING + 1)
                    turn(i, i)
                j = (i - LAG) // 2
                if i >= LAG and i % 2 and j < HALVES:
                    if j >= 2:
                        pe.wait_ge(lt_ready, j - 1)
                    elif j == 0:
                        pe.wait_ge(w_lo, 1)
                    pe.wait_ge(wk_free, 2 * j + 2)
                    c = slice(j % 2 * 2 * P, (j % 2 + 1) * 2 * P)
                    three(WK[j % 2][0:E, 0:2 * P], [((RW[0][:, k, :], RW[1][:, k, :]), (HT[0][:, k, c], HT[1][:, k, c]))
                                                    for k in range(KT)]).then_inc(lg_ready, 1)
                    if j:
                        turn_logits(j - 1)
            turn_logits(HALVES - 1)

            def ranks():
                pe.wait_ge(oh_ready, 1)
                nc.tensor.matmul(RB[:, 0:TILES * E], lower[:], OHb[:].rearrange("p t e -> p (t e)"), start=True, stop=False,
                                 skip_group_check=True)
                for t in range(TILES - 1):
                    n = TILES - 1 - t
                    nc.tensor.matmul(RB[:, (t + 1) * E:TILES * E].rearrange("p (t e) -> p t e", e=E), ones[:],
                                     OHb[:, t:t + 1, :].broadcast_to([P, n, E]), start=False, stop=(n == 1),
                                     skip_group_check=True)
                for t in range(TILES):
                    ins = nc.tensor.matmul(RB[:, TILES * E:(TILES + 1) * E], ones[:], OHb[:, t, :], start=(t == 0),
                                           stop=(t == TILES - 1), skip_group_check=True)
                ins.then_inc(rk_ready, 1)

            def output(n):
                pe.wait_ge(at_ready, FT * (n + 1))
                for t in range(NT):
                    at = down_at(n) + t
                    pe.wait_ge(wk_free, bank_free(at))
                    c = slice(t * P, (t + 1) * P)
                    three(work_bank(at)[:], [((AT[0][:, n % 2, f, c], AT[1][:, n % 2, f, c]), (WSD[0][:, f, :], WSD[1][:, f, :]))
                                             for f in range(FT)]).then_inc(wk_ready, 1)

            pe.wait_ge(w_lo, SPIECES + 1)
            for n, b in enumerate(ORDER):
                if n:
                    pe.wait_ge(wk_free, turned_at(n) + NT)
                for f in range(FT):
                    for i, c0 in enumerate((0, FF)):
                        if n:
                            pe.wait_ge(at0_ready, (n - 1) * FT + f + 1)
                        c = slice(c0 + f * P, c0 + (f + 1) * P)
                        three(GU[2 * f + i][:], [((WS[0][:, k, c], WS[1][:, k, c]), (HT[0][:, k, :], HT[1][:, k, :]))
                                                 for k in range(KT)]).then_inc(gu_ready, 1)
                    if n == 0 and f == 0:
                        ranks()
                if n < B - 1:
                    for t in range(NT):
                        pe.wait_ge(wk_free, bank_free(turned_at(n + 1) + t))
                        turn(ORDER[n + 1] * NT + t, turned_at(n + 1) + t)
                if n:
                    output(n - 1)
            output(B - 1)

        @block.scalar
        def _(act):
            def hi_w(k):
                act.wait_ge(w_in[k], 32 if k < KT else 16)
                dst = WS[0][:, k, :] if k < KT else WSD[0][:, k - KT, :]
                nc.scalar.activation(dst, stage(k), ACT.Copy).then_inc(w_hi, 1)

            def hi_h(t, at):
                act.wait_ge(wk_ready, at + 1)
                nc.scalar.activation(HT[0][:, :, t * P:(t + 1) * P], work_bank(at)[:].rearrange("p (k n) -> p k n", k=KT),
                                     ACT.Copy).then_inc(hi_ready, 1)

            def scaled(i):
                act.wait_ge(h0_ready, i + 1)
                if i == NT:
                    act.wait_ge(rs_ready, 2)
                nc.scalar.activation(h_tile(i), h_tile(i), ACT.Copy, scale=rs[:, i:i + 1]).then_inc(h_ready, 1)

            act.wait_ge(rs_ready, 1)
            for i in range(3):
                scaled(i)
            act.wait_ge(rw_in, 16)
            nc.scalar.activation(RW[0][:], RWf[:], ACT.Copy).then_inc(w_hi, 1)
            for i in range(TILES):
                if i >= NT and i % 2 == 0:
                    act.wait_ge(lg_ready, i // 2 - 1)
                hi_h(i % NT, i)
                if i + 3 < TILES:
                    scaled(i + 3)
                if i % 2 and i >= TILES - 2 * SPIECES:
                    hi_w((i - TILES) // 2 + SPIECES)
            act.wait_ge(e2_in, 1)
            nc.scalar.activation(G[1][:], G[1][:], ACT.Exp).then_inc(e2_out, 1)

            for n in range(B):
                for f in range(FT):
                    act.wait_ge(gu_ready, (n * FT + f) * 2 + 1)
                    if n:
                        act.wait_ge(at_ready, (n - 1) * FT + f + 1)
                    nc.scalar.activation(SG[:, f, :], GU[2 * f][:], ACT.Silu).then_inc(sg_ready, 1)
                if n < B - 1:
                    act.wait_ge(gu_ready, (n + 1) * 2 * FT)
                    for t in range(NT):
                        hi_h(t, turned_at(n + 1) + t)
                for f in range(FT):
                    act.wait_ge(at0_ready, n * FT + f + 1)
                    if n > 1 and f == 0:
                        act.wait_ge(wk_ready, down_at(n - 2) + NT)
                    nc.scalar.activation(AT[0][:, n % 2, f, :], SG[:, f, :], ACT.Copy).then_inc(at_hi, 1)

        @block.vector
        def _(dve):
            d = Tick(0)

            def lo_h(t, at, hi):
                dve.wait_ge(wk_ready, at + 1)
                dve.wait_ge(hi_ready, hi + 1)
                c = slice(t * P, (t + 1) * P)
                nc.vector.tensor_tensor(HT[1][:, :, c], work_bank(at)[:].rearrange("p (k n) -> p k n", k=KT),
                                        HT[0][:, :, c].bitcast(F32), ALU.subtract).then_inc(wk_free, 1)

            def lo_w(k):
                dve.wait_ge(w_hi, k + 2)
                pr, n = (WS, k) if k < KT else (WSD, k - KT)
                nc.vector.tensor_tensor(pr[1][:, n, :], stage(k), pr[0][:, n, :].bitcast(F32), ALU.subtract).then_inc(w_lo, 1)

            def centred(i):
                if i < NT:
                    dve.wait_ge(x0_in[i], 16)
                elif i % NT == 0:
                    dve.wait_ge(x_in[i // NT], 16)
                nc.vector.scalar_tensor_tensor(out=h_tile(i), in0=h_tile(i), scalar=mv[:, i, 0:1], in1=rms[:],
                                               op0=ALU.subtract, op1=ALU.mult).then_inc(h0_ready, 1)

            dve.wait_ge(mv_in, 16)
            nc.vector.tensor_scalar(rs[:], mv[:, :, 1], 1.0 + RMS_EPS, RMS_EPS * LN_EPS, ALU.mult, ALU.add).then_inc(var_ready, 1)
            dve.wait_ge(rms_in, 16)
            for i in range(NT):
                centred(i)
            dve.wait_ge(w_hi, 1)
            nc.vector.tensor_tensor(RW[1][:], RWf[:], RW[0][:].bitcast(F32), ALU.subtract).then_inc(w_lo, 1)

            def keep_logits(j):
                dve.wait_ge(lg_ready, j + 1)
                if j >= 2:
                    dve.wait_ge(lg_turned, j - 1)
                nc.vector.tensor_copy(LT[:, j % 2, :], WK[j % 2][0:E, 0:2 * P]).then_inc(lt_ready, 1)

            for i in range(TILES):
                lo_h(i % NT, i, i)
                if i + NT < TILES:
                    centred(i + NT)
                if i % 2 and i >= TILES - 2 * SPIECES:
                    lo_w((i - TILES) // 2 + SPIECES)
                if i % 2 and i >= LAG:
                    keep_logits((i - LAG) // 2)
            keep_logits(HALVES - 1)
            dve.wait_ge(lg_turned, HALVES)
            nc.vector.tensor_copy(L[:], LG[:, 0:TILES * E].rearrange("p (t e) -> p t e", e=E)).then_inc(dv, 1)
            dve.wait_ge(dv, d.up())
            for t in range(TILES):
                nc.vector.max(M8[:, t, :], L[:, t, :]).then_inc(dv, 1)
            dve.wait_ge(dv, d.up(TILES))
            for t in range(TILES):
                nc.vector.max_index(I8[:, t, :], M8[:, t, :], L[:, t, :]).then_inc(dv, 1)
            nc.vector.tensor_tensor(G[1][:], M8[:, :, 1], M8[:, :, 0], ALU.subtract).then_inc(e2_in, 1)
            dve.wait_ge(dv, d.up(TILES))
            nc.vector.tensor_copy(I8f[:], I8[:]).then_inc(dv, 1)
            dve.wait_ge(dv, d.up())
            dve.wait_ge(c_in, 16)
            experts = c_expert.unsqueeze(1).broadcast_to([P, TILES, E])
            for k in range(TOP):
                nc.vector.tensor_tensor(OH[k][:], I8f[:, :, k:k + 1].broadcast_to([P, TILES, E]), experts, ALU.is_equal
                                        ).then_inc(dv, 1)
            dve.wait_ge(dv, d.up(TOP))
            nc.vector.tensor_tensor(OHb[:], OH[0][:], OH[1][:], ALU.add).then_inc(oh_ready, 1)
            dve.wait_ge(e2_out, 1)
            nc.vector.tensor_scalar(G[0][:], G[1][:], 1.0, None, ALU.add).then_inc(dv, 1)
            dve.wait_ge(dv, d.up())
            nc.vector.reciprocal(G[0][:], G[0][:]).then_inc(dv, 1)
            dve.wait_ge(dv, d.up())
            nc.vector.tensor_tensor(G[1][:], G[1][:], G[0][:], ALU.mult).then_inc(dv, 1)
            dve.wait_ge(dv, d.up())
            dve.wait_ge(rk_ready, 1)
            nc.vector.tensor_copy(cnt[:], RB[:, TILES * E:(TILES + 1) * E]).then_inc(dv, 1)
            dve.wait_ge(dv, d.up())
            nc.vector.tensor_tensor(gt, cnt[:].unsqueeze(2).broadcast_to([P, E, TILES]),
                                    c_full.unsqueeze(1).broadcast_to([P, E, TILES]), ALU.is_gt).then_inc(dv, 1)
            dve.wait_ge(dv, d.up())
            nc.vector.tensor_reduce(ntl[:], gt, AX_X, ALU.add).then_inc(dv, 1)
            dve.wait_ge(dv, d.up())
            nc.vector.tensor_tensor(gt[:, :, 0:E], ntl[:].unsqueeze(1).broadcast_to([P, E, E]), c_before, ALU.mult).then_inc(dv, 1)
            dve.wait_ge(dv, d.up())
            nc.vector.tensor_reduce(base[:], gt[:, :, 0:E], AX_X, ALU.add).then_inc(dv, 1)
            dve.wait_ge(dv, d.up())
            nc.vector.tensor_scalar(cnt[:], base[:], float(P), None, ALU.mult).then_inc(dv, 1)
            dve.wait_ge(dv, d.up())
            nc.vector.tensor_tensor(RK[:], RB[:, 0:TILES * E].rearrange("p (t e) -> p t e", e=E),
                                    cnt[:].unsqueeze(1).broadcast_to([P, TILES, E]), ALU.add).then_inc(dv, 1)
            dve.wait_ge(dv, d.up())
            for k in range(TOP):
                nc.vector.tensor_tensor(TMP[:], RK[:], OH[k][:], ALU.mult).then_inc(dv, 1)
                dve.wait_ge(dv, d.up())
                nc.vector.tensor_reduce(slf[:], TMP[:], AX_X, ALU.add).then_inc(dv, 1)
                dve.wait_ge(dv, d.up())
                nc.vector.tensor_copy(SL[k][:], slf[:]).then_inc(sl_ready, 1)
                dve.wait_ge(sl_ready, k + 1)
            nc.vector.tensor_tensor(base[:], base[:], ntl[:], ALU.add).then_inc(dv, 1)
            dve.wait_ge(dv, d.up())
            nc.vector.tensor_tensor(le, base[:, 0:E - 1].unsqueeze(1).broadcast_to([P, SLOT_TILES, E - 1]),
                                    c_tile.unsqueeze(2).broadcast_to([P, SLOT_TILES, E - 1]), ALU.is_le).then_inc(dv, 1)
            dve.wait_ge(dv, d.up())
            nc.vector.tensor_reduce(eidf[:], le, AX_X, ALU.add).then_inc(dv, 1)
            dve.wait_ge(dv, d.up())
            nc.vector.tensor_copy(EID[:], eidf[:]).then_inc(dv, 1)
            dve.wait_ge(dv, d.up())

            def add_output(n):
                b = ORDER[n]
                dve.wait_ge(scat[b], NT * TOP * 16)
                for t in range(NT):
                    at = down_at(n) + t
                    dve.wait_ge(wk_ready, at + 1)
                    dve.wait_ge(xb_in[t], 16 * (n + 1))
                    nc.vector.tensor_tensor(HR[b][:, t, :], work_bank(at)[:], XB[:, t, :], ALU.add).then_inc(wk_free, 1)

            for n in range(B):
                for f in range(FT):
                    dve.wait_ge(gu_ready, (n * FT + f) * 2 + 2)
                    dve.wait_ge(sg_ready, n * FT + f + 1)
                    nc.vector.tensor_tensor(SG[:, f, :], GU[2 * f + 1][:], SG[:, f, :], ALU.mult).then_inc(at0_ready, 1)
                if n < B - 1:
                    for t in range(NT):
                        lo_h(t, turned_at(n + 1) + t, TILES + n * NT + t)
                for f in range(FT):
                    dve.wait_ge(at_hi, n * FT + f + 1)
                    nc.vector.tensor_tensor(AT[1][:, n % 2, f, :], SG[:, f, :], AT[0][:, n % 2, f, :].bitcast(F32),
                                            ALU.subtract).then_inc(at_ready, 1)
                if n:
                    add_output(n - 1)
            add_output(B - 1)


def routed(nc, slots_dram, y_dram, WGU, WD, EID, w_in):
    with ExitStack() as st:
        sb = lambda name, shape, dt=F32: st.enter_context(nc.sbuf_tensor(name, shape, dt))
        banks = lambda name: [st.enter_context(nc.psum_tensor(f"{name}{i}", [P, 512], F32)) for i in range(2)]
        sem = lambda name: st.enter_context(nc.semaphore(name))
        WLO = sb("WLO", [P, E, KT, 2 * FF], F32R)
        WHI = sb("WHI", [P, E, KT, 2 * FF], F32R)
        XG, YO = sb("XG", [P, 2, D]), sb("YO", [P, 2, D])
        XT = [sb(f"XTs_{n}", [P, 2, KT, P], F32R) for n in ("hi", "lo")]
        HH, HT = sb("HH", [P, 2, FF]), sb("HTs", [P, 2, FT, P])
        ident = sb("ident3", [P, P])
        PX, PG, PH, PD = banks("PX"), banks("PG"), banks("PH"), banks("PD")
        pc = sem("r_pc")
        w_hi, w_split = sem("r_whi"), sem("r_wsp")
        xh_ready = sem("r_xh")
        xg_in, y_out = [sem(f"r_xg{i}") for i in range(2)], [sem(f"r_yo{i}") for i in range(2)]
        px_ready, xt_ready, gu_ready, sg_ready, h_ready, ph_ready, ht_ready, pd_ready, yo_ready = [
            sem(f"r_{n}") for n in ("px", "xt", "gu", "sg", "h", "ph", "ht", "pd", "yo")]
        block = st.enter_context(nc.Block())
        N = SLOT_TILES
        FIRST, UNROLL = 3, 6
        TRIPS = (N - 3 - FIRST) // UNROLL
        LAST = FIRST + UNROLL * TRIPS
        rows = lambda dram, i: dram[bass.ds(i * P, P), :]

        def over_tiles(eng, step):
            for i in range(FIRST):
                step(i, i % 2)
            with eng.Fori(0, TRIPS) as p:
                for j in range(UNROLL):
                    step(FIRST + j + UNROLL * p, (FIRST + j) % 2)
            for i in range(LAST, N + 1):
                step(i, i % 2)

        @block.sync
        def _(sp):
            for i in range(2):
                sp.dma_start(XG[:, i, :], rows(slots_dram, i)).then_inc(xg_in[i], 16)

            def step(i, s):
                k = isinstance(i, int)
                if not (k and i + 2 >= N):
                    sp.wait_ge(px_ready, i + 1)
                    sp.dma_start(XG[:, s, :], rows(slots_dram, i + 2)).then_inc(xg_in[s], 16)
                if not (k and i < 1):
                    sp.wait_ge(yo_ready, i)
                    sp.dma_start(rows(y_dram, i - 1), YO[:, 1 - s, :]).then_inc(y_out[1 - s], 16)

            over_tiles(sp, step)
            for s in range(2):
                sp.wait_ge(y_out[s], 16 * ((N + 1 - s) // 2))

        @block.gpsimd
        def _(pool):
            nc.gpsimd.memset(ident[:], 0.0).then_inc(pc, 1)
            pool.wait_ge(pc, 1)
            nc.gpsimd.affine_select(out=ident[:], in_=ident[:], compare_op=ALU.not_equal, fill=1.0, base=0,
                                    pattern=[[-1, P]], channel_multiplier=1).then_inc(pc, 1)
            for e in range(1, E):
                if e == 1:
                    pool.wait_ge(w_split, 1)
                    pool.wait_ge(w_in, 16 * 3 * E)
                nc.gpsimd.tensor_copy(WHI[:, e, :, :], WGU[:, e, :, :]).then_inc(w_hi, 1)
                pool.wait_ge(w_hi, e + 1)
                nc.gpsimd.tensor_tensor(WLO[:, e, :, :], WGU[:, e, :, :], raw(WHI[:, e, :, :]), ALU.subtract
                                        ).then_inc(w_split, 1)

        @block.tensor
        def _(pe):
            pe.wait_ge(pc, 2)
            pe.wait_ge(w_in, 16 * 3 * E)

            def turn(i, s, n_before):
                pe.wait_ge(xg_in[s], 16 * (n_before + 1))
                if not (isinstance(i, int) and i < 2):
                    pe.wait_ge(xt_ready, i - 1)
                for k in range(KT):
                    ins = nc.tensor.transpose(PX[s][:, k * P:(k + 1) * P], XG[:, s, k * P:(k + 1) * P], ident[:])
                ins.then_inc(px_ready, 1)

            turn(0, 0, 0)

            def step(i, s, e_before, of_parity):
                k0, e = isinstance(i, int), None
                if not (k0 and i >= N):
                    e = load(i)
                    pe.wait_ge(w_split, e + 1)
                    pe.wait_ge(xt_ready, i + 1)
                    if not (k0 and i < 2):
                        pe.wait_ge(h_ready, i - 1)
                    for k in range(KT):
                        for n, (x, w) in enumerate(((0, WHI), (0, WLO), (1, WHI))):
                            ins = nc.tensor.matmul(PG[s][:], XT[x][:, s, k, :], w[:, bass.ds(e, 1), k, :].rearrange("p o n -> p (o n)"),
                                                   start=(k + n == 0), stop=(k == KT - 1 and n == 2))
                    ins.then_inc(gu_ready, 1)
                if not (k0 and i + 1 >= N):
                    turn(i + 1, 1 - s, of_parity)
                if not (k0 and i < 1):
                    pe.wait_ge(ht_ready, i)
                    if not (k0 and i < 3):
                        pe.wait_ge(yo_ready, i - 2)
                    for f in range(FT):
                        ins = nc.tensor.matmul(PD[1 - s][:], HT[:, 1 - s, f, :],
                                               WD[:, bass.ds(e_before, 1), f, :].rearrange("p o n -> p (o n)"),
                                               start=(f == 0), stop=(f == FT - 1))
                    ins.then_inc(pd_ready, 1)
                if not (k0 and i >= N):
                    pe.wait_ge(h_ready, i + 1)
                    for f in range(FT):
                        ins = nc.tensor.transpose(PH[s][:, f * P:(f + 1) * P], HH[:, s, f * P:(f + 1) * P], ident[:])
                    ins.then_inc(ph_ready, 1)
                return e

            def load(i):
                return nc.tensor.value_load(EID[0:1, i:i + 1] if isinstance(i, int) else EID[0:1, bass.ds(i, 1)],
                                            min_val=0, max_val=E - 1)

            e = None
            for i in range(FIRST):
                e = step(i, i % 2, e, i // 2 + (i % 2))
            with pe.Fori(0, TRIPS) as p:
                e = load(FIRST - 1 + UNROLL * p)
                for j in range(UNROLL):
                    e = step(FIRST + j + UNROLL * p, (FIRST + j) % 2, e, UNROLL // 2 * p + (FIRST + j + 1) // 2)
            e = load(LAST - 1)
            for i in range(LAST, N + 1):
                e = step(i, i % 2, e, i // 2 + (i % 2))

        @block.scalar
        def _(act):
            def turned(i, s):
                act.wait_ge(px_ready, i + 1)
                if not (isinstance(i, int) and i < 2):
                    act.wait_ge(gu_ready, i - 1)
                nc.scalar.activation(XT[0][:, s, :, :], PX[s][:].rearrange("p (k n) -> p k n", k=KT), ACT.Copy).then_inc(xh_ready, 1)

            act.wait_ge(w_in, 16 * 3 * E)
            nc.scalar.activation(WHI[:, 0, :, :], WGU[:, 0, :, :], ACT.Copy).then_inc(w_hi, 1)
            turned(0, 0)

            def step(i, s):
                k = isinstance(i, int)
                if not (k and i >= N):
                    act.wait_ge(gu_ready, i + 1)
                    if not (k and i < 2):
                        act.wait_ge(ph_ready, i - 1)
                    nc.scalar.activation(HH[:, s, :], PG[s][:, 0:FF], ACT.Silu).then_inc(sg_ready, 1)
                if not (k and i + 1 >= N):
                    turned(i + 1, 1 - s)

            over_tiles(act, step)

        @block.vector
        def _(dve):
            def turned(i, s):
                dve.wait_ge(xh_ready, i + 1)
                nc.vector.tensor_tensor(XT[1][:, s, :, :], PX[s][:].rearrange("p (k n) -> p k n", k=KT), raw(XT[0][:, s, :, :]),
                                        ALU.subtract).then_inc(xt_ready, 1)

            dve.wait_ge(w_hi, 1)
            nc.vector.tensor_tensor(WLO[:, 0, :, :], WGU[:, 0, :, :], raw(WHI[:, 0, :, :]), ALU.subtract).then_inc(w_split, 1)
            turned(0, 0)

            def step(i, s, stored):
                k = isinstance(i, int)
                if not (k and i >= N):
                    dve.wait_ge(sg_ready, i + 1)
                    nc.vector.tensor_tensor(HH[:, s, :], PG[s][:, FF:2 * FF], HH[:, s, :], ALU.mult).then_inc(h_ready, 1)
                if not (k and i + 1 >= N):
                    turned(i + 1, 1 - s)
                if not (k and i < 1):
                    dve.wait_ge(pd_ready, i)
                    if not (k and i < 3):
                        dve.wait_ge(y_out[1 - s], 16 * stored)
                    nc.vector.tensor_copy(YO[:, 1 - s, :], PD[1 - s][:]).then_inc(yo_ready, 1)
                if not (k and i >= N):
                    dve.wait_ge(ph_ready, i + 1)
                    if not (k and i < 2):
                        dve.wait_ge(pd_ready, i - 1)
                    nc.vector.tensor_copy(HT[:, s, :, :], PH[s][:, 0:FF].rearrange("p (f n) -> p f n", f=FT)).then_inc(ht_ready, 1)

            for i in range(FIRST):
                step(i, i % 2, (i - 1) // 2)
            with dve.Fori(0, TRIPS) as p:
                for j in range(UNROLL):
                    step(FIRST + j + UNROLL * p, (FIRST + j) % 2, UNROLL // 2 * p + (FIRST + j - 1) // 2)
            for i in range(LAST, N + 1):
                step(i, i % 2, (i - 1) // 2)


def combine(nc, x2_dram, y_dram, out, HR, G, SL):
    R = 4
    with ExitStack() as st:
        last = st.enter_context(nc.sbuf_tensor("ACC_last", [P, NT, D], F32))
        ACC = HR + [last]
        Y = [st.enter_context(nc.sbuf_tensor(f"Yc{k}", [P, R, D], F32)) for k in range(TOP)]
        y_in = [[st.enter_context(nc.semaphore(f"c_in{k}{r}")) for r in range(R)] for k in range(TOP)]
        a, done, o, last_in = [st.enter_context(nc.semaphore(f"c_{n}")) for n in ("a", "done", "o", "last")]
        block = st.enter_context(nc.Block())

        @block.gpsimd
        def _(pool):
            for t in range(TILES):
                if t >= R:
                    pool.wait_ge(done, t - R + 1)
                for k in range(TOP):
                    pool.indirect_dma_start(out=Y[k][:, t % R, :], out_offset=None, in_=y_dram,
                                            in_offset=bass.IndirectOffsetOnAxis(ap=SL[k][:, t:t + 1], axis=0)
                                            ).then_inc(y_in[k][t % R], 16)

        @block.vector
        def _(dve):
            for t in range(TILES):
                acc = ACC[t // NT][:, t % NT, :]
                if t == TILES - NT:
                    dve.wait_ge(last_in, 16)
                for k in range(TOP):
                    dve.wait_ge(y_in[k][t % R], 16 * (t // R + 1))
                    if k:
                        dve.wait_ge(a, t + 1)
                    nc.vector.scalar_tensor_tensor(out=acc, in0=Y[k][:, t % R, :], scalar=G[k][:, t:t + 1], in1=acc,
                                                    op0=ALU.mult, op1=ALU.add).then_inc(done if k else a, 1)

        @block.sync
        def _(sp):
            ov = out.rearrange("b (t p) d -> (b t) p d", p=P)
            sp.dma_start(last[:], x2_dram[B - 1].rearrange("(t p) d -> p t d", p=P)).then_inc(last_in, 16)
            for t in range(TILES):
                sp.wait_ge(done, t + 1)
                sp.dma_start(ov[t], ACC[t // NT][:, t % NT, :]).then_inc(o, 16)
            sp.wait_ge(o, 16 * TILES)


def build(nc, io, out):
    x2 = nc.dram_tensor("x2_dram", [B, S, D], F32, kind="Internal").ap()
    slots = nc.dram_tensor("slots_dram", [SLOT_TILES * P, D], F32, kind="Internal").ap()
    y = nc.dram_tensor("y_dram", [SLOT_TILES * P, D], F32, kind="Internal").ap()
    mv = nc.dram_tensor("mv_dram", [B, P, NT * 2], F32, kind="Internal").ap()
    attention_part(nc, io, x2, mv, slots)
    with ExitStack() as st:
        sb = lambda name, shape, dt=F32: st.enter_context(nc.sbuf_tensor(name, shape, dt))
        HR = [sb(f"HR{b}", [P, NT, D]) for b in range(B - 1)]
        G = [sb(f"G{k}", [P, TILES]) for k in range(TOP)]
        SL = [sb(f"SL{k}", [P, TILES], mybir.dt.int32) for k in range(TOP)]
        EID = sb("EID", [P, SLOT_TILES], mybir.dt.int32)
        WD = sb("WDn", [P, E, FT, D])
        w_in = st.enter_context(nc.semaphore("exp_w_in"))

        with nc.sbuf_tensor("WGU", [P, E, KT, 2 * FF], F32) as WGU:
            def load_experts(sp):
                for e in range(E):
                    sp.dma_start(WGU[:, e, :, 0:FF], io["wg"][e].rearrange("(k p) f -> p k f", p=P)).then_inc(w_in, 16)
                    sp.dma_start(WGU[:, e, :, FF:2 * FF], io["wu"][e].rearrange("(k p) f -> p k f", p=P)).then_inc(w_in, 16)
                    sp.dma_start(WD[:, e, :, :], io["wd"][e].rearrange("(f p) d -> p f d", p=P)).then_inc(w_in, 16)

            with nc.sbuf_tensor("HR_last", [P, NT, D], F32) as last:
                router_and_shared(nc, io, x2, mv, slots, HR + [last], G, SL, EID, load_experts)
        routed(nc, slots, y, WGU, WD, EID, w_in)
        combine(nc, x2, y, out, HR, G, SL)


NAMES = {"x": "x", "ctx_512": "ctx", "mask_SxS2_bk1": "am", "mask_BxS2_bf0": "km", "L0_attn_W_qkv": "wqkv",
         "L0_attn_W_o": "wo", "L0_xattn_Wq": "xwq", "L0_xattn_bq": "xbq", "L0_xattn_Wk": "xwk",
         "L0_xattn_bk": "xbk", "L0_ffn_rms_weight": "rms", "L0_ffn_router_w": "router", "L0_ffn_w_gate": "wg",
         "L0_ffn_w_up": "wu", "L0_ffn_w_down": "wd", "L0_ffn_sw_gate": "swg", "L0_ffn_sw_up": "swu",
         "L0_ffn_sw_down": "swd"}


def kernel(**inputs):
    import concourse.bacc as bacc
    from concourse.bass_utils import run_bass_kernel_spmd

    nc = bacc.Bacc("TRN2", target_bir_lowering=False, num_devices=1)
    alibi_q, alibi_k = alibi_rows()
    arrays = {NAMES[name]: np.ascontiguousarray(a) for name, a in inputs.items()}
    arrays.update(alq=alibi_q, alk=alibi_k, cst=routing_constants())
    io = {n: nc.dram_tensor(n, a.shape, mybir.dt.from_np(a.dtype), kind="ExternalInput").ap() for n, a in arrays.items()}
    out = nc.dram_tensor("out", (B, S, D), F32, kind="ExternalOutput").ap()
    build(nc, io, out)
    result = run_bass_kernel_spmd(nc, [arrays], core_ids=[0])
    return result.results[0]["out"]
```
